# Optimizing a Trainium2 kernel written in Bass

```python
import numpy as np
import jax
import jax.numpy as jnp

def _softmax(x, axis=-1):
    return jax.nn.softmax(x, axis=axis)
def _gelu(x):
    return jax.nn.gelu(x, approximate=True)
def _silu(x):
    return jax.nn.silu(x)
def _sigmoid(x):
    return jax.nn.sigmoid(x)
def _layernorm(x, axis=-1, eps=1e-5):
    m = jnp.mean(x, axis=axis, keepdims=True)
    v = jnp.var(x, axis=axis, keepdims=True)
    return (x - m) / jnp.sqrt(v + eps)
def _scatter_add(tgt, idx, src, axis=0):
    return tgt.at[idx].add(src)
def _segment_sum(src, seg, n):
    return jax.ops.segment_sum(src, seg, n)

kernel_name = 'mk_conv_preact_d2_conv_nchw512_1294a0'

def setup_inputs(seed: int = 0):
    np.random.seed(seed)
    _w = jnp.asarray
    def _rec_inputs():
        import jax
        import jax.numpy as jnp
        _gk = jax.random.key(seed)
        x = -0.0002928 + 1 * jax.random.normal(jax.random.fold_in(_gk, 1), (2, 512, 64, 64), jnp.float32)
        return x
    x = _rec_inputs()
    def _L0_conv_setup():
        import jax, jax.numpy as jnp
        import numpy as np
        DIM = 512
        D_STATE = 16
        D_CONV = 4
        D_INNER = 1024
        DT_RANK = 32
        EPS = 1e-05

        def _selective_scan(u, delta, A, Bm, Cm, D_skip):

            def step(h, inp):
                u_t, d_t, b_t, c_t = inp
                dA = jnp.exp(d_t[..., None] * A)
                dBu = (d_t * u_t)[..., None] * b_t[:, None, :]
                h = dA * h + dBu
                y = jnp.einsum('bdn,bn->bd', h, c_t)
                return (h, y)
            B, L, d = u.shape
            h0 = jnp.zeros((B, d, A.shape[1]), u.dtype)
            xs = (u.transpose(1, 0, 2), delta.transpose(1, 0, 2), Bm.transpose(1, 0, 2), Cm.transpose(1, 0, 2))
            _, ys = jax.lax.scan(step, h0, xs)
            y = ys.transpose(1, 0, 2)
            return y + u * D_skip

        def _mamba_layer(x, ln_w, ln_b, in_proj_w, conv_w, conv_b, x_proj_w, dt_proj_w, dt_proj_b, A_log, D_skip, out_proj_w):
            B, C = x.shape[:2]
            img_dims = x.shape[2:]
            xf = x.reshape(B, C, -1).transpose(0, 2, 1)
            mu = jnp.mean(xf, -1, keepdims=True)
            var = jnp.mean(jnp.square(xf - mu), -1, keepdims=True)
            xn = (xf - mu) * jax.lax.rsqrt(var + EPS) * ln_w + ln_b
            xz = xn @ in_proj_w.T
            xin, z = jnp.split(xz, 2, axis=-1)
            xc = xin.transpose(0, 2, 1)
            w = conv_w[:, None, :]
            xc = jax.lax.conv_general_dilated(xc, w, window_strides=(1,), padding=[(D_CONV - 1, 0)], feature_group_count=D_INNER, dimension_numbers=('NCH', 'OIH', 'NCH'))
            xc = jax.nn.silu(xc + conv_b[None, :, None])
            xs = xc.transpose(0, 2, 1)
            x_dbl = xs @ x_proj_w.T
            dt = x_dbl[..., :DT_RANK]
            Bm = x_dbl[..., DT_RANK:DT_RANK + D_STATE]
            Cm = x_dbl[..., DT_RANK + D_STATE:]
            delta = jax.nn.softplus(dt @ dt_proj_w.T + dt_proj_b)
            A = -jnp.exp(A_log)
            y = _selective_scan(xs, delta, A, Bm, Cm, D_skip)
            y = y * jax.nn.silu(z)
            out = y @ out_proj_w.T
            return out.transpose(0, 2, 1).reshape(B, C, *img_dims)
        key = jax.random.key(seed)
        ks = jax.random.split(key, 8)
        s = 0.02
        x = jax.random.normal(ks[0], (2, DIM, 64, 64), jnp.float32)
        in_proj_w = jax.random.normal(ks[1], (2 * D_INNER, DIM), jnp.float32) * s
        conv_w = jax.random.normal(ks[2], (D_INNER, D_CONV), jnp.float32) * 0.25
        conv_b = jnp.zeros((D_INNER,), jnp.float32)
        x_proj_w = jax.random.normal(ks[3], (DT_RANK + 2 * D_STATE, D_INNER), jnp.float32) * s
        dt_proj_w = jax.random.normal(ks[4], (D_INNER, DT_RANK), jnp.float32) * DT_RANK ** (-0.5)
        dt_proj_b = jnp.full((D_INNER,), -4.0, jnp.float32)
        A_log = jnp.log(jnp.broadcast_to(jnp.arange(1, D_STATE + 1, dtype=jnp.float32), (D_INNER, D_STATE)))
        D_skip = jnp.ones((D_INNER,), jnp.float32)
        out_proj_w = jax.random.normal(ks[5], (DIM, D_INNER), jnp.float32) * s
        ln_w = jnp.ones((DIM,), jnp.float32)
        ln_b = jnp.zeros((DIM,), jnp.float32)
        return {'x': x, 'ln_w': ln_w, 'ln_b': ln_b, 'in_proj_w': in_proj_w, 'conv_w': conv_w, 'conv_b': conv_b, 'x_proj_w': x_proj_w, 'dt_proj_w': dt_proj_w, 'dt_proj_b': dt_proj_b, 'A_log': A_log, 'D_skip': D_skip, 'out_proj_w': out_proj_w}
    _L0_conv_all = _L0_conv_setup()
    _L0_conv_in = {k: v for k, v in _L0_conv_all.items() if k in ('ln_w', 'ln_b', 'in_proj_w', 'conv_w', 'conv_b', 'x_proj_w', 'dt_proj_w', 'dt_proj_b', 'A_log', 'D_skip', 'out_proj_w', )}
    del _L0_conv_all

    def _L1_conv_setup():
        import jax, jax.numpy as jnp
        import numpy as np
        MOVING_AVG_RATE = 0.999
        EPS_NORM = 1e-12
        EPS_MEAN = 1e-06

        def _l2norm(a):
            n = jnp.linalg.norm(a, axis=1, keepdims=True)
            return a / jnp.maximum(n, EPS_NORM)
        key = jax.random.key(seed)
        k1, k2 = jax.random.split(key)
        x = jax.random.normal(k1, (8, 512, 64, 64), dtype=jnp.float32)
        m = jax.random.normal(k2, (1024, 512), dtype=jnp.float32)
        return {'x': x, 'm': m}
    _L1_conv_all = _L1_conv_setup()
    _L1_conv_in = {k: v for k, v in _L1_conv_all.items() if k in ('m', )}
    del _L1_conv_all

    return {
        "x": x,
        "L0_conv_ln_w": _L0_conv_in["ln_w"],
        "L0_conv_ln_b": _L0_conv_in["ln_b"],
        "L0_conv_in_proj_w": _L0_conv_in["in_proj_w"],
        "L0_conv_conv_w": _L0_conv_in["conv_w"],
        "L0_conv_conv_b": _L0_conv_in["conv_b"],
        "L0_conv_x_proj_w": _L0_conv_in["x_proj_w"],
        "L0_conv_dt_proj_w": _L0_conv_in["dt_proj_w"],
        "L0_conv_dt_proj_b": _L0_conv_in["dt_proj_b"],
        "L0_conv_A_log": _L0_conv_in["A_log"],
        "L0_conv_D_skip": _L0_conv_in["D_skip"],
        "L0_conv_out_proj_w": _L0_conv_in["out_proj_w"],
        "L1_conv_m": _L1_conv_in["m"],
    }

def reference(x, L0_conv_ln_w, L0_conv_ln_b, L0_conv_in_proj_w, L0_conv_conv_w, L0_conv_conv_b, L0_conv_x_proj_w, L0_conv_dt_proj_w, L0_conv_dt_proj_b, L0_conv_A_log, L0_conv_D_skip, L0_conv_out_proj_w, L1_conv_m):
    import jax
    import jax.numpy as jnp
    def _L0_conv_ref(x, ln_w, ln_b, in_proj_w, conv_w, conv_b, x_proj_w, dt_proj_w, dt_proj_b, A_log, D_skip, out_proj_w):
        import jax, jax.numpy as jnp
        import numpy as np
        DIM = 512
        D_STATE = 16
        D_CONV = 4
        D_INNER = 1024
        DT_RANK = 32
        EPS = 1e-05

        def _selective_scan(u, delta, A, Bm, Cm, D_skip):

            def step(h, inp):
                u_t, d_t, b_t, c_t = inp
                dA = jnp.exp(d_t[..., None] * A)
                dBu = (d_t * u_t)[..., None] * b_t[:, None, :]
                h = dA * h + dBu
                y = jnp.einsum('bdn,bn->bd', h, c_t)
                return (h, y)
            B, L, d = u.shape
            h0 = jnp.zeros((B, d, A.shape[1]), u.dtype)
            xs = (u.transpose(1, 0, 2), delta.transpose(1, 0, 2), Bm.transpose(1, 0, 2), Cm.transpose(1, 0, 2))
            _, ys = jax.lax.scan(step, h0, xs)
            y = ys.transpose(1, 0, 2)
            return y + u * D_skip

        def _mamba_layer(x, ln_w, ln_b, in_proj_w, conv_w, conv_b, x_proj_w, dt_proj_w, dt_proj_b, A_log, D_skip, out_proj_w):
            B, C = x.shape[:2]
            img_dims = x.shape[2:]
            xf = x.reshape(B, C, -1).transpose(0, 2, 1)
            mu = jnp.mean(xf, -1, keepdims=True)
            var = jnp.mean(jnp.square(xf - mu), -1, keepdims=True)
            xn = (xf - mu) * jax.lax.rsqrt(var + EPS) * ln_w + ln_b
            xz = xn @ in_proj_w.T
            xin, z = jnp.split(xz, 2, axis=-1)
            xc = xin.transpose(0, 2, 1)
            w = conv_w[:, None, :]
            xc = jax.lax.conv_general_dilated(xc, w, window_strides=(1,), padding=[(D_CONV - 1, 0)], feature_group_count=D_INNER, dimension_numbers=('NCH', 'OIH', 'NCH'))
            xc = jax.nn.silu(xc + conv_b[None, :, None])
            xs = xc.transpose(0, 2, 1)
            x_dbl = xs @ x_proj_w.T
            dt = x_dbl[..., :DT_RANK]
            Bm = x_dbl[..., DT_RANK:DT_RANK + D_STATE]
            Cm = x_dbl[..., DT_RANK + D_STATE:]
            delta = jax.nn.softplus(dt @ dt_proj_w.T + dt_proj_b)
            A = -jnp.exp(A_log)
            y = _selective_scan(xs, delta, A, Bm, Cm, D_skip)
            y = y * jax.nn.silu(z)
            out = y @ out_proj_w.T
            return out.transpose(0, 2, 1).reshape(B, C, *img_dims)
        return _mamba_layer(x, ln_w, ln_b, in_proj_w, conv_w, conv_b, x_proj_w, dt_proj_w, dt_proj_b, A_log, D_skip, out_proj_w)

    def _L1_conv_ref(x, m):
        import jax, jax.numpy as jnp
        import numpy as np
        MOVING_AVG_RATE = 0.999
        EPS_NORM = 1e-12
        EPS_MEAN = 1e-06

        def _l2norm(a):
            n = jnp.linalg.norm(a, axis=1, keepdims=True)
            return a / jnp.maximum(n, EPS_NORM)
        b, c, h, w = x.shape
        k = m.shape[0]
        xf = jnp.transpose(x, (0, 2, 3, 1)).reshape(-1, c)
        xn = _l2norm(xf)
        mn = _l2norm(m)
        score = xn @ mn.T
        idx = jnp.argmax(score, axis=1)
        counts = jax.ops.segment_sum(jnp.ones(xf.shape[0], dtype=xf.dtype), idx, num_segments=k)
        esum = jax.ops.segment_sum(xf, idx, num_segments=k)
        emean = esum / (counts[:, None] + EPS_MEAN)
        new_m = m * MOVING_AVG_RATE + emean * (1.0 - MOVING_AVG_RATE)
        soft = jax.nn.softmax(score, axis=1)
        out = soft @ new_m
        return jnp.transpose(out.reshape(b, h, w, c), (0, 3, 1, 2))

    def _gn(v, G=32, eps=1e-5):
        B_, C_, H_, W_ = v.shape
        g = v.reshape(B_, G, C_ // G, H_, W_)
        m = jnp.mean(g, axis=(2, 3, 4), keepdims=True)
        s = jnp.var(g, axis=(2, 3, 4), keepdims=True)
        return ((g - m) / jnp.sqrt(s + eps)).reshape(v.shape)

    def _ln_c(v, eps=1e-6):
        m = jnp.mean(v, axis=1, keepdims=True)
        s = jnp.var(v, axis=1, keepdims=True)
        return (v - m) / jnp.sqrt(s + eps)

    def _ln_t(v, eps=1e-5):
        m = jnp.mean(v, axis=-1, keepdims=True)
        s = jnp.var(v, axis=-1, keepdims=True)
        return (v - m) / jnp.sqrt(s + eps)

    def _to_tokens(v):
        B_, C_, H_, W_ = v.shape
        return v.reshape(B_, C_, H_ * W_).transpose(0, 2, 1)
    def _from_tokens(t, like):
        B_, C_, H_, W_ = like.shape
        return t.transpose(0, 2, 1).reshape(B_, C_, H_, W_)

    x = x + _L0_conv_ref(_gn(x), L0_conv_ln_w, L0_conv_ln_b, L0_conv_in_proj_w, L0_conv_conv_w, L0_conv_conv_b, L0_conv_x_proj_w, L0_conv_dt_proj_w, L0_conv_dt_proj_b, L0_conv_A_log, L0_conv_D_skip, L0_conv_out_proj_w)
    x = x + _L1_conv_ref(_gn(x), L1_conv_m)
    return x


_drawn_inputs = setup_inputs


def setup_inputs(seed=0):
    import zlib

    import numpy as np

    out = dict(_drawn_inputs(seed))
    spreads = {'L0_conv_ln_w': (1.0, 0.6),
     'L0_conv_ln_b': (0.0, 0.8),
     'L0_conv_conv_b': (0.0, 0.8),
     'L0_conv_dt_proj_b': (-4.0, 0.6),
     'L0_conv_D_skip': (1.0, 0.6)}
    factors = {'L0_conv_conv_w': 2.739,
     'L0_conv_x_proj_w': 8.0,
     'L0_conv_dt_proj_w': 8.0,
     'L0_conv_A_log': 8.0}
    for name, (base, spread) in spreads.items():
        noise = np.random.default_rng([zlib.crc32(name.encode()), seed]).standard_normal(out[name].shape)
        drawn = base * np.exp(spread * noise) if base else spread * noise
        out[name] = jnp.asarray(drawn.astype(out[name].dtype))
    for name, factor in factors.items():
        out[name] = (out[name] * factor).astype(out[name].dtype)
    return out
```

```python
from contextlib import ExitStack

import concourse.bass as bass
from concourse import mybir

F32 = mybir.dt.float32
F32R = mybir.dt.float32r
U32 = mybir.dt.uint32
ALU = mybir.AluOpType
ACT = mybir.ActivationFunctionType
AXX = mybir.AxisListType.X

P = 128
NB = 2
L = 64 * 64
T = 512
NJ = L // T
NG = NB * NJ
DIM = 512
KC = DIM // P
DI = 1024
KD = DI // P
NS = 16
RANK = 32
TAPS = 4
HIST = TAPS - 1
KM = 1024
KK = KM // P
GN_EPS = 1e-5
LN_EPS = 1e-5
NORM_EPS = 1e-12
MEAN_EPS = 1e-6
RATE = 0.999
DELTA, DU, U, Z = range(4)


class Place:

    def __init__(self, nc, ctx, tag):
        self.nc, self.ctx, self.tag = nc, ctx, tag

    def sb(self, name, shape, dt=F32):
        return self.ctx.enter_context(self.nc.sbuf_tensor(f"{self.tag}_{name}", shape, dt))

    def ps(self, name, shape, dt=F32):
        return self.ctx.enter_context(self.nc.psum_tensor(f"{self.tag}_{name}", shape, dt))

    def sem(self, name):
        return self.ctx.enter_context(self.nc.semaphore(f"{self.tag}_{name}"))


def split_matmul(nc, out, lhs, rhs, start, stop):
    nc.tensor.matmul(out, lhs[0], rhs[0], start=start, stop=False)
    nc.tensor.matmul(out, lhs[1], rhs[0], start=False, stop=False)
    return nc.tensor.matmul(out, lhs[0], rhs[1], start=False, stop=stop)


def group_params(nc, tag, keep, stats, scale, shift):
    n = NB * KC
    with ExitStack() as ctx:
        w = Place(nc, ctx, tag)
        mv = w.sb("mv", [P, n, 2])
        mean = w.sb("mean", [P, n])
        dev = w.sb("dev", [P, n])
        spread = w.sb("spread", [P, n])
        std = w.sb("std", [P, n])
        ps = w.ps("ps", [P, 2, T])
        step = w.sem("step")
        mean_ps = w.sem("mean_ps")
        var_ps = w.sem("var_ps")
        std_done = w.sem("std_done")
        block = ctx.enter_context(nc.Block())

        @block.vector
        def _(dve):
            for i in range(n):
                nc.vector.bn_aggr(mv[:, i, :], stats[:, i, :, :]).then_inc(step, 1)
            dve.wait_ge(step, n)
            nc.vector.tensor_copy(mean[:], mv[:, :, 0]).then_inc(step, 1)
            dve.wait_ge(mean_ps, 1)
            dve.wait_ge(step, n + 1)
            nc.vector.tensor_tensor(dev[:], mean[:], ps[:, 0, 0:n], ALU.subtract).then_inc(step, 1)
            dve.wait_ge(step, n + 2)
            nc.vector.tensor_tensor(dev[:], dev[:], dev[:], ALU.mult).then_inc(step, 1)
            dve.wait_ge(step, n + 3)
            nc.vector.tensor_tensor(spread[:], dev[:], mv[:, :, 1], ALU.add).then_inc(step, 1)
            dve.wait_ge(std_done, 1)
            nc.vector.reciprocal(scale[:], std[:]).then_inc(step, 1)
            dve.wait_ge(step, n + 5)
            nc.vector.scalar_tensor_tensor(shift[:], ps[:, 0, 0:n], -1.0, scale[:], ALU.mult, ALU.mult).then_inc(step, 1)
            dve.wait_ge(step, n + 6)

        @block.tensor
        def _(pe):
            pe.wait_ge(step, n + 1)
            nc.tensor.matmul(ps[:, 0, 0:n], keep.gavg[:], mean[:], start=True, stop=True).then_inc(mean_ps, 1)
            pe.wait_ge(step, n + 4)
            nc.tensor.matmul(ps[:, 1, 0:n], keep.gavg[:], spread[:], start=True, stop=True).then_inc(var_ps, 1)

        @block.scalar
        def _(act):
            act.wait_ge(var_ps, 1)
            nc.scalar.activation(std[:], ps[:, 1, 0:n], ACT.Sqrt, bias=keep.gn_eps[:, 0:1]).then_inc(std_done, 1)


def setup(nc, keep, d):
    with ExitStack() as ctx:
        w = Place(nc, ctx, "su")
        wf = w.sb("wf", [P, KC, 2 * DI])
        lnw = w.sb("lnw", [P, KC])
        lnb = w.sb("lnb", [P, KC])
        alog = w.sb("alog", [P, KD * NS])
        xt = w.sb("xt", [P, 2, L])
        bias_ps = w.ps("bias_ps", [P, T])
        consts = w.sem("consts")
        weights = w.sem("weights")
        x_tile = [w.sem(f"x_tile{i}") for i in range(2)]
        eps_set = w.sem("eps_set")
        stats_done = w.sem("stats_done")
        bias_done = w.sem("bias_done")
        exp_done = w.sem("exp_done")
        scaled = w.sem("scaled")
        high = w.sem("high")
        rest = w.sem("rest")
        n_const = 11
        block = ctx.enter_context(nc.Block())
        x_rows = d.x.rearrange("b (k p) h w -> (b k) p (h w)", p=P)

        @block.sync
        def _(sp):
            sp.dma_start(wf[:], d.w_in).then_inc(weights, 16)
            with sp.Fori(0, NB * KC // 2) as i:
                for s in range(2):
                    sp.wait_ge(stats_done, 2 * i + s)
                    sp.dma_start(xt[:, s, :], x_rows[2 * i + s]).then_inc(x_tile[s], 16)

        @block.gpsimd
        def _(pool):
            for dst, src in ((keep.ident, d.ident), (keep.gavg, d.gavg), (lnw, d.ln_w), (lnb, d.ln_b), (alog, d.a_log),
                             (keep.conv_w, d.conv_w), (keep.conv_b, d.conv_b), (keep.dskip, d.d_skip), (keep.w_xp, d.w_xp)):
                pool.dma_start(dst[:], src).then_inc(consts, 16)
            pool.dma_start(keep.w_dt[0:RANK, :], d.w_dt).then_inc(consts, 16)
            pool.dma_start(keep.w_dt[RANK:RANK + 1, :], d.b_dt).then_inc(consts, 16)

        @block.scalar
        def _(act):
            act.wait_ge(consts, 16 * n_const)
            nc.scalar.activation(alog[:], alog[:], ACT.Exp).then_inc(exp_done, 1)
            act.wait_ge(scaled, KC)
            nc.scalar.activation(keep.w_in[0][:], wf[:], ACT.Copy).then_inc(high, 1)

        @block.tensor
        def _(pe):
            pe.wait_ge(consts, 16 * n_const)
            pe.wait_ge(weights, 16)
            for m in range(2 * KD):
                for k in range(KC):
                    last = nc.tensor.matmul(bias_ps[:, m:m + 1], wf[:, k, m * P:(m + 1) * P], lnb[:, k:k + 1],
                                            start=(k == 0), stop=(k == KC - 1))
            last.then_inc(bias_done, 1)

        @block.vector
        def _(dve):
            nc.vector.memset(keep.gn_eps[:], GN_EPS).then_inc(eps_set, 1)
            nc.vector.memset(keep.mean_w[:], 1.0 / DIM).then_inc(eps_set, 1)
            dve.sem_inc(stats_done, 1)
            dve.wait_ge(consts, 16 * n_const)
            dve.wait_ge(weights, 16)
            dve.wait_ge(bias_done, 1)
            nc.vector.tensor_copy(keep.b_in[:], bias_ps[:, 0:2 * KD]).then_inc(rest, 1)
            for k in range(KC):
                nc.vector.tensor_scalar(wf[:, k, :], wf[:, k, :], lnw[:, k:k + 1], None, ALU.mult).then_inc(scaled, 1)
            dve.wait_ge(exp_done, 1)
            nc.vector.tensor_scalar(keep.neg_a[:], alog[:], -1.0, None, ALU.mult).then_inc(rest, 1)
            with dve.Fori(0, NB * KC // 2) as i:
                for s in range(2):
                    dve.wait_ge(x_tile[s], 16 * i + 16)
                    for j in range(NJ):
                        last = nc.vector.bn_stats(keep.stats[:, 2 * i + s, j, :], xt[:, s, j * T:(j + 1) * T])
                    last.then_inc(stats_done, 1)
            dve.wait_ge(high, 1)
            nc.vector.tensor_tensor(keep.w_in[1][:], wf[:], keep.w_in[0][:].bitcast(F32), ALU.subtract).then_inc(rest, 1)
            dve.wait_ge(rest, 3)
            dve.wait_ge(eps_set, 2)


def front(nc, keep, d):
    with ExitStack() as ctx:
        w = Place(nc, ctx, "fr")
        x_in = w.sb("x_in", [P, KC, T])
        v = w.sb("v", [P, KC, T])
        sq = w.sb("sq", [P, KC, T])
        sd = w.sb("sd", [P, T])
        rs = w.sb("rs", [P, T])
        xn = [w.sb("xn_hi", [P, KC, T], F32R), w.sb("xn_lo", [P, KC, T], F32R)]
        xr = w.sb("xr", [P, 2, HIST + T])
        hist = w.sb("hist", [P, KD, HIST])
        acc = w.sb("acc", [P, 2, T])
        u = w.sb("u", [P, KD, T])
        z = w.sb("z", [P, KD, T])
        delta = w.sb("delta", [P, KD, T])
        dt = w.sb("dt", [RANK + 1, T])
        bc = w.sb("bc", [64, T])
        e = w.sb("e", [P, 2, T])
        ln = w.sb("ln", [P, 2, T])
        u1 = w.sb("u1", [P, 2, T])
        mm = w.ps("mm", [P, 4, T])
        mu_ps = w.ps("mu_ps", [P, T])
        var_ps = w.ps("var_ps", [P, T])
        xd_ps = w.ps("xd_ps", [64, T])

        s_x = w.sem("x_loaded")
        s_v = w.sem("v_done")
        s_mu = w.sem("mu_done")
        s_vc = w.sem("centred")
        s_sq = w.sem("squared")
        s_var = w.sem("var_done")
        s_sd = w.sem("sd_done")
        s_rs = w.sem("rs_done")
        s_xn = w.sem("xn_done")
        s_xh = w.sem("xn_hi_done")
        s_xl = w.sem("xn_lo_done")
        s_mm = w.sem("mm_done")
        s_ev = w.sem("mm_evacuated")
        s_cs = w.sem("conv_step")
        s_cv = w.sem("conv_done")
        s_u = w.sem("u_done")
        s_xd = w.sem("xdbl_done")
        s_dt = w.sem("dt_copied")
        s_bc = w.sem("bc_copied")
        s_ab = w.sem("abs_done")
        s_e = w.sem("e_done")
        s_ln = w.sem("ln_done")
        s_ds = w.sem("delta_step")
        s_dl = w.sem("delta_done")
        s_du = w.sem("du_done")
        s_zero = w.sem("hist_zeroed")
        s_one = w.sem("ones_set")
        st_u = w.sem("u_stored")
        st_z = w.sem("z_stored")
        st_bc = w.sem("bc_stored")
        st_dl = w.sem("delta_stored")
        st_du = w.sem("du_stored")
        block = ctx.enter_context(nc.Block())
        x_view = d.x.rearrange("b (k p) (j r) w -> b j p k (r w)", p=P, j=NJ)
        NQ = 2 * KD + KD

        def batches(eng, prologue, main, peeled=1):
            for b in range(NB):
                prologue(b * NJ)
                with eng.Fori(0, NJ - peeled) as j:
                    main(b, j, peeled)
                for j in range(NJ - peeled, NJ):
                    main(b, j, NJ - 1 - j)

        @block.sync
        def _(sp):
            def load(b, j, n):
                sp.dma_start(x_in[:], x_view[b, j]).then_inc(s_x, 16)

            def prologue(g):
                b = g // NJ
                if b:
                    sp.wait_ge(s_v, g)
                load(b, 0, g)
                sp.wait_ge(s_v, g + 1)
                load(b, 1, g + 1)

            def main(b, j, ahead):
                g = b * NJ + j
                if ahead >= 1:
                    sp.wait_ge(s_v, g + 2)
                if ahead >= 2:
                    load(b, j + 2, g + 2)
                sp.wait_ge(s_u, KD * g + KD)
                sp.dma_start(d.spill[g][:, :, U, :], u[:]).then_inc(st_u, 16)
                sp.wait_ge(s_ev, 2 * KD * g + 2 * KD)
                sp.dma_start(d.spill[g][:, :, Z, :], z[:]).then_inc(st_z, 16)
                sp.wait_ge(s_bc, g + 1)
                sp.dma_start(d.bc[g], bc[RANK:64, :]).then_inc(st_bc, 16)
                sp.wait_ge(s_du, KD * g + KD + KD)
                sp.dma_start(d.spill[g][:, :, DU, :], u[:]).then_inc(st_du, 16)
                sp.dma_start(d.spill[g][:, :, DELTA, :], delta[:]).then_inc(st_dl, 16)

            batches(sp, prologue, main, 2)
            for s in (st_u, st_z, st_bc, st_dl, st_du):
                sp.wait_ge(s, 16 * NG)

        @block.gpsimd
        def _(pool):
            pool.sem_inc(s_du, KD)

            def main(b, j, ahead):
                g = b * NJ + j
                pool.wait_ge(st_u, 16 * g + 16)
                for m in range(KD):
                    pool.wait_ge(s_dl, KD * g + m + 1 + KD)
                    nc.gpsimd.tensor_tensor(u[:, m, :], u[:, m, :], delta[:, m, :], ALU.mult).then_inc(s_du, 1)

            batches(pool, lambda g: None, main)

        @block.scalar
        def _(act):
            def norm_v(b, g):
                act.wait_ge(s_x, 16 * g + 16)
                act.wait_ge(s_xl, g)
                for k in range(KC):
                    c = b * KC + k
                    last = nc.scalar.activation(v[:, k, :], x_in[:, k, :], ACT.Identity,
                                                bias=keep.shift[:, c:c + 1], scale=keep.scale[:, c:c + 1])
                last.then_inc(s_v, 1)

            def square(g):
                act.wait_ge(s_vc, g + 1)
                act.wait_ge(s_var, g)
                nc.scalar.activation(sq[:], v[:], ACT.Square).then_inc(s_sq, 1)

            def root(g):
                act.wait_ge(s_var, g + 1)
                act.wait_ge(s_rs, g)
                nc.scalar.activation(sd[:], var_ps[:], ACT.Sqrt, bias=keep.gn_eps[:, 0:1]).then_inc(s_sd, 1)

            def split(g, mm_before):
                act.wait_ge(s_xn, g + 1)
                act.wait_ge(s_mm, mm_before)
                nc.scalar.activation(xn[0][:], v[:], ACT.Copy).then_inc(s_xh, 1)

            def prologue(g):
                norm_v(g // NJ, g)
                square(g)
                root(g)
                split(g, NQ * g)

            def silu_u(g, m):
                act.wait_ge(s_cv, KD * g + m + 1)
                act.wait_ge(s_du, KD * g + m + 1)
                if m == 0:
                    act.wait_ge(st_du, 16 * g)
                nc.scalar.activation(u[:, m, :], acc[:, m % 2, :], ACT.Silu).then_inc(s_u, 1)

            def main(b, j, ahead):
                g = b * NJ + j
                for m in range(KD):
                    act.wait_ge(s_mm, NQ * g + m + 1)
                    act.wait_ge(s_cv, KD * g + max(m - 1, 0))
                    nc.scalar.activation(xr[:, m % 2, HIST:], mm[:, m % 4, :], ACT.Identity,
                                         bias=keep.b_in[:, m:m + 1]).then_inc(s_ev, 1)
                    if m:
                        silu_u(g, m - 1)
                silu_u(g, KD - 1)
                if ahead:
                    norm_v(b, g + 1)
                act.wait_ge(st_z, 16 * g)
                for m in range(KD):
                    q = KD + m
                    act.wait_ge(s_mm, NQ * g + q + 1)
                    nc.scalar.activation(z[:, m, :], mm[:, q % 4, :], ACT.Silu,
                                         bias=keep.b_in[:, q:q + 1]).then_inc(s_ev, 1)
                    if m == 3 and ahead:
                        square(g + 1)
                if ahead:
                    root(g + 1)
                act.wait_ge(s_xd, g + 1)
                act.wait_ge(s_mm, NQ * g)
                nc.scalar.activation(dt[0:RANK, :], xd_ps[0:RANK, :], ACT.Copy).then_inc(s_dt, 1)
                act.wait_ge(st_bc, 16 * g)
                nc.scalar.activation(bc[RANK:64, :], xd_ps[RANK:64, :], ACT.Copy).then_inc(s_bc, 1)
                for m in range(KD):
                    q = 2 * KD + m
                    act.wait_ge(s_mm, NQ * g + q + 1)
                    act.wait_ge(s_dl, KD * g + KD + m - 1)
                    nc.scalar.activation(e[:, m % 2, :], mm[:, q % 4, :], ACT.Abs).then_inc(s_ab, 1)
                    act.wait_ge(s_ab, KD * g + m + 1)
                    nc.scalar.activation(e[:, m % 2, :], e[:, m % 2, :], ACT.Exp, scale=-1.0).then_inc(s_e, 1)
                    act.wait_ge(s_e, KD * g + m + 1)
                    nc.scalar.activation(ln[:, m % 2, :], e[:, m % 2, :], ACT.Ln, bias=1.0).then_inc(s_ln, 1)
                    if m == 3 and ahead:
                        split(g + 1, NQ * g + 2 * KD)

            batches(act, prologue, main)

        @block.tensor
        def _(pe):
            def mean(g):
                pe.wait_ge(s_v, g + 1)
                for k in range(KC):
                    last = nc.tensor.matmul(mu_ps[:], keep.mean_w[:], v[:, k, :], start=(k == 0), stop=(k == KC - 1))
                last.then_inc(s_mu, 1)

            def var(g):
                pe.wait_ge(s_sq, g + 1)
                pe.wait_ge(s_sd, g)
                for k in range(KC):
                    last = nc.tensor.matmul(var_ps[:], keep.mean_w[:], sq[:, k, :], start=(k == 0), stop=(k == KC - 1))
                last.then_inc(s_var, 1)

            def prologue(g):
                mean(g)
                var(g)

            def bank_free(g, q):
                if q < 4:
                    pe.wait_ge(s_dl, KD * g + q + 5)
                elif q < 4 + 2 * KD:
                    pe.wait_ge(s_ev, 2 * KD * g + q - 3)
                else:
                    pe.wait_ge(s_dl, KD * g + KD + q - 2 * KD - 3)

            def main(b, j, ahead):
                g = b * NJ + j
                pe.wait_ge(s_xh, g + 1)
                pe.wait_ge(s_xl, g + 1)
                for q in range(2 * KD):
                    if q == KD and ahead:
                        mean(g + 1)
                    if q == KD + 4 and ahead:
                        var(g + 1)
                    bank_free(g, q)
                    for k in range(KC):
                        cols = slice(q * P, (q + 1) * P)
                        last = split_matmul(nc, mm[:, q % 4, :], [part[:, k, cols] for part in keep.w_in],
                                            [part[:, k, :] for part in xn], k == 0, k == KC - 1)
                    last.then_inc(s_mm, 1)
                pe.wait_ge(s_dt, g)
                pe.wait_ge(s_bc, g)
                for m in range(KD):
                    pe.wait_ge(s_u, KD * g + m + 1)
                    last = nc.tensor.matmul(xd_ps[:], keep.w_xp[:, m, :], u[:, m, :], start=(m == 0), stop=(m == KD - 1))
                last.then_inc(s_xd, 1)
                pe.wait_ge(s_dt, g + 1)
                for m in range(KD):
                    q = 2 * KD + m
                    bank_free(g, q)
                    nc.tensor.matmul(mm[:, q % 4, :], keep.w_dt[:, m * P:(m + 1) * P], dt[:], start=True,
                                     stop=True).then_inc(s_mm, 1)

            pe.wait_ge(s_one, 1)
            batches(pe, prologue, main)

        @block.vector
        def _(dve):
            nc.vector.memset(dt[RANK:RANK + 1, :], 1.0).then_inc(s_one, 1)
            dve.sem_inc(s_dl, KD)

            def over_blocks(t):
                return t[:].rearrange("p (k t) -> p k t", k=1).broadcast_to([P, KC, T])

            def centre(g):
                dve.wait_ge(s_mu, g + 1)
                nc.vector.tensor_tensor(v[:], v[:], over_blocks(mu_ps), ALU.subtract).then_inc(s_vc, 1)

            def normalise(g):
                dve.wait_ge(s_sd, g + 1)
                nc.vector.reciprocal(rs[:], sd[:]).then_inc(s_rs, 1)
                dve.wait_ge(s_rs, g + 1)
                nc.vector.tensor_tensor(v[:], v[:], over_blocks(rs), ALU.mult).then_inc(s_xn, 1)

            def split(g):
                dve.wait_ge(s_xh, g + 1)
                nc.vector.tensor_tensor(xn[1][:], v[:], xn[0][:].bitcast(F32), ALU.subtract).then_inc(s_xl, 1)

            def prologue(g):
                nc.vector.memset(hist[:], 0.0).then_inc(s_zero, 1)
                centre(g)
                normalise(g)
                split(g)
                dve.wait_ge(s_zero, g // NJ + 1)

            def conv(g, m):
                base = 5 * (KD * g + m)
                slot = m % 2
                dve.wait_ge(s_ev, 2 * KD * g + m + 1)
                dve.wait_ge(s_cs, 5 * KD * g)
                nc.vector.tensor_copy(xr[:, slot, 0:HIST], hist[:, m, :]).then_inc(s_cs, 1)
                dve.wait_ge(s_cs, base + 1)
                dve.wait_ge(s_u, KD * g + max(m - 1, 0))
                nc.vector.tensor_scalar(acc[:, slot, :], xr[:, slot, 0:T], keep.conv_w[:, m, 0:1],
                                        keep.conv_b[:, m:m + 1], ALU.mult, ALU.add).then_inc(s_cs, 1)
                nc.vector.tensor_copy(hist[:, m, :], xr[:, slot, T:T + HIST]).then_inc(s_cs, 1)
                for i in range(1, TAPS):
                    dve.wait_ge(s_cs, base + 2 + (i if i > 1 else 0))
                    last = nc.vector.scalar_tensor_tensor(acc[:, slot, :], xr[:, slot, i:i + T], keep.conv_w[:, m, i:i + 1],
                                                          acc[:, slot, :], ALU.mult, ALU.add)
                    last.then_inc(s_cs if i < TAPS - 1 else s_cv, 1)

            def softplus(g, m):
                base = 3 * (KD * g + m)
                q = 2 * KD + m
                slot = m % 2
                dve.wait_ge(s_e, KD * g + m + 1)
                dve.wait_ge(s_dl, KD * g + KD + m - 1)
                nc.vector.tensor_scalar(u1[:, slot, :], e[:, slot, :], 1.0, None, ALU.add).then_inc(s_ds, 1)
                dve.wait_ge(s_ds, base + 1)
                nc.vector.scalar_tensor_tensor(u1[:, slot, :], u1[:, slot, :], 1.0, e[:, slot, :], ALU.subtract,
                                               ALU.subtract).then_inc(s_ds, 1)
                dve.wait_ge(s_ln, KD * g + m + 1)
                nc.vector.scalar_tensor_tensor(ln[:, slot, :], mm[:, q % 4, :], 0.0, ln[:, slot, :], ALU.max,
                                               ALU.add).then_inc(s_ds, 1)
                dve.wait_ge(s_ds, base + 3)
                if m == 0:
                    dve.wait_ge(st_dl, 16 * g)
                    dve.wait_ge(s_du, KD * g + KD)
                nc.vector.tensor_tensor(delta[:, m, :], ln[:, slot, :], u1[:, slot, :], ALU.subtract).then_inc(s_dl, 1)

            def main(b, j, ahead):
                g = b * NJ + j
                for m in range(KD):
                    conv(g, m)
                if ahead:
                    centre(g + 1)
                    normalise(g + 1)
                for m in range(KD):
                    softplus(g, m)
                    if m == 4 and ahead:
                        split(g + 1)

            batches(dve, prologue, main)


def scan(nc, keep, d):
    NQ = NS // 4
    NC = KD * NQ
    with ExitStack() as ctx:
        w = Place(nc, ctx, "sc")
        b_all = w.sb("b_all", [P, NS, T])
        c_all = w.sb("c_all", [P, NS, T])
        blk = w.sb("blk", [P, 4, 4, T])
        da = w.sb("da", [P, 2, 4, T])
        dbu = w.sb("dbu", [P, 2, 4, T])
        h = w.sb("h", [P, 2, 4, T])
        hc = w.sb("hc", [P, 2, 4, T])
        state = w.sb("state", [P, KD, NS])
        yg = w.sb("yg", [P, 2, T])
        w_out = w.sb("w_out", [P, KD, DIM])
        skip = w.sb("skip", [P, KD, P])
        x_res = w.sb("x_res", [P, KC, T])
        y_ps = w.ps("y_ps", [P, 2, T])
        o_ps = w.ps("o_ps", [P, KC, T])

        s_w = w.sem("w_out_loaded")
        s_skip = w.sem("skip_made")
        s_b = [w.sem(f"b_loaded{q}") for q in range(NQ)]
        s_c = [w.sem(f"c_loaded{q}") for q in range(NQ)]
        s_blk = [w.sem(f"block_loaded{i}") for i in range(4)]
        s_x = w.sem("x_loaded")
        s_zero = w.sem("state_zeroed")
        s_da = w.sem("da_done")
        s_dbu = w.sem("dbu_done")
        s_h = w.sem("h_done")
        s_st = w.sem("state_kept")
        s_hc = w.sem("hc_done")
        s_acc = w.sem("hc_summed")
        s_y = w.sem("y_done")
        s_yg = w.sem("gated")
        s_op = w.sem("projected")
        s_res = w.sem("x1_done")
        s_add = w.sem("x1_summed")
        st_x1 = w.sem("x1_stored")
        block = ctx.enter_context(nc.Block())
        x_view = d.x.rearrange("b (k p) (j r) w -> b j p k (r w)", p=P, j=NJ)

        def chunks(eng, body, before=None):
            for b in range(NB):
                if before:
                    before(b)
                with eng.Fori(0, NJ) as j:
                    body(b, j, b * NJ + j)

        @block.sync
        def _(sp):
            sp.sem_inc(st_x1, 16)
            sp.dma_start(w_out[:], d.w_out).then_inc(s_w, 16)

            def block_in(g, i):
                sp.wait_ge(s_yg, KD * g + i + 1)
                sp.dma_start(blk[:, i % 4], d.spill[g][:, i]).then_inc(s_blk[i % 4], 16)

            def first_loads(g):
                for i in range(3):
                    block_in(g, i)
                    if i == 0:
                        for q in range(NQ):
                            rows = slice(4 * q, 4 * q + 4)
                            for t, s_t, used, at in ((b_all, s_b, s_dbu, 0), (c_all, s_c, s_hc, NS)):
                                sp.wait_ge(used, NC * g + q + 1)
                                src = d.bc[g][at + 4 * q:at + 4 * q + 4, :].rearrange("(a n) t -> a n t", a=1)
                                sp.dma_start(t[:, rows, :], src.broadcast_to([P, 4, T])).then_inc(s_t[q], 16)

            def body(b, j, more):
                g = b * NJ + j
                for i in range(3, KD):
                    block_in(g, i)
                    if i == 4:
                        sp.wait_ge(st_x1, 16 * g + 16)
                        sp.dma_start(x_res[:], x_view[b, j]).then_inc(s_x, 16)
                if more:
                    first_loads(g + 1)
                sp.wait_ge(s_res, KC * g + KC)
                sp.dma_start(d.x1[g], x_res[:]).then_inc(st_x1, 16)

            first_loads(0)
            for b in range(NB):
                with sp.Fori(0, NJ - 1) as j:
                    body(b, j, True)
                body(b, NJ - 1, b < NB - 1)
            sp.wait_ge(st_x1, 16 * NG + 16)


        @block.gpsimd
        def _(pool):
            pool.sem_inc(s_dbu, NQ)

            def body(b, j, g):
                for i in range(KD):
                    pool.wait_ge(s_blk[i % 4], 32 * g + 16 * (i // 4) + 16)
                    for q in range(NQ):
                        n = NC * g + NQ * i + q
                        if i == 0:
                            pool.wait_ge(s_b[q], 16 * g + 16)
                        pool.wait_ge(s_h, n + 1)
                        du = blk[:, i % 4, DU:DU + 1, :].broadcast_to([P, 4, T])
                        nc.gpsimd.tensor_tensor(dbu[:, q % 2], b_all[:, 4 * q:4 * q + 4, :], du,
                                                ALU.mult).then_inc(s_dbu, 1)

            chunks(pool, body)

        @block.scalar
        def _(act):
            def body(b, j, g):
                for i in range(KD):
                    act.wait_ge(s_blk[i % 4], 32 * g + 16 * (i // 4) + 16)
                    for q in range(NQ):
                        n = NC * g + NQ * i + q
                        act.wait_ge(s_h, n + 1)
                        for r in range(4):
                            c = i * NS + 4 * q + r
                            last = nc.scalar.activation(da[:, q % 2, r, :], blk[:, i % 4, DELTA, :], ACT.Exp,
                                                        scale=keep.neg_a[:, c:c + 1])
                        last.then_inc(s_da, 1)

            chunks(act, body)

        @block.tensor
        def _(pe):
            pe.sem_inc(s_acc, 2)
            pe.sem_inc(s_op, 2)
            pe.wait_ge(s_w, 16)
            pe.wait_ge(s_skip, KD)

            def body(b, j, g):
                def project(i):
                    n = KD * g + i
                    pe.wait_ge(s_yg, n + 5)
                    if i == 0:
                        pe.wait_ge(s_res, KC * g)
                    for m in range(KC):
                        last = nc.tensor.matmul(o_ps[:, m, :], w_out[:, i, m * P:(m + 1) * P], yg[:, i % 2, :],
                                                start=(i == 0), stop=(i == KD - 1))
                    last.then_inc(s_op, 1)

                for i in range(KD):
                    n = KD * g + i
                    pe.wait_ge(s_blk[i % 4], 32 * g + 16 * (i // 4) + 16)
                    pe.wait_ge(s_yg, n + 3)
                    nc.tensor.matmul(y_ps[:, i % 2, :], skip[:, i, :], blk[:, i % 4, U, :], start=True, stop=False)
                    for q in range(NQ):
                        pe.wait_ge(s_hc, NC * g + NQ * i + q + 1 + NQ)
                        for r in range(4):
                            last = nc.tensor.matmul(y_ps[:, i % 2, :], keep.ident[:], hc[:, q % 2, r, :],
                                                    start=False, stop=(q == NQ - 1 and r == 3))
                        last.then_inc(s_acc, 1)
                        if q == 2 and i:
                            project(i - 1)
                project(KD - 1)

            chunks(pe, body)

        @block.vector
        def _(dve):
            for i in range(KD):
                nc.vector.tensor_scalar(skip[:, i, :], keep.ident[:], keep.dskip[:, i:i + 1], None,
                                        ALU.mult).then_inc(s_skip, 1)
            dve.sem_inc(s_h, 2)
            dve.sem_inc(s_st, 2)
            dve.sem_inc(s_hc, NQ)
            dve.sem_inc(s_yg, 4)

            def before(b):
                dve.wait_ge(s_st, b * NJ * NC + 2)
                nc.vector.memset(state[:], 0.0).then_inc(s_zero, 1)
                dve.wait_ge(s_zero, b + 1)

            def body(b, j, g):
                def recur(k):
                    i, q = divmod(k, NQ)
                    n = NC * g + k
                    dve.wait_ge(s_da, n + 1)
                    dve.wait_ge(s_dbu, n + 1 + NQ)
                    dve.wait_ge(s_st, n + 1)
                    for r in range(4):
                        c = 4 * q + r
                        last = nc.vector.tensor_tensor_scan(h[:, k % 2, r, :], da[:, k % 2, r, :], dbu[:, k % 2, r, :],
                                                            state[:, i, c:c + 1], ALU.mult, ALU.add)
                    last.then_inc(s_h, 1)

                def weigh(k):
                    i, q = divmod(k, NQ)
                    n = NC * g + k
                    dve.wait_ge(s_h, n + 3)
                    if i == 0:
                        dve.wait_ge(s_c[q], 16 * g + 16)
                    dve.wait_ge(s_acc, n + 1)
                    nc.vector.tensor_tensor(hc[:, k % 2], h[:, k % 2], c_all[:, 4 * q:4 * q + 4, :],
                                            ALU.mult).then_inc(s_hc, 1)
                    nc.vector.tensor_copy(state[:, i, 4 * q:4 * q + 4], h[:, k % 2, :, T - 1]).then_inc(s_st, 1)

                def gate(i):
                    n = KD * g + i
                    dve.wait_ge(s_acc, NC * g + NQ * i + NQ + 2)
                    dve.wait_ge(s_op, n + 1)
                    nc.vector.tensor_tensor(yg[:, i % 2, :], y_ps[:, i % 2, :], blk[:, i % 4, Z, :],
                                            ALU.mult).then_inc(s_yg, 1)

                for k in range(NC):
                    recur(k)
                    if k:
                        weigh(k - 1)
                    if k % NQ == 2 and k > NQ:
                        gate(k // NQ - 1)
                weigh(NC - 1)
                gate(KD - 1)
                dve.wait_ge(s_x, 16 * g + 16)
                dve.wait_ge(s_op, KD * g + KD + 2)
                for m in range(KC):
                    nc.vector.tensor_tensor(x_res[:, m, :], x_res[:, m, :], o_ps[:, m, :], ALU.add).then_inc(s_add, 1)
                    dve.wait_ge(s_add, KC * g + m + 1)
                    nc.vector.bn_stats(keep.stats[:, b * KC + m, j, :], x_res[:, m, :]).then_inc(s_res, 1)

            chunks(dve, body, before)
            dve.wait_ge(s_res, KC * NG)


def memory_setup(nc, keep, d):
    with ExitStack() as ctx:
        w = Place(nc, ctx, "ms")
        mn = w.sb("mn", [P, KK, DIM])
        sq = w.sb("sq", [P, DIM])
        norm = w.sb("norm", [P, KK])
        tr = w.ps("tr", [P, 2, T])
        loads = w.sem("loads")
        s_sq = w.sem("squares")
        s_root = w.sem("root")
        step = w.sem("step")
        s_mn = w.sem("scaled")
        s_tr = w.sem("transposed")
        s_hi = w.sem("high")
        s_lo = w.sem("low")
        block = ctx.enter_context(nc.Block())
        HALVES = [(c, f) for c in range(KC) for f in range(KM // T)]
        PER = T // P

        @block.sync
        def _(sp):
            sp.dma_start(keep.m[:], d.m.rearrange("(k p) c -> p k c", p=P)).then_inc(loads, 16)
            sp.dma_start(keep.iota[:], d.iota.broadcast_to([P, KM])).then_inc(loads, 16)

        @block.scalar
        def _(act):
            act.wait_ge(loads, 32)
            for k in range(KK):
                if k:
                    act.wait_ge(s_sq, k)
                nc.scalar.activation(sq[:], keep.m[:, k, :], ACT.Square, accum_out=norm[:, k:k + 1]).then_inc(s_sq, 1)
            act.wait_ge(s_sq, KK)
            nc.scalar.activation(norm[:], norm[:], ACT.Sqrt).then_inc(s_root, 1)
            for n, (c, f) in enumerate(HALVES):
                act.wait_ge(s_tr, n + 1)
                nc.scalar.activation(keep.mt[0][:, c, f * T:(f + 1) * T], tr[:, n % 2, :], ACT.Copy).then_inc(s_hi, 1)

        @block.tensor
        def _(pe):
            pe.sem_inc(s_lo, 2)
            pe.wait_ge(s_mn, KK)
            for n, (c, f) in enumerate(HALVES):
                pe.wait_ge(s_lo, n + 1)
                for i in range(PER):
                    last = nc.tensor.transpose(tr[:, n % 2, i * P:(i + 1) * P], mn[:, f * PER + i, c * P:(c + 1) * P],
                                               keep.ident[:])
                last.then_inc(s_tr, 1)

        @block.vector
        def _(dve):
            dve.wait_ge(s_root, 1)
            nc.vector.tensor_scalar(norm[:], norm[:], NORM_EPS, None, ALU.max).then_inc(step, 1)
            dve.wait_ge(step, 1)
            nc.vector.reciprocal(norm[:], norm[:]).then_inc(step, 1)
            dve.wait_ge(step, 2)
            for k in range(KK):
                nc.vector.tensor_scalar(mn[:, k, :], keep.m[:, k, :], norm[:, k:k + 1], None, ALU.mult).then_inc(s_mn, 1)
            for n, (c, f) in enumerate(HALVES):
                cols = slice(f * T, (f + 1) * T)
                dve.wait_ge(s_hi, n + 1)
                nc.vector.tensor_tensor(keep.mt[1][:, c, cols], tr[:, n % 2, :], keep.mt[0][:, c, cols].bitcast(F32),
                                        ALU.subtract).then_inc(s_lo, 1)
            dve.wait_ge(s_lo, len(HALVES) + 2)


def assign(nc, keep, d):
    TT = T // P
    with ExitStack() as ctx:
        w = Place(nc, ctx, "as")
        x1 = w.sb("x1", [P, KC, T])
        v = w.sb("v", [P, KC, T])
        vp = [w.sb("v_hi", [P, KC, T], F32R), w.sb("v_lo", [P, KC, T], F32R)]
        xt = [w.sb("xt_hi", [P, TT, DIM], F32R), w.sb("xt_lo", [P, TT, DIM], F32R)]
        sq = w.sb("sq", [P, DIM])
        ss = w.sb("ss", [P, TT])
        nrm = w.sb("nrm", [P, TT])
        rn = w.sb("rn", [P, TT])
        top = w.sb("top", [P, TT, 8])
        nb = w.sb("nb", [P, TT])
        idx = w.sb("idx", [P, TT, 8], U32)
        idxf = w.sb("idxf", [P, TT])
        oh = w.sb("oh", [P, TT, KM], F32R)
        e = w.sb("e", [P, 2, KM])
        es = w.sb("es", [P, TT])
        er = w.sb("er", [P, TT])
        et = w.sb("et", [P, KK, T])
        sc_ps = w.ps("sc_ps", [P, 2, KM])
        tr_ps = w.ps("tr_ps", [P, 2, T])
        sum_ps = w.ps("sum_ps", [P, 2, T])

        s_x = w.sem("x1_loaded")
        s_v = w.sem("v_done")
        s_vh = w.sem("v_hi_done")
        s_vl = w.sem("v_lo_done")
        s_tr = w.sem("transposed")
        s_xh = w.sem("xt_hi_done")
        s_ss = w.sem("squares")
        s_xl = w.sem("xt_lo_done")
        s_nr = w.sem("norm_done")
        s_cl = w.sem("norm_clamped")
        s_rn = w.sem("rn_done")
        s_sc = w.sem("scored")
        s_top = w.sem("top_done")
        s_nb = w.sem("bias_done")
        s_ix = w.sem("index_done")
        s_if = w.sem("index_float")
        s_oh = w.sem("onehot_done")
        s_ex = w.sem("exp_done")
        s_er = w.sem("exp_sum_inverted")
        s_en = w.sem("softmax_done")
        s_et = w.sem("softmax_turned")
        s_sp = w.sem("sums_done")
        s_ad = w.sem("sums_added")
        s_ct = w.sem("counted")
        s_zc = w.sem("count_zeroed")
        s_zs = w.sem("sums_zeroed")
        st_e = w.sem("softmax_stored")
        block = ctx.enter_context(nc.Block())
        NTR = 3 * TT

        def batches(eng, prologue, main, peeled=1):
            for b in range(NB):
                prologue(b, b * NJ)
                with eng.Fori(0, NJ - peeled) as j:
                    main(b, b * NJ + j, peeled)
                for j in range(NJ - peeled, NJ):
                    main(b, b * NJ + j, NJ - 1 - j)

        @block.sync
        def _(sp):
            def load(g):
                sp.dma_start(x1[:], d.x1[g]).then_inc(s_x, 16)

            def prologue(b, g):
                load(g)
                sp.wait_ge(s_v, g + 1)
                load(g + 1)

            def main(b, g, ahead):
                if ahead >= 1:
                    sp.wait_ge(s_v, g + 2)
                if ahead >= 2:
                    load(g + 2)
                sp.wait_ge(s_et, 2 * TT * g + 2 * TT)
                sp.dma_start(d.soft[g], et[:]).then_inc(st_e, 16)

            batches(sp, prologue, main, 2)
            sp.wait_ge(st_e, 16 * NG)

        @block.gpsimd
        def _(pool):
            nc.gpsimd.memset(keep.count[:], 0.0).then_inc(s_zc, 1)
            pool.wait_ge(s_zc, 1)

            def main(b, g, ahead):
                for s in range(TT):
                    n = TT * g + s
                    pool.wait_ge(s_oh, n + 3)
                    pool.wait_ge(s_ct, n)
                    nc.gpsimd.tensor_tensor(keep.count[:], keep.count[:], oh[:, s, :].bitcast(F32),
                                            ALU.add).then_inc(s_ct, 1)

            batches(pool, lambda b, g: None, main)
            pool.wait_ge(s_ct, TT * NG)

        @block.scalar
        def _(act):
            def norm_v(b, g):
                act.wait_ge(s_x, 16 * g + 16)
                act.wait_ge(s_vl, g)
                act.wait_ge(s_tr, NTR * g)
                for k in range(KC):
                    c = b * KC + k
                    last = nc.scalar.activation(v[:, k, :], x1[:, k, :], ACT.Identity,
                                                bias=keep.shift[:, c:c + 1], scale=keep.scale[:, c:c + 1])
                last.then_inc(s_v, 1)

            def split(g):
                act.wait_ge(s_v, g + 1)
                act.wait_ge(s_sc, TT * g)
                nc.scalar.activation(vp[0][:], v[:], ACT.Copy).then_inc(s_vh, 1)

            def norm_ahead(b, g):
                act.wait_ge(s_x, 16 * g + 16)
                act.wait_ge(s_vl, g)
                act.wait_ge(s_tr, NTR * (g - 1) + TT)
                for k in range(KC):
                    c = b * KC + k
                    last = nc.scalar.activation(v[:, k, :], x1[:, k, :], ACT.Identity,
                                                bias=keep.shift[:, c:c + 1], scale=keep.scale[:, c:c + 1])
                last.then_inc(s_v, 1)

            def exp(g, s):
                act.wait_ge(s_nb, TT * g + s + 1)
                act.wait_ge(s_ix, TT * g + s + 1)
                act.wait_ge(s_tr, NTR * g + (TT + 2 * (s - 2) + 2 if s >= 2 else 0))
                nc.scalar.activation(e[:, s % 2, :], sc_ps[:, s % 2, :], ACT.Exp, bias=nb[:, s:s + 1],
                                     scale=rn[:, s:s + 1], accum_out=es[:, s:s + 1]).then_inc(s_ex, 1)

            def turned(g, s):
                if s == 0:
                    act.wait_ge(st_e, 16 * g)
                for f in range(2):
                    r = TT + 2 * s + f
                    act.wait_ge(s_tr, NTR * g + r + 1)
                    nc.scalar.activation(et[:, 4 * f:4 * f + 4, s * P:(s + 1) * P],
                                         tr_ps[:, r % 2, :].rearrange("p (k t) -> p k t", t=P), ACT.Copy).then_inc(s_et, 1)

            def main(b, g, ahead):
                for s in range(TT):
                    act.wait_ge(s_tr, NTR * g + s + 1)
                    if s == 0:
                        act.wait_ge(s_sp, KK * g)
                    nc.scalar.activation(xt[0][:, s, :], tr_ps[:, s % 2, :], ACT.Copy).then_inc(s_xh, 1)
                    act.wait_ge(s_ss, TT * g + s)
                    nc.scalar.activation(sq[:], tr_ps[:, s % 2, :], ACT.Square, accum_out=ss[:, s:s + 1]).then_inc(s_ss, 1)
                act.wait_ge(s_ss, TT * g + TT)
                act.wait_ge(s_cl, g)
                nc.scalar.activation(nrm[:], ss[:], ACT.Sqrt).then_inc(s_nr, 1)
                exp(g, 0)
                for s in range(1, TT):
                    exp(g, s)
                    turned(g, s - 1)
                if ahead:
                    norm_ahead(b, g + 1)
                    split(g + 1)
                turned(g, TT - 1)

            def prologue(b, g):
                norm_v(b, g)
                split(g)

            act.sem_inc(s_ex, 2)
            batches(act, prologue, main)

        @block.tensor
        def _(pe):
            def turn_exp(g, s):
                pe.wait_ge(s_en, TT * g + s + 1)
                for f in range(2):
                    r = TT + 2 * s + f
                    if r - 2 < TT:
                        pe.wait_ge(s_xl, TT * g + r - 1)
                        pe.wait_ge(s_ss, TT * g + r - 1)
                    else:
                        pe.wait_ge(s_et, 2 * TT * g + r - 1 - TT)
                    for i in range(4):
                        k = 4 * f + i
                        last = nc.tensor.transpose(tr_ps[:, r % 2, i * P:(i + 1) * P], e[:, s % 2, k * P:(k + 1) * P],
                                                   keep.ident[:])
                    last.then_inc(s_tr, 1)

            def main(b, g, ahead):
                pe.wait_ge(s_v, g + 1)
                pe.wait_ge(s_et, 2 * TT * g)
                for s in range(TT):
                    if s >= 2:
                        pe.wait_ge(s_xl, TT * g + s - 1)
                        pe.wait_ge(s_ss, TT * g + s - 1)
                    for k in range(KC):
                        last = nc.tensor.transpose(tr_ps[:, s % 2, k * P:(k + 1) * P], v[:, k, s * P:(s + 1) * P],
                                                   keep.ident[:])
                    last.then_inc(s_tr, 1)
                pe.wait_ge(s_vh, g + 1)
                pe.wait_ge(s_vl, g + 1)
                for s in range(TT):
                    n = TT * g + s
                    pe.wait_ge(s_ex, n + 1)
                    pe.wait_ge(s_oh, n + 1)
                    for f in range(KM // T):
                        cols = slice(f * T, (f + 1) * T)
                        for k in range(KC):
                            last = split_matmul(nc, sc_ps[:, s % 2, cols], [t[:, k, s * P:(s + 1) * P] for t in vp],
                                                [t[:, k, cols] for t in keep.mt], k == 0, k == KC - 1)
                    last.then_inc(s_sc, 1)
                    if s:
                        turn_exp(g, s - 1)
                pe.wait_ge(s_oh, TT * g + TT + 2)
                pe.wait_ge(s_xl, TT * g + TT)
                for k in range(KK):
                    pe.wait_ge(s_ad, KK * g + k + 1)
                    for s in range(TT):
                        nc.tensor.matmul(sum_ps[:, k % 2, :], oh[:, s, k * P:(k + 1) * P], xt[0][:, s, :],
                                         start=(s == 0), stop=False)
                        last = nc.tensor.matmul(sum_ps[:, k % 2, :], oh[:, s, k * P:(k + 1) * P], xt[1][:, s, :],
                                                start=False, stop=(s == TT - 1))
                    last.then_inc(s_sp, 1)
                    if k == 1:
                        turn_exp(g, TT - 1)

            batches(pe, lambda b, g: None, main)

        @block.vector
        def _(dve):
            nc.vector.memset(keep.sums[:], 0.0).then_inc(s_zs, 1)
            dve.wait_ge(s_zs, 1)
            dve.sem_inc(s_oh, 2)
            dve.sem_inc(s_ad, 2)

            def split(g):
                dve.wait_ge(s_vh, g + 1)
                nc.vector.tensor_tensor(vp[1][:], v[:], vp[0][:].bitcast(F32), ALU.subtract).then_inc(s_vl, 1)

            def nearest(g, s):
                n = TT * g + s
                dve.wait_ge(s_sc, n + 1)
                nc.vector.memset(nb[:, s:s + 1], 0.0)
                nc.vector.max(top[:, s, :], sc_ps[:, s % 2, :]).then_inc(s_top, 1)
                dve.wait_ge(s_top, n + 1)
                nc.vector.tensor_scalar(nb[:, s:s + 1], top[:, s, 0:1], rn[:, s:s + 1], -1.0, ALU.mult,
                                        ALU.mult).then_inc(s_nb, 1)
                nc.vector.max_index(idx[:, s, :], top[:, s, :], sc_ps[:, s % 2, :]).then_inc(s_ix, 1)
                dve.wait_ge(s_ix, n + 1)
                nc.vector.tensor_copy(idxf[:, s:s + 1], idx[:, s, 0:1]).then_inc(s_if, 1)
                dve.wait_ge(s_if, n + 1)
                if s == 0:
                    dve.wait_ge(s_ct, TT * g)
                    dve.wait_ge(s_sp, KK * g)
                nc.vector.tensor_scalar(oh[:, s, :], keep.iota[:], idxf[:, s:s + 1], None, ALU.is_equal).then_inc(s_oh, 1)

            def softmax(g, s):
                n = TT * g + s
                dve.wait_ge(s_ex, n + 3)
                nc.vector.reciprocal(er[:, s:s + 1], es[:, s:s + 1]).then_inc(s_er, 1)
                dve.wait_ge(s_er, n + 1)
                nc.vector.tensor_scalar(e[:, s % 2, :], e[:, s % 2, :], er[:, s:s + 1], None, ALU.mult).then_inc(s_en, 1)

            def main(b, g, ahead):
                for s in range(TT):
                    dve.wait_ge(s_xh, TT * g + s + 1)
                    dve.wait_ge(s_ss, TT * g + s + 1)
                    nc.vector.tensor_tensor(xt[1][:, s, :], tr_ps[:, s % 2, :], xt[0][:, s, :].bitcast(F32),
                                            ALU.subtract).then_inc(s_xl, 1)
                dve.wait_ge(s_nr, g + 1)
                nc.vector.tensor_scalar(rn[:], nrm[:], NORM_EPS, None, ALU.max).then_inc(s_cl, 1)
                dve.wait_ge(s_cl, g + 1)
                nc.vector.reciprocal(rn[:], rn[:]).then_inc(s_rn, 1)
                dve.wait_ge(s_rn, g + 1)
                nearest(g, 0)
                for s in range(1, TT):
                    nearest(g, s)
                    softmax(g, s - 1)
                softmax(g, TT - 1)
                for k in range(KK):
                    n = KK * g + k
                    dve.wait_ge(s_sp, n + 1)
                    nc.vector.tensor_tensor(keep.sums[:, k, :], keep.sums[:, k, :], sum_ps[:, k % 2, :],
                                            ALU.add).then_inc(s_ad, 1)
                    if k == 2 and ahead:
                        split(g + 1)

            batches(dve, lambda b, g: split(g), main)
            dve.wait_ge(s_ad, KK * NG + 2)


def readout(nc, keep, d):
    with ExitStack() as ctx:
        w = Place(nc, ctx, "ro")
        nm = [w.sb("nm_hi", [P, KK, DIM], F32R), w.sb("nm_lo", [P, KK, DIM], F32R)]
        share = w.sb("share", [P, KK])
        ones = w.sb("ones", [P, 1])
        et = w.sb("et", [P, KK, T])
        ep = [w.sb("e_hi", [P, 2, KK, T], F32R), w.sb("e_lo", [P, 2, KK, T], F32R)]
        x1 = w.sb("x1", [P, 2, KC, T])
        o_ps = w.ps("o_ps", [P, 2, KC, T])

        s_step = w.sem("step")
        s_one = w.sem("ones_set")
        s_cnt = w.sem("counts_done")
        s_nm = w.sem("new_m_done")
        s_nh = w.sem("new_m_hi")
        s_nl = w.sem("new_m_lo")
        s_e = w.sem("softmax_loaded")
        s_x = [w.sem(f"x1_loaded{i}") for i in range(2)]
        s_eh = w.sem("e_hi_done")
        s_el = w.sem("e_lo_done")
        s_o = w.sem("out_summed")
        s_r = w.sem("residual_added")
        s_st = [w.sem(f"out_stored{i}") for i in range(2)]
        block = ctx.enter_context(nc.Block())
        out_view = d.out.rearrange("b (k p) (j r) w -> b j p k (r w)", p=P, j=NJ)

        def chunks(eng, body):
            for b in range(NB):
                with eng.Fori(0, NJ // 2) as i:
                    for u in range(2):
                        body(b, 2 * i + u, b * NJ + 2 * i + u, u, b * (NJ // 2) + i)

        @block.sync
        def _(sp):
            def body(b, j, g, u, i):
                sp.wait_ge(s_el, g)
                sp.dma_start(et[:], d.soft[g]).then_inc(s_e, 16)
                sp.wait_ge(s_st[u], 16 * i)
                sp.dma_start(x1[:, u], d.x1[g]).then_inc(s_x[u], 16)

            chunks(sp, body)

        @block.gpsimd
        def _(pool):
            def body(b, j, g, u, i):
                pool.wait_ge(s_r, KC * g + 3 * KC)
                pool.dma_start(out_view[b, j], x1[:, u]).then_inc(s_st[u], 16)

            chunks(pool, body)
            for u in range(2):
                pool.wait_ge(s_st[u], 16 * NG // 2)

        @block.scalar
        def _(act):
            act.wait_ge(s_nm, KK)
            nc.scalar.activation(nm[0][:], keep.m[:], ACT.Copy).then_inc(s_nh, 1)

            def body(b, j, g, u, i):
                act.wait_ge(s_e, 16 * g + 16)
                act.wait_ge(s_o, KC * g + KC)
                nc.scalar.activation(ep[0][:, u], et[:], ACT.Copy).then_inc(s_eh, 1)

            chunks(act, body)

        @block.tensor
        def _(pe):
            pe.sem_inc(s_o, 2 * KC)
            pe.wait_ge(s_one, 1)
            for k in range(KK):
                last = nc.tensor.matmul(o_ps[:, 0, 0, k:k + 1], keep.count[:, k * P:(k + 1) * P], ones[:],
                                        start=True, stop=True)
            last.then_inc(s_cnt, 1)
            pe.wait_ge(s_nl, 1)

            def body(b, j, g, u, i):
                pe.wait_ge(s_eh, g + 1)
                pe.wait_ge(s_el, g + 1)
                for m in range(KC):
                    pe.wait_ge(s_r, KC * g + m + 1)
                    for k in range(KK):
                        last = split_matmul(nc, o_ps[:, u, m, :], [t[:, k, m * P:(m + 1) * P] for t in nm],
                                            [t[:, u, k, :] for t in ep], k == 0, k == KK - 1)
                    last.then_inc(s_o, 1)

            chunks(pe, body)

        @block.vector
        def _(dve):
            dve.sem_inc(s_r, 2 * KC)
            nc.vector.memset(ones[:], 1.0).then_inc(s_one, 1)
            nc.vector.tensor_scalar(keep.m[:], keep.m[:], RATE, None, ALU.mult).then_inc(s_step, 1)
            dve.wait_ge(s_cnt, 1)
            nc.vector.tensor_scalar(share[:], o_ps[:, 0, 0, 0:KK], MEAN_EPS, None, ALU.add).then_inc(s_step, 1)
            dve.wait_ge(s_step, 2)
            nc.vector.reciprocal(share[:], share[:]).then_inc(s_step, 1)
            dve.wait_ge(s_step, 3)
            nc.vector.tensor_scalar(share[:], share[:], 1.0 - RATE, None, ALU.mult).then_inc(s_step, 1)
            dve.wait_ge(s_step, 4)
            for k in range(KK):
                nc.vector.scalar_tensor_tensor(keep.m[:, k, :], keep.sums[:, k, :], share[:, k:k + 1], keep.m[:, k, :],
                                               ALU.mult, ALU.add).then_inc(s_nm, 1)
            dve.wait_ge(s_nh, 1)
            nc.vector.tensor_tensor(nm[1][:], keep.m[:], nm[0][:].bitcast(F32), ALU.subtract).then_inc(s_nl, 1)

            def body(b, j, g, u, i):
                dve.wait_ge(s_eh, g + 1)
                nc.vector.tensor_tensor(ep[1][:, u], et[:], ep[0][:, u].bitcast(F32), ALU.subtract).then_inc(s_el, 1)
                dve.wait_ge(s_x[u], 16 * i + 16)
                for m in range(KC):
                    dve.wait_ge(s_o, KC * g + m + 1 + 2 * KC)
                    nc.vector.tensor_tensor(x1[:, u, m, :], x1[:, u, m, :], o_ps[:, u, m, :], ALU.add).then_inc(s_r, 1)

            chunks(dve, body)


class Names:
    pass


def program(nc, d):
    d.spill = nc.dram_tensor("spill", (NG, P, KD, 4, T), F32).ap()
    d.bc = nc.dram_tensor("bc", (NG, 2 * NS, T), F32).ap()
    d.x1 = nc.dram_tensor("x1", (NG, P, KC, T), F32).ap()
    d.soft = nc.dram_tensor("soft", (NG, P, KK, T), F32).ap()
    keep = Names()
    with ExitStack() as all_phases:
        w = Place(nc, all_phases, "keep")
        keep.ident = w.sb("ident", [P, P])
        keep.gavg = w.sb("gavg", [P, P])
        keep.gn_eps = w.sb("gn_eps", [P, 1])
        keep.stats = w.sb("stats", [P, NB * KC, NJ, 6])
        keep.scale = w.sb("scale", [P, NB * KC])
        keep.shift = w.sb("shift", [P, NB * KC])
        with ExitStack() as mamba:
            w = Place(nc, mamba, "l0")
            keep.neg_a = w.sb("neg_a", [P, KD * NS])
            keep.dskip = w.sb("dskip", [P, KD])
            with ExitStack() as first:
                w = Place(nc, first, "l0f")
                keep.w_in = [w.sb("w_in_hi", [P, KC, 2 * DI], F32R), w.sb("w_in_lo", [P, KC, 2 * DI], F32R)]
                keep.b_in = w.sb("b_in", [P, 2 * KD])
                keep.mean_w = w.sb("mean_w", [P, P])
                keep.conv_w = w.sb("conv_w", [P, KD, TAPS])
                keep.conv_b = w.sb("conv_b", [P, KD])
                keep.w_xp = w.sb("w_xp", [P, KD, 64])
                keep.w_dt = w.sb("w_dt", [RANK + 1, DI])
                setup(nc, keep, d)
                group_params(nc, "g1", keep, keep.stats, keep.scale, keep.shift)
                front(nc, keep, d)
            scan(nc, keep, d)
        group_params(nc, "g2", keep, keep.stats, keep.scale, keep.shift)
        with ExitStack() as memory:
            w = Place(nc, memory, "l1")
            keep.m = w.sb("m", [P, KK, DIM])
            keep.sums = w.sb("sums", [P, KK, DIM])
            keep.count = w.sb("count", [P, KM])
            with ExitStack() as scores:
                w = Place(nc, scores, "l1s")
                keep.mt = [w.sb("mt_hi", [P, KC, KM], F32R), w.sb("mt_lo", [P, KC, KM], F32R)]
                keep.iota = w.sb("iota", [P, KM])
                memory_setup(nc, keep, d)
                assign(nc, keep, d)
            readout(nc, keep, d)


def kernel(**inputs):
    import numpy as np
    from concourse import bacc
    from concourse.bass_utils import run_bass_kernel_spmd

    a = {k.replace("L0_conv_", "").replace("L1_conv_", ""): np.asarray(v) for k, v in inputs.items()}
    rows = lambda t: t.reshape(-1, P, *t.shape[1:]).swapaxes(0, 1)
    channel = np.arange(P)
    arrays = {
        "x": a["x"],
        "m": a["m"],
        "w_in": rows(a["in_proj_w"].T),
        "w_out": rows(a["out_proj_w"].T),
        "w_xp": rows(a["x_proj_w"].T),
        "w_dt": a["dt_proj_w"].T,
        "b_dt": a["dt_proj_b"][None, :],
        "ln_w": rows(a["ln_w"]),
        "ln_b": rows(a["ln_b"]),
        "conv_w": rows(a["conv_w"]),
        "conv_b": rows(a["conv_b"]),
        "d_skip": rows(a["D_skip"]),
        "a_log": rows(a["A_log"]).reshape(P, -1),
        "ident": np.eye(P, dtype=np.float32),
        "gavg": ((channel[:, None] // 16 == channel[None, :] // 16) / np.float32(16)).astype(np.float32),
        "iota": np.arange(KM, dtype=np.float32)[None, :],
    }
    nc = bacc.Bacc("TRN2", target_bir_lowering=False, num_devices=1)
    d = Names()
    sent = {}
    for name, value in arrays.items():
        value = np.ascontiguousarray(value)
        sent[f"in_{name}"] = value
        d.__dict__[name] = nc.dram_tensor(f"in_{name}", value.shape, mybir.dt.from_np(value.dtype), kind="ExternalInput").ap()
    d.out = nc.dram_tensor("out", (NB, DIM, 64, 64), F32, kind="ExternalOutput").ap()
    program(nc, d)
    r = run_bass_kernel_spmd(nc, [sent], core_ids=[0])
    return r.results[0]["out"]
```

```python
from contextlib import ExitStack

import concourse.bass as bass
from concourse import mybir

F32 = mybir.dt.float32
F32R = mybir.dt.float32r
U32 = mybir.dt.uint32
ALU = mybir.AluOpType
ACT = mybir.ActivationFunctionType
AXX = mybir.AxisListType.X

P = 128
NB = 2
L = 64 * 64
T = 512
NJ = L // T
NG = NB * NJ
DIM = 512
KC = DIM // P
DI = 1024
KD = DI // P
NS = 16
RANK = 32
TAPS = 4
HIST = TAPS - 1
KM = 1024
KK = KM // P
GN_EPS = 1e-5
LN_EPS = 1e-5
NORM_EPS = 1e-12
MEAN_EPS = 1e-6
RATE = 0.999
DELTA, DU, U, Z = range(4)


class Place:

    def __init__(self, nc, ctx, tag):
        self.nc, self.ctx, self.tag = nc, ctx, tag

    def sb(self, name, shape, dt=F32):
        return self.ctx.enter_context(self.nc.sbuf_tensor(f"{self.tag}_{name}", shape, dt))

    def ps(self, name, shape, dt=F32):
        return self.ctx.enter_context(self.nc.psum_tensor(f"{self.tag}_{name}", shape, dt))

    def sem(self, name):
        return self.ctx.enter_context(self.nc.semaphore(f"{self.tag}_{name}"))


def split_matmul(nc, out, lhs, rhs, start, stop):
    nc.tensor.matmul(out, lhs[0], rhs[0], start=start, stop=False)
    nc.tensor.matmul(out, lhs[1], rhs[0], start=False, stop=False)
    return nc.tensor.matmul(out, lhs[0], rhs[1], start=False, stop=stop)


def group_params(nc, tag, keep, stats, scale, shift):
    n = NB * KC
    with ExitStack() as ctx:
        w = Place(nc, ctx, tag)
        mv = w.sb("mv", [P, n, 2])
        mean = w.sb("mean", [P, n])
        dev = w.sb("dev", [P, n])
        spread = w.sb("spread", [P, n])
        std = w.sb("std", [P, n])
        ps = w.ps("ps", [P, 2, T])
        step = w.sem("step")
        mean_ps = w.sem("mean_ps")
        var_ps = w.sem("var_ps")
        std_done = w.sem("std_done")
        block = ctx.enter_context(nc.Block())

        @block.vector
        def _(dve):
            for i in range(n):
                nc.vector.bn_aggr(mv[:, i, :], stats[:, i, :, :]).then_inc(step, 1)
            dve.wait_ge(step, n)
            nc.vector.tensor_copy(mean[:], mv[:, :, 0]).then_inc(step, 1)
            dve.wait_ge(mean_ps, 1)
            dve.wait_ge(step, n + 1)
            nc.vector.tensor_tensor(dev[:], mean[:], ps[:, 0, 0:n], ALU.subtract).then_inc(step, 1)
            dve.wait_ge(step, n + 2)
            nc.vector.tensor_tensor(dev[:], dev[:], dev[:], ALU.mult).then_inc(step, 1)
            dve.wait_ge(step, n + 3)
            nc.vector.tensor_tensor(spread[:], dev[:], mv[:, :, 1], ALU.add).then_inc(step, 1)
            dve.wait_ge(std_done, 1)
            nc.vector.reciprocal(scale[:], std[:]).then_inc(step, 1)
            dve.wait_ge(step, n + 5)
            nc.vector.scalar_tensor_tensor(shift[:], ps[:, 0, 0:n], -1.0, scale[:], ALU.mult, ALU.mult).then_inc(step, 1)
            dve.wait_ge(step, n + 6)

        @block.tensor
        def _(pe):
            pe.wait_ge(step, n + 1)
            nc.tensor.matmul(ps[:, 0, 0:n], keep.gavg[:], mean[:], start=True, stop=True).then_inc(mean_ps, 1)
            pe.wait_ge(step, n + 4)
            nc.tensor.matmul(ps[:, 1, 0:n], keep.gavg[:], spread[:], start=True, stop=True).then_inc(var_ps, 1)

        @block.scalar
        def _(act):
            act.wait_ge(var_ps, 1)
            nc.scalar.activation(std[:], ps[:, 1, 0:n], ACT.Sqrt, bias=keep.gn_eps[:, 0:1]).then_inc(std_done, 1)


def setup(nc, keep, d):
    with ExitStack() as ctx:
        w = Place(nc, ctx, "su")
        wf = w.sb("wf", [P, KC, 2 * DI])
        lnw = w.sb("lnw", [P, KC])
        lnb = w.sb("lnb", [P, KC])
        alog = w.sb("alog", [P, KD * NS])
        xt = w.sb("xt", [P, 4, L])
        bias_ps = w.ps("bias_ps", [P, T])
        consts = w.sem("consts")
        weights = w.sem("weights")
        x_tile = [w.sem(f"x_tile{i}") for i in range(4)]
        eps_set = w.sem("eps_set")
        stats_done = w.sem("stats_done")
        bias_done = w.sem("bias_done")
        exp_done = w.sem("exp_done")
        scaled = w.sem("scaled")
        high = w.sem("high")
        rest = w.sem("rest")
        n_const = 11
        block = ctx.enter_context(nc.Block())
        x_rows = d.x.rearrange("b (k p) h w -> (b k) p (h w)", p=P)

        @block.sync
        def _(sp):
            sp.dma_start(wf[:], d.w_in).then_inc(weights, 16)
            with sp.Fori(0, NB * KC // 4) as i:
                for s in range(4):
                    sp.wait_ge(stats_done, 4 * i + s + 1)
                    sp.dma_start(xt[:, s, :], x_rows[4 * i + s]).then_inc(x_tile[s], 16)

        @block.gpsimd
        def _(pool):
            for dst, src in ((keep.ident, d.ident), (keep.gavg, d.gavg), (lnw, d.ln_w), (lnb, d.ln_b), (alog, d.a_log),
                             (keep.conv_w, d.conv_w), (keep.conv_b, d.conv_b), (keep.dskip, d.d_skip), (keep.w_xp, d.w_xp)):
                pool.dma_start(dst[:], src).then_inc(consts, 16)
            pool.dma_start(keep.w_dt[0:RANK, :], d.w_dt).then_inc(consts, 16)
            pool.dma_start(keep.w_dt[RANK:RANK + 1, :], d.b_dt).then_inc(consts, 16)

        @block.scalar
        def _(act):
            act.wait_ge(consts, 16 * n_const)
            nc.scalar.activation(alog[:], alog[:], ACT.Exp).then_inc(exp_done, 1)
            act.wait_ge(scaled, KC)
            nc.scalar.activation(keep.w_in[0][:], wf[:], ACT.Copy).then_inc(high, 1)

        @block.tensor
        def _(pe):
            pe.wait_ge(consts, 16 * n_const)
            pe.wait_ge(weights, 16)
            for m in range(2 * KD):
                for k in range(KC):
                    last = nc.tensor.matmul(bias_ps[:, m:m + 1], wf[:, k, m * P:(m + 1) * P], lnb[:, k:k + 1],
                                            start=(k == 0), stop=(k == KC - 1))
            last.then_inc(bias_done, 1)

        @block.vector
        def _(dve):
            nc.vector.memset(keep.gn_eps[:], GN_EPS).then_inc(eps_set, 1)
            nc.vector.memset(keep.mean_w[:], 1.0 / DIM).then_inc(eps_set, 1)
            dve.sem_inc(stats_done, 4)
            dve.wait_ge(consts, 16 * n_const)
            dve.wait_ge(weights, 16)
            dve.wait_ge(bias_done, 1)
            nc.vector.tensor_copy(keep.b_in[:], bias_ps[:, 0:2 * KD]).then_inc(rest, 1)
            for k in range(KC):
                nc.vector.tensor_scalar(wf[:, k, :], wf[:, k, :], lnw[:, k:k + 1], None, ALU.mult).then_inc(scaled, 1)
            dve.wait_ge(exp_done, 1)
            nc.vector.tensor_scalar(keep.neg_a[:], alog[:], -1.0, None, ALU.mult).then_inc(rest, 1)
            with dve.Fori(0, NB * KC // 4) as i:
                for s in range(4):
                    dve.wait_ge(x_tile[s], 16 * i + 16)
                    for j in range(NJ):
                        last = nc.vector.bn_stats(keep.stats[:, 4 * i + s, j, :], xt[:, s, j * T:(j + 1) * T])
                    last.then_inc(stats_done, 1)
            dve.wait_ge(high, 1)
            nc.vector.tensor_tensor(keep.w_in[1][:], wf[:], keep.w_in[0][:].bitcast(F32), ALU.subtract).then_inc(rest, 1)
            dve.wait_ge(rest, 3)
            dve.wait_ge(eps_set, 2)


def front(nc, keep, d):
    with ExitStack() as ctx:
        w = Place(nc, ctx, "fr")
        RING = 6
        v = w.sb("v", [P, KC, T])
        sd = w.sb("sd", [P, T])
        rs = w.sb("rs", [P, T])
        xn = [w.sb("xn_hi", [P, KC, T], F32R), w.sb("xn_lo", [P, KC, T], F32R)]
        xr = w.sb("xr", [P, 2, HIST + T])
        hist = w.sb("hist", [P, KD, HIST])
        acc = w.sb("acc", [P, 2, T])
        u = w.sb("u", [P, KD, T])
        z = w.sb("z", [P, KD, T])
        delta = w.sb("delta", [P, KD, T])
        du = w.sb("du", [P, KD, T])
        e = w.sb("e", [P, KD, T])
        u1 = w.sb("u1", [P, 2, T])
        dt = w.sb("dt", [RANK + 1, T])
        bc = w.sb("bc", [64, T])
        mm = w.ps("mm", [P, RING, T])
        st_ps = w.ps("st_ps", [P, T])
        xd_ps = w.ps("xd_ps", [64, T])
        sq = e[:, 0:KC, :]

        s_x = w.sem("x_loaded")
        s_v = w.sem("v_done")
        s_mu = w.sem("mu_done")
        s_vc = w.sem("centred")
        s_sq = w.sem("squared")
        s_var = w.sem("var_done")
        s_sd = w.sem("sd_done")
        s_rs = w.sem("rs_done")
        s_xn = w.sem("xn_done")
        s_xh = w.sem("xn_hi_done")
        s_xl = w.sem("xn_lo_done")
        s_mm = w.sem("mm_done")
        s_ev = w.sem("mm_evacuated")
        s_cs = w.sem("conv_step")
        s_cv = w.sem("conv_done")
        s_u = w.sem("u_done")
        s_xd = w.sem("xdbl_done")
        s_dt = w.sem("dt_copied")
        s_bc = w.sem("bc_copied")
        s_ab = w.sem("abs_done")
        s_e = w.sem("e_done")
        s_rl = w.sem("relu_done")
        s_u1 = w.sem("one_plus_e")
        s_c = w.sem("rounding_error_found")
        s_rc = w.sem("rounding_error_taken")
        s_ln = w.sem("ln_done")
        s_dl = w.sem("delta_done")
        s_du = w.sem("du_done")
        s_zero = w.sem("hist_zeroed")
        s_one = w.sem("ones_set")
        st_u = w.sem("u_stored")
        st_z = w.sem("z_stored")
        st_bc = w.sem("bc_stored")
        st_dl = w.sem("delta_stored")
        st_du = w.sem("du_stored")
        block = ctx.enter_context(nc.Block())
        x_view = d.x.rearrange("b (k p) (j r) w -> b j p k (r w)", p=P, j=NJ)
        NQ = 2 * KD + KD

        def batches(eng, prologue, main, peeled=1):
            for b in range(NB):
                prologue(b, b * NJ)
                with eng.Fori(0, NJ - peeled) as j:
                    main(b, j, peeled)
                for j in range(NJ - peeled, NJ):
                    main(b, j, NJ - 1 - j)

        @block.sync
        def _(sp):
            def load(b, j, g):
                sp.wait_ge(s_xl, g + 1)
                sp.dma_start(v[:], x_view[b, j]).then_inc(s_x, 16)

            def prologue(b, g):
                load(b, 0, g)
                load(b, 1, g + 1)

            def main(b, j, ahead):
                g = b * NJ + j
                sp.wait_ge(s_ev, 2 * KD * g + 2 * KD)
                sp.dma_start(d.spill[g][:, :, Z, :], z[:]).then_inc(st_z, 16)
                sp.wait_ge(s_u, KD * g + KD + 2)
                sp.dma_start(d.spill[g][:, :, U, :], u[:]).then_inc(st_u, 16)
                sp.wait_ge(s_bc, g + 2)
                sp.dma_start(d.bc[g], bc[RANK:64, :]).then_inc(st_bc, 16)
                if ahead >= 2:
                    load(b, j + 2, g + 2)
                sp.wait_ge(s_du, KD * g + KD + KD)
                sp.dma_start(d.spill[g][:, :, DU, :], du[:]).then_inc(st_du, 16)
                sp.dma_start(d.spill[g][:, :, DELTA, :], delta[:]).then_inc(st_dl, 16)

            for s in (st_u, st_z, st_bc, st_dl, st_du):
                sp.sem_inc(s, 16)
            batches(sp, prologue, main, 2)
            for s in (st_u, st_z, st_bc, st_dl, st_du):
                sp.wait_ge(s, 16 * NG + 16)

        @block.gpsimd
        def _(pool):
            def main(b, j, ahead):
                g = b * NJ + j
                for m in range(KD):
                    n = KD * g + m
                    pool.wait_ge(s_rl, n + 1 + KD)
                    pool.wait_ge(s_c, n + 1)
                    nc.gpsimd.tensor_tensor(delta[:, m, :], delta[:, m, :], u1[:, m % 2, :],
                                            ALU.subtract).then_inc(s_rc, 1)
                pool.wait_ge(s_ln, g + 1)
                pool.wait_ge(st_du, 16 * g + 16)
                for m in range(KD):
                    n = KD * g + m
                    pool.wait_ge(s_rc, n + 3)
                    nc.gpsimd.tensor_tensor(delta[:, m, :], delta[:, m, :], e[:, m, :], ALU.add).then_inc(s_dl, 1)
                    pool.wait_ge(s_dl, n + 1 + KD)
                    nc.gpsimd.tensor_tensor(du[:, m, :], u[:, m, :], delta[:, m, :], ALU.mult).then_inc(s_du, 1)

            pool.sem_inc(s_rc, 2)
            pool.sem_inc(s_dl, KD)
            pool.sem_inc(s_du, KD)
            batches(pool, lambda b, g: None, main)

        @block.scalar
        def _(act):
            def norm_v(b, g):
                act.wait_ge(s_x, 16 * g + 16)
                for k in range(KC):
                    c = b * KC + k
                    last = nc.scalar.activation(v[:, k, :], v[:, k, :], ACT.Identity,
                                                bias=keep.shift[:, c:c + 1], scale=keep.scale[:, c:c + 1])
                last.then_inc(s_v, 1)

            def square(g, chunks_done):
                act.wait_ge(s_vc, g + 1)
                act.wait_ge(s_var, g + 1)
                act.wait_ge(s_dl, KD * chunks_done + KD)
                nc.scalar.activation(sq, v[:], ACT.Square).then_inc(s_sq, 1)

            def root(g):
                act.wait_ge(s_var, g + 2)
                act.wait_ge(s_rs, g + 1)
                nc.scalar.activation(sd[:], st_ps[:], ACT.Sqrt, bias=keep.gn_eps[:, 0:1]).then_inc(s_sd, 1)

            def split(g):
                act.wait_ge(s_xn, g + 1)
                nc.scalar.activation(xn[0][:], v[:], ACT.Copy).then_inc(s_xh, 1)

            def prologue(b, g):
                norm_v(b, g)
                square(g, g)
                root(g)
                split(g)

            def silu_u(g, m):
                n = KD * g + m
                act.wait_ge(s_cv, n + 3)
                act.wait_ge(s_du, n + 1)
                if m == 0:
                    act.wait_ge(st_u, 16 * g + 16)
                nc.scalar.activation(u[:, m, :], acc[:, m % 2, :], ACT.Silu).then_inc(s_u, 1)

            def main(b, j, ahead):
                g = b * NJ + j
                act.wait_ge(st_z, 16 * g + 16)
                for m in range(KD):
                    q = 2 * m
                    act.wait_ge(s_mm, NQ * g + q + 1)
                    act.wait_ge(s_cv, KD * g + m + 1)
                    nc.scalar.activation(xr[:, m % 2, HIST:], mm[:, q % RING, :], ACT.Identity,
                                         bias=keep.b_in[:, m:m + 1]).then_inc(s_ev, 1)
                    if m:
                        silu_u(g, m - 1)
                    act.wait_ge(s_mm, NQ * g + q + 2)
                    nc.scalar.activation(z[:, m, :], mm[:, (q + 1) % RING, :], ACT.Silu,
                                         bias=keep.b_in[:, KD + m:KD + m + 1]).then_inc(s_ev, 1)
                    if m == 2 and ahead:
                        norm_v(b, g + 1)
                    if m == 5 and ahead:
                        square(g + 1, g)
                silu_u(g, KD - 1)
                if ahead:
                    root(g + 1)
                act.wait_ge(s_xd, g + 1)
                nc.scalar.activation(dt[0:RANK, :], xd_ps[0:RANK, :], ACT.Copy).then_inc(s_dt, 1)
                act.wait_ge(st_bc, 16 * g + 16)
                nc.scalar.activation(bc[RANK:64, :], xd_ps[RANK:64, :], ACT.Copy).then_inc(s_bc, 1)
                if ahead:
                    act.wait_ge(s_var, g + 3)
                for m in range(KD):
                    n = KD * g + m
                    q = 2 * KD + m
                    act.wait_ge(s_mm, NQ * g + q + 1)
                    act.wait_ge(s_dl, n + 1)
                    nc.scalar.activation(e[:, m, :], mm[:, q % RING, :], ACT.Abs).then_inc(s_ab, 1)
                    if m == 0:
                        act.wait_ge(st_dl, 16 * g + 16)
                    nc.scalar.activation(delta[:, m, :], mm[:, q % RING, :], ACT.Relu).then_inc(s_rl, 1)
                    act.wait_ge(s_ab, n + 1 + KD)
                    nc.scalar.activation(e[:, m, :], e[:, m, :], ACT.Exp, scale=-1.0).then_inc(s_e, 1)
                    if m == 2 and ahead:
                        split(g + 1)
                act.wait_ge(s_c, KD * g + KD)
                nc.scalar.activation(e[:], e[:], ACT.Ln, bias=1.0).then_inc(s_ln, 1)

            act.sem_inc(s_u, 2)
            act.sem_inc(s_ab, KD)
            act.sem_inc(s_rl, KD)
            act.sem_inc(s_dt, 1)
            act.sem_inc(s_bc, 1)
            batches(act, prologue, main)

        @block.tensor
        def _(pe):
            def mean(g):
                pe.wait_ge(s_v, g + 1)
                pe.wait_ge(s_rs, g + 1)
                for k in range(KC):
                    last = nc.tensor.matmul(st_ps[:], keep.mean_w[:], v[:, k, :], start=(k == 0), stop=(k == KC - 1))
                last.then_inc(s_mu, 1)

            def var(g):
                pe.wait_ge(s_sq, g + 1)
                for k in range(KC):
                    last = nc.tensor.matmul(st_ps[:], keep.mean_w[:], sq[:, k, :], start=(k == 0), stop=(k == KC - 1))
                last.then_inc(s_var, 1)

            def prologue(b, g):
                mean(g)
                var(g)

            def bank_free(g, q):
                if RING <= q < RING + 2 * KD:
                    pe.wait_ge(s_ev, 2 * KD * g + q - RING + 1)
                else:
                    past = KD * g + (q + KD - RING if q < RING else KD + q - 2 * KD - RING) + 1
                    pe.wait_ge(s_ab, past)
                    pe.wait_ge(s_rl, past)

            def main(b, j, ahead):
                g = b * NJ + j
                pe.wait_ge(s_xh, g + 1)
                pe.wait_ge(s_xl, g + 2)
                for q in range(2 * KD):
                    if q == 7 and ahead:
                        mean(g + 1)
                    if q == 13 and ahead:
                        var(g + 1)
                    bank_free(g, q)
                    col = (q // 2 + (q % 2) * KD) * P
                    for k in range(KC):
                        last = split_matmul(nc, mm[:, q % RING, :], [part[:, k, col:col + P] for part in keep.w_in],
                                            [part[:, k, :] for part in xn], k == 0, k == KC - 1)
                    last.then_inc(s_mm, 1)
                pe.wait_ge(s_dt, g + 1)
                pe.wait_ge(s_bc, g + 1)
                for m in range(KD):
                    pe.wait_ge(s_u, KD * g + m + 3)
                    last = nc.tensor.matmul(xd_ps[:], keep.w_xp[:, m, :], u[:, m, :], start=(m == 0), stop=(m == KD - 1))
                last.then_inc(s_xd, 1)
                pe.wait_ge(s_dt, g + 2)
                for m in range(KD):
                    q = 2 * KD + m
                    bank_free(g, q)
                    nc.tensor.matmul(mm[:, q % RING, :], keep.w_dt[:, m * P:(m + 1) * P], dt[:], start=True,
                                     stop=True).then_inc(s_mm, 1)

            pe.sem_inc(s_var, 1)
            pe.wait_ge(s_one, 1)
            batches(pe, prologue, main)

        @block.vector
        def _(dve):
            nc.vector.memset(dt[RANK:RANK + 1, :], 1.0).then_inc(s_one, 1)
            dve.sem_inc(s_rs, 1)
            dve.sem_inc(s_xl, 1)
            dve.sem_inc(s_cs, 1)
            dve.sem_inc(s_cv, 2)

            def over_blocks(t):
                return t[:].rearrange("p (k t) -> p k t", k=1).broadcast_to([P, KC, T])

            def centre(g):
                dve.wait_ge(s_mu, g + 1)
                nc.vector.tensor_tensor(v[:], v[:], over_blocks(st_ps), ALU.subtract).then_inc(s_vc, 1)

            def normalise(g):
                dve.wait_ge(s_sd, g + 1)
                nc.vector.reciprocal(rs[:], sd[:]).then_inc(s_rs, 1)
                dve.wait_ge(s_rs, g + 2)
                nc.vector.tensor_tensor(v[:], v[:], over_blocks(rs), ALU.mult).then_inc(s_xn, 1)

            def split(g):
                dve.wait_ge(s_xh, g + 1)
                nc.vector.tensor_tensor(xn[1][:], v[:], xn[0][:].bitcast(F32), ALU.subtract).then_inc(s_xl, 1)

            def prologue(b, g):
                nc.vector.memset(hist[:], 0.0).then_inc(s_zero, 1)
                centre(g)
                normalise(g)
                split(g)
                dve.wait_ge(s_zero, b + 1)

            def conv(g, m):
                n = KD * g + m
                base = 5 * n + 1
                slot = m % 2
                dve.wait_ge(s_ev, 2 * n + 1)
                dve.wait_ge(s_cs, 5 * KD * g + 1)
                nc.vector.tensor_copy(xr[:, slot, 0:HIST], hist[:, m, :]).then_inc(s_cs, 1)
                dve.wait_ge(s_cs, base + 1)
                dve.wait_ge(s_u, n + 1)
                nc.vector.tensor_scalar(acc[:, slot, :], xr[:, slot, 0:T], keep.conv_w[:, m, 0:1],
                                        keep.conv_b[:, m:m + 1], ALU.mult, ALU.add).then_inc(s_cs, 1)
                nc.vector.tensor_copy(hist[:, m, :], xr[:, slot, T:T + HIST]).then_inc(s_cs, 1)
                for i in range(1, TAPS):
                    dve.wait_ge(s_cs, base + 2 + (i if i > 1 else 0))
                    last = nc.vector.scalar_tensor_tensor(acc[:, slot, :], xr[:, slot, i:i + T], keep.conv_w[:, m, i:i + 1],
                                                          acc[:, slot, :], ALU.mult, ALU.add)
                    last.then_inc(s_cs if i < TAPS - 1 else s_cv, 1)

            def rounding_error(g, m):
                n = KD * g + m
                slot = m % 2
                dve.wait_ge(s_e, n + 1)
                dve.wait_ge(s_rc, n + 1)
                nc.vector.tensor_scalar(u1[:, slot, :], e[:, m, :], 1.0, None, ALU.add).then_inc(s_u1, 1)
                dve.wait_ge(s_u1, n + 1)
                nc.vector.scalar_tensor_tensor(u1[:, slot, :], u1[:, slot, :], 1.0, e[:, m, :], ALU.subtract,
                                               ALU.subtract).then_inc(s_c, 1)

            def main(b, j, ahead):
                g = b * NJ + j
                for m in range(KD):
                    conv(g, m)
                    if m == 3 and ahead:
                        centre(g + 1)
                if ahead:
                    normalise(g + 1)
                for m in range(KD):
                    rounding_error(g, m)
                    if m == 3 and ahead:
                        split(g + 1)

            batches(dve, prologue, main)


def scan(nc, keep, d):
    NQ = NS // 4
    NC = KD * NQ
    with ExitStack() as ctx:
        w = Place(nc, ctx, "sc")
        b_all = w.sb("b_all", [P, NS, T])
        c_all = w.sb("c_all", [P, NS, T])
        blk = w.sb("blk", [P, 4, 4, T])
        da = w.sb("da", [P, 2, 4, T])
        dbu = w.sb("dbu", [P, 2, 4, T])
        h = w.sb("h", [P, 2, 4, T])
        hc = w.sb("hc", [P, 2, 4, T])
        state = w.sb("state", [P, KD, NS])
        e0 = w.sb("e0", [P, 2, NS])
        carry = w.sb("carry", [P, 2, NS])
        yg = w.sb("yg", [P, 2, T])
        w_out = w.sb("w_out", [P, KD, DIM])
        skip = w.sb("skip", [P, KD, P])
        x_res = w.sb("x_res", [P, KC, T])
        y_ps = w.ps("y_ps", [P, 2, T])
        o_ps = w.ps("o_ps", [P, KC, T])

        s_w = w.sem("w_out_loaded")
        s_skip = w.sem("skip_made")
        s_b = [w.sem(f"b_loaded{q}") for q in range(NQ)]
        s_c = [w.sem(f"c_loaded{q}") for q in range(NQ)]
        s_blk = [w.sem(f"block_loaded{i}") for i in range(4)]
        s_x = w.sem("x_loaded")
        s_zero = w.sem("state_zeroed")
        s_gap = w.sem("decay_gap_zeroed")
        s_da = w.sem("da_done")
        s_dbu = w.sem("dbu_done")
        s_h = w.sem("h_done")
        s_st = w.sem("state_kept")
        s_e0 = w.sem("e0_done")
        s_car = w.sem("carry_done")
        s_first = w.sem("first_column_done")
        s_hc = w.sem("hc_done")
        s_acc = w.sem("hc_summed")
        s_y = w.sem("y_done")
        s_yg = w.sem("gated")
        s_op = w.sem("projected")
        s_res = w.sem("x1_done")
        s_add = w.sem("x1_summed")
        st_x1 = w.sem("x1_stored")
        block = ctx.enter_context(nc.Block())
        x_view = d.x.rearrange("b (k p) (j r) w -> b j p k (r w)", p=P, j=NJ)

        def chunks(eng, body, before=None):
            for b in range(NB):
                if before:
                    before(b)
                body(b, 0, b * NJ, (b - 1, NJ - 1) if b else None)
                with eng.Fori(1, NJ) as j:
                    body(b, j, b * NJ + j, (b, j - 1))

        @block.sync
        def _(sp):
            sp.sem_inc(st_x1, 16)
            sp.dma_start(w_out[:], d.w_out).then_inc(s_w, 16)

            def block_in(g, i):
                sp.wait_ge(s_yg, KD * g + i + 1)
                sp.dma_start(blk[:, i % 4], d.spill[g][:, i]).then_inc(s_blk[i % 4], 16)

            def rows_in(g, t, s_t, read, at, q):
                for s in read:
                    sp.wait_ge(s, NC * g + q + 1)
                src = d.bc[g][at + 4 * q:at + 4 * q + 4, :].rearrange("(a n) t -> a n t", a=1)
                sp.dma_start(t[:, 4 * q:4 * q + 4, :], src.broadcast_to([P, 4, T])).then_inc(s_t[q], 16)

            def first_loads(g):
                block_in(g, 0)
                block_in(g, 1)
                for q in range(NQ + 1):
                    if q < NQ:
                        rows_in(g, b_all, s_b, (s_dbu, s_first), 0, q)
                    if q > 0:
                        rows_in(g, c_all, s_c, (s_hc,), NS, q - 1)
                    if q == 1:
                        block_in(g, 2)

            def store(g):
                sp.wait_ge(s_res, KC * g + 2 * KC)
                sp.dma_start(d.x1[g], x_res[:]).then_inc(st_x1, 16)

            def body(b, j, before, more):
                g = b * NJ + j
                for i in range(3, KD):
                    block_in(g, i)
                    if i == 4 and before:
                        store(g - 1)
                    if i == 5:
                        sp.wait_ge(st_x1, 16 * g + 16)
                        sp.dma_start(x_res[:], x_view[b, j]).then_inc(s_x, 16)
                if more:
                    first_loads(g + 1)

            first_loads(0)
            for b in range(NB):
                body(b, 0, b > 0, True)
                with sp.Fori(1, NJ - 1) as j:
                    body(b, j, True, True)
                body(b, NJ - 1, True, b < NB - 1)
            store(NG - 1)
            sp.wait_ge(st_x1, 16 * NG + 16)


        @block.gpsimd
        def _(pool):
            pool.sem_inc(s_dbu, NQ)

            def body(b, j, g, past):
                for i in range(KD):
                    pool.wait_ge(s_blk[i % 4], 32 * g + 16 * (i // 4) + 16)
                    for q in range(NQ):
                        n = NC * g + NQ * i + q
                        if i == 0:
                            pool.wait_ge(s_b[q], 16 * g + 16)
                        pool.wait_ge(s_h, n + 1)
                        du = blk[:, i % 4, DU:DU + 1, 1:].broadcast_to([P, 4, T - 1])
                        nc.gpsimd.tensor_tensor(dbu[:, q % 2, :, 1:], b_all[:, 4 * q:4 * q + 4, 1:], du,
                                                ALU.mult).then_inc(s_dbu, 1)

            chunks(pool, body)

        @block.scalar
        def _(act):
            def keep_state(k):
                i, q = divmod(k, NQ)
                nc.scalar.activation(state[:, i, 4 * q:4 * q + 4], h[:, k % 2, :, T - 1], ACT.Copy).then_inc(s_st, 1)

            def first_decay(g, i):
                act.wait_ge(s_blk[i % 4], 32 * g + 16 * (i // 4) + 16)
                act.wait_ge(s_car, KD * g + i + 1)
                nc.scalar.activation(e0[:, i % 2, :], keep.neg_a[:, i * NS:(i + 1) * NS], ACT.Exp,
                                     scale=blk[:, i % 4, DELTA, 0:1]).then_inc(s_e0, 1)

            def body(b, j, g, past):
                first_decay(g, 0)
                for k in range(NC):
                    i, q = divmod(k, NQ)
                    act.wait_ge(s_h, NC * g + k + 1)
                    if k >= 2:
                        keep_state(k - 2)
                    elif past:
                        keep_state(NC - 2 + k)
                    for r in range(4):
                        c = i * NS + 4 * q + r
                        last = nc.scalar.activation(da[:, k % 2, r, 1:], blk[:, i % 4, DELTA, 1:], ACT.Exp,
                                                    scale=keep.neg_a[:, c:c + 1])
                    last.then_inc(s_da, 1)
                    if q == 0 and i < KD - 1:
                        first_decay(g, i + 1)

            act.sem_inc(s_st, 2)
            chunks(act, body)

        @block.tensor
        def _(pe):
            pe.sem_inc(s_acc, 2)
            pe.sem_inc(s_op, 2 * KC)
            pe.wait_ge(s_w, 16)
            pe.wait_ge(s_skip, KD)

            def project(g, i, m):
                if m == 0:
                    pe.wait_ge(s_yg, KD * g + i + 5)
                if i == 0:
                    pe.wait_ge(s_res, KC * g + m + 1)
                nc.tensor.matmul(o_ps[:, m, :], w_out[:, i, m * P:(m + 1) * P], yg[:, i % 2, :],
                                 start=(i == 0), stop=(i == KD - 1)).then_inc(s_op, 1)

            def body(b, j, g, past):
                for k in range(NC):
                    i, q = divmod(k, NQ)
                    n = KD * g + i
                    if q == 0:
                        pe.wait_ge(s_blk[i % 4], 32 * g + 16 * (i // 4) + 16)
                        pe.wait_ge(s_yg, n + 3)
                        nc.tensor.matmul(y_ps[:, i % 2, :], skip[:, i, :], blk[:, i % 4, U, :], start=True, stop=False)
                    pe.wait_ge(s_hc, NC * g + k + 1 + NQ)
                    for r in range(4):
                        last = nc.tensor.matmul(y_ps[:, i % 2, :], keep.ident[:], hc[:, q % 2, r, :],
                                                start=False, stop=(q == NQ - 1 and r == 3))
                    last.then_inc(s_acc, 1)
                    late, m = divmod(k - 7, KC)
                    if late >= 0:
                        project(g, late, m)
                    elif past:
                        project(g - 1, KD + late, m)

            chunks(pe, body)
            for k in range(NC, NC + 7):
                project(NG - 1, *divmod(k - 7, KC))

        @block.vector
        def _(dve):
            for i in range(KD):
                nc.vector.tensor_scalar(skip[:, i, :], keep.ident[:], keep.dskip[:, i:i + 1], None,
                                        ALU.mult).then_inc(s_skip, 1)
            dve.sem_inc(s_h, 2)
            dve.sem_inc(s_car, 2)
            dve.sem_inc(s_first, NQ)
            nc.vector.memset(da[:, :, :, 0], 0.0).then_inc(s_gap, 1)
            dve.wait_ge(s_gap, 1)
            dve.sem_inc(s_hc, NQ)
            dve.sem_inc(s_yg, 4)
            dve.sem_inc(s_res, KC)

            def before(b):
                dve.wait_ge(s_st, b * NJ * NC + 2)
                dve.wait_ge(s_car, KD * NJ * b + 2)
                nc.vector.memset(state[:], 0.0).then_inc(s_zero, 1)
                dve.wait_ge(s_zero, b + 1)

            def gate(g, i):
                n = KD * g + i
                dve.wait_ge(s_acc, NC * g + NQ * i + NQ + 2)
                dve.wait_ge(s_op, KC * n + KC)
                nc.vector.tensor_tensor(yg[:, i % 2, :], y_ps[:, i % 2, :], blk[:, i % 4, Z, :],
                                        ALU.mult).then_inc(s_yg, 1)

            def residual(g, b, j, m):
                dve.wait_ge(s_x, 16 * g + 16)
                dve.wait_ge(s_op, KC * (KD * g + KD - 1) + m + 1 + 2 * KC)
                nc.vector.tensor_tensor(x_res[:, m, :], x_res[:, m, :], o_ps[:, m, :], ALU.add).then_inc(s_add, 1)
                dve.wait_ge(s_add, KC * g + m + 1)
                nc.vector.bn_stats(keep.stats[:, b * KC + m, j, :], x_res[:, m, :]).then_inc(s_res, 1)

            def body(b, j, g, past):
                def carry_in(i):
                    dve.wait_ge(s_e0, KD * g + i + 1)
                    nc.vector.tensor_tensor(carry[:, i % 2, :], e0[:, i % 2, :], state[:, i, :], ALU.mult).then_inc(s_car, 1)

                def first_column(k):
                    i, q = divmod(k, NQ)
                    n = NC * g + k
                    dve.wait_ge(s_h, n + 1)
                    dve.wait_ge(s_car, KD * g + i + 3)
                    if i == 0:
                        dve.wait_ge(s_b[q], 16 * g + 16)
                    nc.vector.scalar_tensor_tensor(dbu[:, k % 2, :, 0], b_all[:, 4 * q:4 * q + 4, 0],
                                                   blk[:, i % 4, DU, 0:1], carry[:, i % 2, 4 * q:4 * q + 4],
                                                   ALU.mult, ALU.add).then_inc(s_first, 1)

                def recur(k):
                    n = NC * g + k
                    dve.wait_ge(s_first, n + 1 + NQ)
                    dve.wait_ge(s_da, n + 1)
                    dve.wait_ge(s_dbu, n + 1 + NQ)
                    dve.wait_ge(s_st, n + 1)
                    dve.wait_ge(s_hc, n - 1 + NQ)
                    flat = [t[:, k % 2].rearrange("p r t -> p (r t)") for t in (h, da, dbu)]
                    nc.vector.tensor_tensor_scan(*flat, 0.0, ALU.mult, ALU.add).then_inc(s_h, 1)

                def weigh(k):
                    i, q = divmod(k, NQ)
                    n = NC * g + k
                    dve.wait_ge(s_h, n + 3)
                    if i == 0:
                        dve.wait_ge(s_c[q], 16 * g + 16)
                    dve.wait_ge(s_acc, n + 1)
                    nc.vector.tensor_tensor(hc[:, k % 2], h[:, k % 2], c_all[:, 4 * q:4 * q + 4, :],
                                            ALU.mult).then_inc(s_hc, 1)

                carry_in(0)
                first_column(0)
                for k in range(NC):
                    recur(k)
                    if k % NQ == 2 and k < NC - NQ:
                        carry_in(k // NQ + 1)
                    if k < NC - 1:
                        first_column(k + 1)
                    if k:
                        weigh(k - 1)
                    if k == 2 and past:
                        gate(g - 1, KD - 1)
                    if 5 <= k < 5 + KC and past:
                        residual(g - 1, *past, k - 5)
                    if k % NQ == 2 and k > NQ:
                        gate(g, k // NQ - 1)
                weigh(NC - 1)

            chunks(dve, body, before)
            gate(NG - 1, KD - 1)
            for m in range(KC):
                residual(NG - 1, NB - 1, NJ - 1, m)
            dve.wait_ge(s_res, KC * NG + KC)


def memory_setup(nc, keep, d):
    with ExitStack() as ctx:
        w = Place(nc, ctx, "ms")
        mn = w.sb("mn", [P, KK, DIM])
        sq = w.sb("sq", [P, DIM])
        norm = w.sb("norm", [P, KK])
        tr = w.ps("tr", [P, 2, T])
        loads = w.sem("loads")
        s_sq = w.sem("squares")
        s_root = w.sem("root")
        step = w.sem("step")
        s_mn = w.sem("scaled")
        s_tr = w.sem("transposed")
        s_hi = w.sem("high")
        s_lo = w.sem("low")
        block = ctx.enter_context(nc.Block())
        HALVES = [(c, f) for c in range(KC) for f in range(KM // T)]
        PER = T // P

        @block.sync
        def _(sp):
            sp.dma_start(keep.m[:], d.m.rearrange("(k p) c -> p k c", p=P)).then_inc(loads, 16)
            sp.dma_start(keep.iota[:], d.iota.broadcast_to([P, KM])).then_inc(loads, 16)

        @block.scalar
        def _(act):
            act.wait_ge(loads, 32)
            for k in range(KK):
                if k:
                    act.wait_ge(s_sq, k)
                nc.scalar.activation(sq[:], keep.m[:, k, :], ACT.Square, accum_out=norm[:, k:k + 1]).then_inc(s_sq, 1)
            act.wait_ge(s_sq, KK)
            nc.scalar.activation(norm[:], norm[:], ACT.Sqrt).then_inc(s_root, 1)
            for n, (c, f) in enumerate(HALVES):
                act.wait_ge(s_tr, n + 1)
                nc.scalar.activation(keep.mt[0][:, c, f * T:(f + 1) * T], tr[:, n % 2, :], ACT.Copy).then_inc(s_hi, 1)

        @block.tensor
        def _(pe):
            pe.sem_inc(s_lo, 2)
            pe.wait_ge(s_mn, KK)
            for n, (c, f) in enumerate(HALVES):
                pe.wait_ge(s_lo, n + 1)
                for i in range(PER):
                    last = nc.tensor.transpose(tr[:, n % 2, i * P:(i + 1) * P], mn[:, f * PER + i, c * P:(c + 1) * P],
                                               keep.ident[:])
                last.then_inc(s_tr, 1)

        @block.vector
        def _(dve):
            dve.wait_ge(s_root, 1)
            nc.vector.tensor_scalar(norm[:], norm[:], NORM_EPS, None, ALU.max).then_inc(step, 1)
            dve.wait_ge(step, 1)
            nc.vector.reciprocal(norm[:], norm[:]).then_inc(step, 1)
            dve.wait_ge(step, 2)
            for k in range(KK):
                nc.vector.tensor_scalar(mn[:, k, :], keep.m[:, k, :], norm[:, k:k + 1], None, ALU.mult).then_inc(s_mn, 1)
            for n, (c, f) in enumerate(HALVES):
                cols = slice(f * T, (f + 1) * T)
                dve.wait_ge(s_hi, n + 1)
                nc.vector.tensor_tensor(keep.mt[1][:, c, cols], tr[:, n % 2, :], keep.mt[0][:, c, cols].bitcast(F32),
                                        ALU.subtract).then_inc(s_lo, 1)
            dve.wait_ge(s_lo, len(HALVES) + 2)


def assign(nc, keep, d):
    TT = T // P
    with ExitStack() as ctx:
        w = Place(nc, ctx, "as")
        x1 = w.sb("x1", [P, KC, T])
        v = w.sb("v", [P, KC, T])
        vp = [w.sb("v_hi", [P, KC, T], F32R), w.sb("v_lo", [P, KC, T], F32R)]
        xt = [w.sb("xt_hi", [P, TT, DIM], F32R), w.sb("xt_lo", [P, TT, DIM], F32R)]
        sq = w.sb("sq", [P, DIM])
        ss = w.sb("ss", [P, TT])
        nrm = w.sb("nrm", [P, TT])
        rn = w.sb("rn", [P, TT])
        top = w.sb("top", [P, TT, 8])
        nb = w.sb("nb", [P, TT])
        idx = w.sb("idx", [P, TT, 8], U32)
        idxf = w.sb("idxf", [P, TT])
        oh = w.sb("oh", [P, TT, KM], F32R)
        e = w.sb("e", [P, 2, KM])
        es = w.sb("es", [P, TT])
        er = w.sb("er", [P, TT])
        et = w.sb("et", [P, KK, T])
        sc_ps = w.ps("sc_ps", [P, 2, KM])
        tr_ps = w.ps("tr_ps", [P, 2, T])
        sum_ps = w.ps("sum_ps", [P, 2, T])

        s_x = w.sem("x1_loaded")
        s_v = w.sem("v_done")
        s_vh = w.sem("v_hi_done")
        s_vl = w.sem("v_lo_done")
        s_tr = w.sem("transposed")
        s_xh = w.sem("xt_hi_done")
        s_ss = w.sem("squares")
        s_xl = w.sem("xt_lo_done")
        s_nr = w.sem("norm_done")
        s_cl = w.sem("norm_clamped")
        s_rn = w.sem("rn_done")
        s_sc = w.sem("scored")
        s_top = w.sem("top_done")
        s_nb = w.sem("bias_done")
        s_ix = w.sem("index_done")
        s_if = w.sem("index_float")
        s_oh = w.sem("onehot_done")
        s_ex = w.sem("exp_done")
        s_er = w.sem("exp_sum_inverted")
        s_en = w.sem("softmax_done")
        s_et = w.sem("softmax_turned")
        s_sp = w.sem("sums_done")
        s_ad = w.sem("sums_added")
        s_ct = w.sem("counted")
        s_zc = w.sem("count_zeroed")
        s_zs = w.sem("sums_zeroed")
        st_e = w.sem("softmax_stored")
        block = ctx.enter_context(nc.Block())
        NTR = 3 * TT

        def batches(eng, prologue, main, peeled=1):
            for b in range(NB):
                prologue(b, b * NJ)
                with eng.Fori(0, NJ - peeled) as j:
                    main(b, b * NJ + j, peeled)
                for j in range(NJ - peeled, NJ):
                    main(b, b * NJ + j, NJ - 1 - j)

        @block.sync
        def _(sp):
            def load(g):
                sp.dma_start(x1[:], d.x1[g]).then_inc(s_x, 16)

            def prologue(b, g):
                load(g)
                sp.wait_ge(s_v, g + 1)
                load(g + 1)

            def main(b, g, ahead):
                if ahead >= 1:
                    sp.wait_ge(s_v, g + 2)
                if ahead >= 2:
                    load(g + 2)
                sp.wait_ge(s_et, 2 * TT * g + 2 * TT + 1)
                sp.dma_start(d.soft[g], et[:]).then_inc(st_e, 16)

            sp.sem_inc(st_e, 16)
            batches(sp, prologue, main, 2)
            sp.wait_ge(st_e, 16 * NG + 16)

        @block.gpsimd
        def _(pool):
            nc.gpsimd.memset(keep.count[:], 0.0).then_inc(s_zc, 1)
            pool.wait_ge(s_zc, 1)

            def main(b, g, ahead):
                for s in range(TT):
                    n = TT * g + s
                    pool.wait_ge(s_oh, n + 3)
                    pool.wait_ge(s_ct, n + 1)
                    nc.gpsimd.tensor_tensor(keep.count[:], keep.count[:], oh[:, s, :].bitcast(F32),
                                            ALU.add).then_inc(s_ct, 1)

            pool.sem_inc(s_ct, 1)
            batches(pool, lambda b, g: None, main)
            pool.wait_ge(s_ct, TT * NG + 1)

        @block.scalar
        def _(act):
            def norm_v(b, g):
                act.wait_ge(s_x, 16 * g + 16)
                act.wait_ge(s_vl, g + 1)
                act.wait_ge(s_tr, NTR * g + 1)
                for k in range(KC):
                    c = b * KC + k
                    last = nc.scalar.activation(v[:, k, :], x1[:, k, :], ACT.Identity,
                                                bias=keep.shift[:, c:c + 1], scale=keep.scale[:, c:c + 1])
                last.then_inc(s_v, 1)

            def split(g):
                act.wait_ge(s_v, g + 1)
                act.wait_ge(s_sc, TT * g + 1)
                nc.scalar.activation(vp[0][:], v[:], ACT.Copy).then_inc(s_vh, 1)

            def norm_ahead(b, g):
                act.wait_ge(s_x, 16 * g + 16)
                act.wait_ge(s_vl, g + 1)
                act.wait_ge(s_tr, NTR * (g - 1) + TT + 1)
                for k in range(KC):
                    c = b * KC + k
                    last = nc.scalar.activation(v[:, k, :], x1[:, k, :], ACT.Identity,
                                                bias=keep.shift[:, c:c + 1], scale=keep.scale[:, c:c + 1])
                last.then_inc(s_v, 1)

            def exp(g, s):
                act.wait_ge(s_nb, TT * g + s + 1)
                act.wait_ge(s_ix, TT * g + s + 1)
                act.wait_ge(s_tr, NTR * g + 1 + (TT + 2 * (s - 2) + 2 if s >= 2 else 0))
                nc.scalar.activation(e[:, s % 2, :], sc_ps[:, s % 2, :], ACT.Exp, bias=nb[:, s:s + 1],
                                     scale=rn[:, s:s + 1], accum_out=es[:, s:s + 1]).then_inc(s_ex, 1)

            def turned(g, s):
                if s == 0:
                    act.wait_ge(st_e, 16 * g + 16)
                for f in range(2):
                    r = TT + 2 * s + f
                    act.wait_ge(s_tr, NTR * g + r + 2)
                    nc.scalar.activation(et[:, 4 * f:4 * f + 4, s * P:(s + 1) * P],
                                         tr_ps[:, r % 2, :].rearrange("p (k t) -> p k t", t=P), ACT.Copy).then_inc(s_et, 1)

            def main(b, g, ahead):
                for s in range(TT):
                    act.wait_ge(s_tr, NTR * g + s + 2)
                    if s == 0:
                        act.wait_ge(s_sp, KK * g + 1)
                    nc.scalar.activation(xt[0][:, s, :], tr_ps[:, s % 2, :], ACT.Copy).then_inc(s_xh, 1)
                    act.wait_ge(s_ss, TT * g + s + 1)
                    nc.scalar.activation(sq[:], tr_ps[:, s % 2, :], ACT.Square, accum_out=ss[:, s:s + 1]).then_inc(s_ss, 1)
                act.wait_ge(s_ss, TT * g + TT + 1)
                act.wait_ge(s_cl, g + 1)
                nc.scalar.activation(nrm[:], ss[:], ACT.Sqrt).then_inc(s_nr, 1)
                for s in range(TT):
                    exp(g, s)
                    if s >= 2:
                        turned(g, s - 2)
                if ahead:
                    norm_ahead(b, g + 1)
                    split(g + 1)
                turned(g, TT - 2)
                turned(g, TT - 1)

            def prologue(b, g):
                norm_v(b, g)
                split(g)

            act.sem_inc(s_ex, 2)
            act.sem_inc(s_ss, 1)
            act.sem_inc(s_et, 1)
            batches(act, prologue, main)

        @block.tensor
        def _(pe):
            def turn_exp(g, s):
                pe.wait_ge(s_en, TT * g + s + 1)
                for f in range(2):
                    r = TT + 2 * s + f
                    if r - 2 < TT:
                        pe.wait_ge(s_xl, TT * g + r - 1)
                    else:
                        pe.wait_ge(s_et, 2 * TT * g + r - TT)
                    for i in range(4):
                        k = 4 * f + i
                        last = nc.tensor.transpose(tr_ps[:, r % 2, i * P:(i + 1) * P], e[:, s % 2, k * P:(k + 1) * P],
                                                   keep.ident[:])
                    last.then_inc(s_tr, 1)

            def main(b, g, ahead):
                pe.wait_ge(s_v, g + 1)
                pe.wait_ge(s_et, 2 * TT * g + 1)
                for s in range(TT):
                    if s >= 2:
                        pe.wait_ge(s_xl, TT * g + s - 1)
                    for k in range(KC):
                        last = nc.tensor.transpose(tr_ps[:, s % 2, k * P:(k + 1) * P], v[:, k, s * P:(s + 1) * P],
                                                   keep.ident[:])
                    last.then_inc(s_tr, 1)
                pe.wait_ge(s_vh, g + 1)
                pe.wait_ge(s_vl, g + 2)
                for s in range(TT):
                    n = TT * g + s
                    pe.wait_ge(s_ex, n + 1)
                    pe.wait_ge(s_oh, n + 1)
                    for f in range(KM // T):
                        cols = slice(f * T, (f + 1) * T)
                        for k in range(KC):
                            last = split_matmul(nc, sc_ps[:, s % 2, cols], [t[:, k, s * P:(s + 1) * P] for t in vp],
                                                [t[:, k, cols] for t in keep.mt], k == 0, k == KC - 1)
                    last.then_inc(s_sc, 1)
                    if s >= 2:
                        turn_exp(g, s - 2)
                pe.wait_ge(s_oh, TT * g + TT + 2)
                pe.wait_ge(s_xl, TT * g + TT)
                for k in range(KK):
                    pe.wait_ge(s_ad, KK * g + k + 1)
                    for s in range(TT):
                        nc.tensor.matmul(sum_ps[:, k % 2, :], oh[:, s, k * P:(k + 1) * P], xt[0][:, s, :],
                                         start=(s == 0), stop=False)
                        last = nc.tensor.matmul(sum_ps[:, k % 2, :], oh[:, s, k * P:(k + 1) * P], xt[1][:, s, :],
                                                start=False, stop=(s == TT - 1))
                    last.then_inc(s_sp, 1)
                    if k in (1, 3):
                        turn_exp(g, TT - 2 + k // 2)

            pe.sem_inc(s_tr, 1)
            pe.sem_inc(s_sc, 1)
            pe.sem_inc(s_sp, 1)
            batches(pe, lambda b, g: None, main)

        @block.vector
        def _(dve):
            nc.vector.memset(keep.sums[:], 0.0).then_inc(s_zs, 1)
            dve.wait_ge(s_zs, 1)
            dve.sem_inc(s_oh, 2)
            dve.sem_inc(s_ad, 2)
            dve.sem_inc(s_vl, 1)
            dve.sem_inc(s_cl, 1)

            def split(g):
                dve.wait_ge(s_vh, g + 1)
                nc.vector.tensor_tensor(vp[1][:], v[:], vp[0][:].bitcast(F32), ALU.subtract).then_inc(s_vl, 1)

            def nearest(g, s):
                n = TT * g + s
                dve.wait_ge(s_sc, n + 2)
                nc.vector.memset(nb[:, s:s + 1], 0.0)
                nc.vector.max(top[:, s, :], sc_ps[:, s % 2, :]).then_inc(s_top, 1)
                dve.wait_ge(s_top, n + 1)
                nc.vector.tensor_scalar(nb[:, s:s + 1], top[:, s, 0:1], rn[:, s:s + 1], -1.0, ALU.mult,
                                        ALU.mult).then_inc(s_nb, 1)
                nc.vector.max_index(idx[:, s, :], top[:, s, :], sc_ps[:, s % 2, :]).then_inc(s_ix, 1)
                dve.wait_ge(s_ix, n + 1)
                nc.vector.tensor_copy(idxf[:, s:s + 1], idx[:, s, 0:1]).then_inc(s_if, 1)
                dve.wait_ge(s_if, n + 1)
                if s == 0:
                    dve.wait_ge(s_ct, TT * g + 1)
                    dve.wait_ge(s_sp, KK * g + 1)
                nc.vector.tensor_scalar(oh[:, s, :], keep.iota[:], idxf[:, s:s + 1], None, ALU.is_equal).then_inc(s_oh, 1)

            def softmax(g, s):
                n = TT * g + s
                dve.wait_ge(s_ex, n + 3)
                nc.vector.reciprocal(er[:, s:s + 1], es[:, s:s + 1]).then_inc(s_er, 1)
                dve.wait_ge(s_er, n + 1)
                nc.vector.tensor_scalar(e[:, s % 2, :], e[:, s % 2, :], er[:, s:s + 1], None, ALU.mult).then_inc(s_en, 1)

            def main(b, g, ahead):
                for s in range(TT):
                    dve.wait_ge(s_xh, TT * g + s + 1)
                    dve.wait_ge(s_ss, TT * g + s + 2)
                    nc.vector.tensor_tensor(xt[1][:, s, :], tr_ps[:, s % 2, :], xt[0][:, s, :].bitcast(F32),
                                            ALU.subtract).then_inc(s_xl, 1)
                dve.wait_ge(s_nr, g + 1)
                nc.vector.tensor_scalar(rn[:], nrm[:], NORM_EPS, None, ALU.max).then_inc(s_cl, 1)
                dve.wait_ge(s_cl, g + 2)
                nc.vector.reciprocal(rn[:], rn[:]).then_inc(s_rn, 1)
                dve.wait_ge(s_rn, g + 1)
                for s in range(TT):
                    if s:
                        softmax(g, s - 1)
                    nearest(g, s)
                softmax(g, TT - 1)
                for k in range(KK):
                    n = KK * g + k
                    dve.wait_ge(s_sp, n + 2)
                    nc.vector.tensor_tensor(keep.sums[:, k, :], keep.sums[:, k, :], sum_ps[:, k % 2, :],
                                            ALU.add).then_inc(s_ad, 1)
                    if k == 2 and ahead:
                        split(g + 1)

            batches(dve, lambda b, g: split(g), main)
            dve.wait_ge(s_ad, KK * NG + 2)


def readout(nc, keep, d):
    with ExitStack() as ctx:
        w = Place(nc, ctx, "ro")
        nm = [w.sb("nm_hi", [P, KK, DIM], F32R), w.sb("nm_lo", [P, KK, DIM], F32R)]
        share = w.sb("share", [P, KK])
        ones = w.sb("ones", [P, 1])
        et = w.sb("et", [P, 2, KK, T])
        ep = [w.sb("e_hi", [P, 2, KK, T], F32R), w.sb("e_lo", [P, 2, KK, T], F32R)]
        x1 = w.sb("x1", [P, 2, KC, T])
        o_ps = w.ps("o_ps", [P, 2, KC, T])

        s_step = w.sem("step")
        s_one = w.sem("ones_set")
        s_cnt = w.sem("counts_done")
        s_nm = w.sem("new_m_done")
        s_nh = w.sem("new_m_hi")
        s_nl = w.sem("new_m_lo")
        s_e = [w.sem(f"softmax_loaded{i}") for i in range(2)]
        s_x = [w.sem(f"x1_loaded{i}") for i in range(2)]
        s_eh = w.sem("e_hi_done")
        s_el = w.sem("e_lo_done")
        s_o = w.sem("out_summed")
        s_r = w.sem("residual_added")
        s_st = [w.sem(f"out_stored{i}") for i in range(2)]
        block = ctx.enter_context(nc.Block())
        out_view = d.out.rearrange("b (k p) (j r) w -> b j p k (r w)", p=P, j=NJ)

        def chunks(eng, body):
            with eng.Fori(0, NG // 2) as i:
                for u in range(2):
                    body(2 * i + u, u, i)

        @block.gpsimd
        def _(pool):
            def body(g, u, i):
                pool.wait_ge(s_el, g + 1)
                pool.dma_start(et[:, u], d.soft[g]).then_inc(s_e[u], 16)
                pool.wait_ge(s_st[u], 16 * i + 16)
                pool.dma_start(x1[:, u], d.x1[g]).then_inc(s_x[u], 16)

            chunks(pool, body)

        @block.sync
        def _(sp):
            for u in range(2):
                sp.sem_inc(s_st[u], 16)
            for b in range(NB):
                with sp.Fori(0, NJ // 2) as i:
                    for u in range(2):
                        j = 2 * i + u
                        sp.wait_ge(s_r, KC * (b * NJ + j) + 3 * KC)
                        sp.dma_start(out_view[b, j], x1[:, u]).then_inc(s_st[u], 16)
            for u in range(2):
                sp.wait_ge(s_st[u], 16 * NG // 2 + 16)

        @block.scalar
        def _(act):
            act.wait_ge(s_nm, KK)
            nc.scalar.activation(nm[0][:], keep.m[:], ACT.Copy).then_inc(s_nh, 1)

            def body(g, u, i):
                act.wait_ge(s_e[u], 16 * i + 16)
                act.wait_ge(s_o, KC * g + KC)
                nc.scalar.activation(ep[0][:, u], et[:, u], ACT.Copy).then_inc(s_eh, 1)

            chunks(act, body)

        @block.tensor
        def _(pe):
            pe.sem_inc(s_o, 2 * KC)
            pe.wait_ge(s_one, 1)
            for k in range(KK):
                last = nc.tensor.matmul(o_ps[:, 0, 0, k:k + 1], keep.count[:, k * P:(k + 1) * P], ones[:],
                                        start=True, stop=True)
            last.then_inc(s_cnt, 1)
            pe.wait_ge(s_nl, 1)

            def body(g, u, i):
                pe.wait_ge(s_eh, g + 1)
                pe.wait_ge(s_el, g + 3)
                for m in range(KC):
                    pe.wait_ge(s_r, KC * g + m + 1)
                    for k in range(KK):
                        last = split_matmul(nc, o_ps[:, u, m, :], [t[:, k, m * P:(m + 1) * P] for t in nm],
                                            [t[:, u, k, :] for t in ep], k == 0, k == KK - 1)
                    last.then_inc(s_o, 1)

            chunks(pe, body)

        @block.vector
        def _(dve):
            dve.sem_inc(s_r, 2 * KC)
            dve.sem_inc(s_el, 2)
            nc.vector.memset(ones[:], 1.0).then_inc(s_one, 1)
            nc.vector.tensor_scalar(keep.m[:], keep.m[:], RATE, None, ALU.mult).then_inc(s_step, 1)
            dve.wait_ge(s_cnt, 1)
            nc.vector.tensor_scalar(share[:], o_ps[:, 0, 0, 0:KK], MEAN_EPS, None, ALU.add).then_inc(s_step, 1)
            dve.wait_ge(s_step, 2)
            nc.vector.reciprocal(share[:], share[:]).then_inc(s_step, 1)
            dve.wait_ge(s_step, 3)
            nc.vector.tensor_scalar(share[:], share[:], 1.0 - RATE, None, ALU.mult).then_inc(s_step, 1)
            dve.wait_ge(s_step, 4)
            for k in range(KK):
                nc.vector.scalar_tensor_tensor(keep.m[:, k, :], keep.sums[:, k, :], share[:, k:k + 1], keep.m[:, k, :],
                                               ALU.mult, ALU.add).then_inc(s_nm, 1)
            dve.wait_ge(s_nh, 1)
            nc.vector.tensor_tensor(nm[1][:], keep.m[:], nm[0][:].bitcast(F32), ALU.subtract).then_inc(s_nl, 1)

            def split(g, u):
                dve.wait_ge(s_eh, g + 1)
                nc.vector.tensor_tensor(ep[1][:, u], et[:, u], ep[0][:, u].bitcast(F32), ALU.subtract).then_inc(s_el, 1)

            def residual(g, u, i):
                dve.wait_ge(s_x[u], 16 * i + 16)
                for m in range(KC):
                    dve.wait_ge(s_o, KC * g + m + 1 + 2 * KC)
                    nc.vector.tensor_tensor(x1[:, u, m, :], x1[:, u, m, :], o_ps[:, u, m, :], ALU.add).then_inc(s_r, 1)

            split(0, 0)
            with dve.Fori(0, NG // 2 - 1) as i:
                for u in range(2):
                    split(2 * i + u + 1, 1 - u)
                    residual(2 * i + u, u, i)
            split(NG - 1, 1)
            residual(NG - 2, 0, NG // 2 - 1)
            residual(NG - 1, 1, NG // 2 - 1)


class Names:
    pass


def program(nc, d):
    d.spill = nc.dram_tensor("spill", (NG, P, KD, 4, T), F32).ap()
    d.bc = nc.dram_tensor("bc", (NG, 2 * NS, T), F32).ap()
    d.x1 = nc.dram_tensor("x1", (NG, P, KC, T), F32).ap()
    d.soft = nc.dram_tensor("soft", (NG, P, KK, T), F32).ap()
    keep = Names()
    with ExitStack() as all_phases:
        w = Place(nc, all_phases, "keep")
        keep.ident = w.sb("ident", [P, P])
        keep.gavg = w.sb("gavg", [P, P])
        keep.gn_eps = w.sb("gn_eps", [P, 1])
        keep.stats = w.sb("stats", [P, NB * KC, NJ, 6])
        keep.scale = w.sb("scale", [P, NB * KC])
        keep.shift = w.sb("shift", [P, NB * KC])
        with ExitStack() as mamba:
            w = Place(nc, mamba, "l0")
            keep.neg_a = w.sb("neg_a", [P, KD * NS])
            keep.dskip = w.sb("dskip", [P, KD])
            with ExitStack() as first:
                w = Place(nc, first, "l0f")
                keep.w_in = [w.sb("w_in_hi", [P, KC, 2 * DI], F32R), w.sb("w_in_lo", [P, KC, 2 * DI], F32R)]
                keep.b_in = w.sb("b_in", [P, 2 * KD])
                keep.mean_w = w.sb("mean_w", [P, P])
                keep.conv_w = w.sb("conv_w", [P, KD, TAPS])
                keep.conv_b = w.sb("conv_b", [P, KD])
                keep.w_xp = w.sb("w_xp", [P, KD, 64])
                keep.w_dt = w.sb("w_dt", [RANK + 1, DI])
                setup(nc, keep, d)
                group_params(nc, "g1", keep, keep.stats, keep.scale, keep.shift)
                front(nc, keep, d)
            scan(nc, keep, d)
        group_params(nc, "g2", keep, keep.stats, keep.scale, keep.shift)
        with ExitStack() as memory:
            w = Place(nc, memory, "l1")
            keep.m = w.sb("m", [P, KK, DIM])
            keep.sums = w.sb("sums", [P, KK, DIM])
            keep.count = w.sb("count", [P, KM])
            with ExitStack() as scores:
                w = Place(nc, scores, "l1s")
                keep.mt = [w.sb("mt_hi", [P, KC, KM], F32R), w.sb("mt_lo", [P, KC, KM], F32R)]
                keep.iota = w.sb("iota", [P, KM])
                memory_setup(nc, keep, d)
                assign(nc, keep, d)
            readout(nc, keep, d)


def kernel(**inputs):
    import numpy as np
    from concourse import bacc
    from concourse.bass_utils import run_bass_kernel_spmd

    a = {k.replace("L0_conv_", "").replace("L1_conv_", ""): np.asarray(v) for k, v in inputs.items()}
    rows = lambda t: t.reshape(-1, P, *t.shape[1:]).swapaxes(0, 1)
    channel = np.arange(P)
    arrays = {
        "x": a["x"],
        "m": a["m"],
        "w_in": rows(a["in_proj_w"].T),
        "w_out": rows(a["out_proj_w"].T),
        "w_xp": rows(a["x_proj_w"].T),
        "w_dt": a["dt_proj_w"].T,
        "b_dt": a["dt_proj_b"][None, :],
        "ln_w": rows(a["ln_w"]),
        "ln_b": rows(a["ln_b"]),
        "conv_w": rows(a["conv_w"]),
        "conv_b": rows(a["conv_b"]),
        "d_skip": rows(a["D_skip"]),
        "a_log": rows(a["A_log"]).reshape(P, -1),
        "ident": np.eye(P, dtype=np.float32),
        "gavg": ((channel[:, None] // 16 == channel[None, :] // 16) / np.float32(16)).astype(np.float32),
        "iota": np.arange(KM, dtype=np.float32)[None, :],
    }
    nc = bacc.Bacc("TRN2", target_bir_lowering=False, num_devices=1)
    d = Names()
    sent = {}
    for name, value in arrays.items():
        value = np.ascontiguousarray(value)
        sent[f"in_{name}"] = value
        d.__dict__[name] = nc.dram_tensor(f"in_{name}", value.shape, mybir.dt.from_np(value.dtype), kind="ExternalInput").ap()
    d.out = nc.dram_tensor("out", (NB, DIM, 64, 64), F32, kind="ExternalOutput").ap()
    program(nc, d)
    r = run_bass_kernel_spmd(nc, [sent], core_ids=[0])
    return r.results[0]["out"]
```

```python
from contextlib import ExitStack

import concourse.bass as bass
from concourse import mybir

F32 = mybir.dt.float32
F32R = mybir.dt.float32r
U32 = mybir.dt.uint32
ALU = mybir.AluOpType
ACT = mybir.ActivationFunctionType
AXX = mybir.AxisListType.X

P = 128
NB = 2
L = 64 * 64
T = 512
NJ = L // T
NG = NB * NJ
DIM = 512
KC = DIM // P
DI = 1024
KD = DI // P
NS = 16
RANK = 32
TAPS = 4
HIST = TAPS - 1
KM = 1024
KK = KM // P
GN_EPS = 1e-5
LN_EPS = 1e-5
NORM_EPS = 1e-12
MEAN_EPS = 1e-6
RATE = 0.999
DELTA, DU, U, Z = range(4)


class Place:

    def __init__(self, nc, ctx, tag):
        self.nc, self.ctx, self.tag = nc, ctx, tag

    def sb(self, name, shape, dt=F32):
        return self.ctx.enter_context(self.nc.sbuf_tensor(f"{self.tag}_{name}", shape, dt))

    def ps(self, name, shape, dt=F32):
        return self.ctx.enter_context(self.nc.psum_tensor(f"{self.tag}_{name}", shape, dt))

    def sem(self, name):
        return self.ctx.enter_context(self.nc.semaphore(f"{self.tag}_{name}"))


def split_matmul(nc, out, lhs, rhs, start, stop):
    nc.tensor.matmul(out, lhs[0], rhs[0], start=start, stop=False)
    nc.tensor.matmul(out, lhs[1], rhs[0], start=False, stop=False)
    return nc.tensor.matmul(out, lhs[0], rhs[1], start=False, stop=stop)


def group_params(nc, tag, keep, stats, scale, shift, early=()):
    n = NB * KC
    with ExitStack() as ctx:
        w = Place(nc, ctx, tag)
        mv = w.sb("mv", [P, n, 2])
        mean = w.sb("mean", [P, n])
        dev = w.sb("dev", [P, n])
        spread = w.sb("spread", [P, n])
        std = w.sb("std", [P, n])
        ps = w.ps("ps", [P, 2, T])
        step = w.sem("step")
        mean_ps = w.sem("mean_ps")
        var_ps = w.sem("var_ps")
        std_done = w.sem("std_done")
        block = ctx.enter_context(nc.Block())

        @block.sync
        def _(sp):
            for to, source, loaded in early:
                sp.dma_start(to[:], source).then_inc(loaded, 16)

        @block.vector
        def _(dve):
            for i in range(n):
                nc.vector.bn_aggr(mv[:, i, :], stats[:, i, :, :]).then_inc(step, 1)
            dve.wait_ge(step, n)
            nc.vector.tensor_copy(mean[:], mv[:, :, 0]).then_inc(step, 1)
            dve.wait_ge(mean_ps, 1)
            dve.wait_ge(step, n + 1)
            nc.vector.tensor_tensor(dev[:], mean[:], ps[:, 0, 0:n], ALU.subtract).then_inc(step, 1)
            dve.wait_ge(step, n + 2)
            nc.vector.tensor_tensor(dev[:], dev[:], dev[:], ALU.mult).then_inc(step, 1)
            dve.wait_ge(step, n + 3)
            nc.vector.tensor_tensor(spread[:], dev[:], mv[:, :, 1], ALU.add).then_inc(step, 1)
            dve.wait_ge(std_done, 1)
            nc.vector.reciprocal(scale[:], std[:]).then_inc(step, 1)
            dve.wait_ge(step, n + 5)
            nc.vector.scalar_tensor_tensor(shift[:], ps[:, 0, 0:n], -1.0, scale[:], ALU.mult, ALU.mult).then_inc(step, 1)
            dve.wait_ge(step, n + 6)

        @block.tensor
        def _(pe):
            pe.wait_ge(step, n + 1)
            nc.tensor.matmul(ps[:, 0, 0:n], keep.gavg[:], mean[:], start=True, stop=True).then_inc(mean_ps, 1)
            pe.wait_ge(step, n + 4)
            nc.tensor.matmul(ps[:, 1, 0:n], keep.gavg[:], spread[:], start=True, stop=True).then_inc(var_ps, 1)

        @block.scalar
        def _(act):
            act.wait_ge(var_ps, 1)
            nc.scalar.activation(std[:], ps[:, 1, 0:n], ACT.Sqrt, bias=keep.gn_eps[:, 0:1]).then_inc(std_done, 1)


def setup(nc, keep, d):
    with ExitStack() as ctx:
        w = Place(nc, ctx, "su")
        wf = w.sb("wf", [P, KC, 2 * DI])
        lnw = w.sb("lnw", [P, KC])
        lnb = w.sb("lnb", [P, KC])
        alog = w.sb("alog", [P, KD * NS])
        xt = w.sb("xt", [P, 4, L])
        bias_ps = w.ps("bias_ps", [P, T])
        consts = w.sem("consts")
        weights = w.sem("weights")
        x_tile = [w.sem(f"x_tile{i}") for i in range(4)]
        eps_set = w.sem("eps_set")
        stats_done = w.sem("stats_done")
        bias_done = w.sem("bias_done")
        exp_done = w.sem("exp_done")
        high = w.sem("high")
        rest = w.sem("rest")
        norm_w = w.sem("norm_weights")
        n_const = 9
        block = ctx.enter_context(nc.Block())
        x_rows = d.x.rearrange("b (k p) h w -> (b k) p (h w)", p=P)

        @block.sync
        def _(sp):
            sp.dma_start(wf[:], d.w_in).then_inc(weights, 16)
            with sp.Fori(0, NB * KC // 4) as i:
                for s in range(4):
                    sp.wait_ge(stats_done, 4 * i + s + 1)
                    sp.dma_start(xt[:, s, :], x_rows[4 * i + s]).then_inc(x_tile[s], 16)

        @block.gpsimd
        def _(pool):
            for dst, src in ((keep.ident, d.ident), (keep.gavg, d.gavg), (alog, d.a_log),
                             (keep.conv_w, d.conv_w), (keep.conv_b, d.conv_b), (keep.dskip, d.d_skip), (keep.w_xp, d.w_xp)):
                pool.dma_start(dst[:], src).then_inc(consts, 16)
            pool.dma_start(keep.w_dt[0:RANK, :], d.w_dt).then_inc(consts, 16)
            pool.dma_start(keep.w_dt[RANK:RANK + 1, :], d.b_dt).then_inc(consts, 16)

        @block.scalar
        def _(act):
            act.dma_start(lnw[:], d.ln_w).then_inc(norm_w, 16)
            act.dma_start(lnb[:], d.ln_b).then_inc(norm_w, 16)
            act.wait_ge(norm_w, 32)
            act.wait_ge(weights, 16)
            for k in range(KC):
                nc.scalar.activation(keep.w_in[0][:, k, :], wf[:, k, :], ACT.Copy, scale=lnw[:, k:k + 1]).then_inc(high, 1)
            act.wait_ge(consts, 16 * n_const)
            nc.scalar.activation(alog[:], alog[:], ACT.Exp).then_inc(exp_done, 1)

        @block.tensor
        def _(pe):
            pe.wait_ge(norm_w, 32)
            pe.wait_ge(weights, 16)
            for m in range(2 * KD):
                for k in range(KC):
                    last = nc.tensor.matmul(bias_ps[:, m:m + 1], wf[:, k, m * P:(m + 1) * P], lnb[:, k:k + 1],
                                            start=(k == 0), stop=(k == KC - 1))
            last.then_inc(bias_done, 1)

        @block.vector
        def _(dve):
            nc.vector.memset(keep.gn_eps[:], GN_EPS).then_inc(eps_set, 1)
            nc.vector.memset(keep.mean_w[:], 1.0 / DIM).then_inc(eps_set, 1)
            dve.sem_inc(stats_done, 4)
            dve.wait_ge(norm_w, 32)
            for k in range(KC):
                dve.wait_ge(high, k + 1)
                nc.vector.scalar_tensor_tensor(keep.w_in[1][:, k, :], wf[:, k, :], lnw[:, k:k + 1],
                                               keep.w_in[0][:, k, :].bitcast(F32), ALU.mult, ALU.subtract).then_inc(rest, 1)
            with dve.Fori(0, NB * KC // 4) as i:
                for s in range(4):
                    dve.wait_ge(x_tile[s], 16 * i + 16)
                    for j in range(NJ):
                        last = nc.vector.bn_stats(keep.stats[:, 4 * i + s, j, :], xt[:, s, j * T:(j + 1) * T])
                    last.then_inc(stats_done, 1)
            dve.wait_ge(bias_done, 1)
            nc.vector.tensor_copy(keep.b_in[:], bias_ps[:, 0:2 * KD]).then_inc(rest, 1)
            dve.wait_ge(exp_done, 1)
            nc.vector.tensor_scalar(keep.neg_a[:], alog[:], -1.0, None, ALU.mult).then_inc(rest, 1)
            dve.wait_ge(rest, KC + 2)
            dve.wait_ge(eps_set, 2)


def front(nc, keep, d):
    with ExitStack() as ctx:
        w = Place(nc, ctx, "fr")
        RING = 6
        v = keep.v
        sd = w.sb("sd", [P, T])
        rs = w.sb("rs", [P, T])
        xn = [w.sb("xn_hi", [P, KC, T], F32R), w.sb("xn_lo", [P, KC, T], F32R)]
        xr = w.sb("xr", [P, 2, HIST + T])
        hist = w.sb("hist", [P, KD, HIST])
        acc = w.sb("acc", [P, 2, T])
        u = w.sb("u", [P, KD, T])
        z = w.sb("z", [P, KD, T])
        delta = w.sb("delta", [P, KD, T])
        du = w.sb("du", [P, KD, T])
        e = w.sb("e", [P, KD, T])
        u1 = w.sb("u1", [P, 2, T])
        dt = w.sb("dt", [RANK + 1, T])
        warm = w.sb("warm", [P, 1])
        half = w.sb("half", [P, 2, T])
        bc = w.sb("bc", [64, T])
        mm = w.ps("mm", [P, RING, T])
        st_ps = w.ps("st_ps", [P, T])
        xd_ps = w.ps("xd_ps", [64, T])
        sq = e[:, 0:KC, :]

        s_x = keep.x_loaded
        s_v = w.sem("v_done")
        s_mu = w.sem("mu_done")
        s_vc = w.sem("centred")
        s_half = w.sem("half_summed")
        s_pre = w.sem("blocks_summed")
        s_sq = w.sem("squared")
        s_var = w.sem("var_done")
        s_sd = w.sem("sd_done")
        s_rs = w.sem("rs_done")
        s_xn = w.sem("xn_done")
        s_xh = w.sem("xn_hi_done")
        s_xl = w.sem("xn_lo_done")
        s_mm = w.sem("mm_done")
        s_ev = w.sem("mm_evacuated")
        s_cs = w.sem("conv_step")
        s_cv = w.sem("conv_done")
        s_u = w.sem("u_done")
        s_xd = w.sem("xdbl_done")
        s_dt = w.sem("dt_copied")
        s_bc = w.sem("bc_copied")
        s_ab = w.sem("abs_done")
        s_e = w.sem("e_done")
        s_rl = w.sem("relu_done")
        s_u1 = w.sem("one_plus_e")
        s_c = w.sem("rounding_error_found")
        s_rc = w.sem("rounding_error_taken")
        s_ln = w.sem("ln_done")
        s_dl = w.sem("delta_done")
        s_du = w.sem("du_done")
        s_zero = w.sem("hist_zeroed")
        s_one = w.sem("ones_set")
        s_warm = w.sem("table_warmed")
        st_u = w.sem("u_stored")
        st_z = w.sem("z_stored")
        st_bc = w.sem("bc_stored")
        st_dl = w.sem("delta_stored")
        st_du = w.sem("du_stored")
        block = ctx.enter_context(nc.Block())
        x_view = d.x.rearrange("b (k p) (j r) w -> b j p k (r w)", p=P, j=NJ)
        NQ = 2 * KD + KD

        def chunks(eng, prologue, main, peeled=1):
            prologue()
            for b in range(NB):
                with eng.Fori(0, NJ - peeled) as j:
                    main(b, j, lambda n: (b, j + n))
                for j in range(NJ - peeled, NJ):
                    main(b, j, lambda n: divmod(b * NJ + j + n, NJ) if b * NJ + j + n < NG else None)

        @block.sync
        def _(sp):
            def load(b, j, g):
                sp.wait_ge(s_xl, g + 1)
                sp.dma_start(v[:], x_view[b, j]).then_inc(s_x, 16)

            def prologue():
                load(0, 1, 1)

            def main(b, j, after):
                g = b * NJ + j
                sp.wait_ge(s_ev, 2 * KD * g + 2 * KD)
                sp.dma_start(d.spill[g][:, :, Z, :], z[:]).then_inc(st_z, 16)
                sp.wait_ge(s_u, KD * g + KD + 2)
                sp.dma_start(d.spill[g][:, :, U, :], u[:]).then_inc(st_u, 16)
                sp.wait_ge(s_bc, g + 2)
                sp.dma_start(d.bc[g], bc[RANK:64, :]).then_inc(st_bc, 16)
                if after(2):
                    load(*after(2), g + 2)
                sp.wait_ge(s_du, KD * g + KD + KD)
                sp.dma_start(d.spill[g][:, :, DU, :], du[:]).then_inc(st_du, 16)
                sp.dma_start(d.spill[g][:, :, DELTA, :], delta[:]).then_inc(st_dl, 16)

            for s in (st_u, st_z, st_bc, st_dl, st_du):
                sp.sem_inc(s, 16)
            chunks(sp, prologue, main, 2)
            for s in (st_u, st_z, st_bc, st_dl, st_du):
                sp.wait_ge(s, 16 * NG + 16)

        @block.gpsimd
        def _(pool):
            def main(b, j, after):
                g = b * NJ + j
                for m in range(KD):
                    n = KD * g + m
                    pool.wait_ge(s_rl, n + 1 + KD)
                    pool.wait_ge(s_c, n + 1)
                    nc.gpsimd.tensor_tensor(delta[:, m, :], delta[:, m, :], u1[:, m % 2, :],
                                            ALU.subtract).then_inc(s_rc, 1)
                pool.wait_ge(s_ln, g + 1)
                for m in range(KD):
                    n = KD * g + m
                    pool.wait_ge(s_rc, n + 3)
                    nc.gpsimd.tensor_tensor(delta[:, m, :], delta[:, m, :], du[:, m, :], ALU.add).then_inc(s_dl, 1)
                    pool.wait_ge(s_dl, n + 1 + KD)
                    nc.gpsimd.tensor_tensor(du[:, m, :], u[:, m, :], delta[:, m, :], ALU.mult).then_inc(s_du, 1)

            pool.sem_inc(s_rc, 2)
            pool.sem_inc(s_dl, KD)
            pool.sem_inc(s_du, KD)
            chunks(pool, lambda: None, main)

        @block.scalar
        def _(act):
            def norm_v(b, g):
                act.wait_ge(s_x, 16 * g + 16)
                for k in range(KC):
                    c = b * KC + k
                    last = nc.scalar.activation(v[:, k, :], v[:, k, :], ACT.Identity,
                                                bias=keep.shift[:, c:c + 1], scale=keep.scale[:, c:c + 1])
                last.then_inc(s_v, 1)

            def square(g, chunks_done):
                act.wait_ge(s_vc, g + 1)
                act.wait_ge(s_var, g + 1)
                act.wait_ge(s_dl, KD * chunks_done + KD)
                nc.scalar.activation(sq, v[:], ACT.Square).then_inc(s_sq, 1)

            def root(g):
                act.wait_ge(s_var, g + 2)
                act.wait_ge(s_rs, g + 1)
                nc.scalar.activation(sd[:], st_ps[:], ACT.Sqrt, bias=keep.gn_eps[:, 0:1]).then_inc(s_sd, 1)

            def prologue():
                norm_v(0, 0)
                square(0, 0)
                root(0)

            def silu_u(g, m):
                n = KD * g + m
                act.wait_ge(s_cv, n + 3)
                act.wait_ge(s_du, n + 1)
                if m == 0:
                    act.wait_ge(st_u, 16 * g + 16)
                nc.scalar.activation(u[:, m, :], acc[:, m % 2, :], ACT.Silu).then_inc(s_u, 1)

            def main(b, j, after):
                g = b * NJ + j
                act.wait_ge(s_warm, g + 1)
                nc.scalar.activation(warm[:], keep.gn_eps[:, 0:1], ACT.Silu).then_inc(s_warm, 1)
                act.wait_ge(st_z, 16 * g + 16)
                for m in range(KD):
                    q = 2 * m
                    act.wait_ge(s_mm, NQ * g + q + 1)
                    act.wait_ge(s_cv, KD * g + m + 1)
                    nc.scalar.activation(xr[:, m % 2, HIST:], mm[:, q % RING, :], ACT.Identity,
                                         bias=keep.b_in[:, m:m + 1]).then_inc(s_ev, 1)
                    if m:
                        silu_u(g, m - 1)
                    act.wait_ge(s_mm, NQ * g + q + 2)
                    nc.scalar.activation(z[:, m, :], mm[:, (q + 1) % RING, :], ACT.Silu,
                                         bias=keep.b_in[:, KD + m:KD + m + 1]).then_inc(s_ev, 1)
                    if m == 2 and after(1):
                        norm_v(after(1)[0], g + 1)
                    if m == 5 and after(1):
                        square(g + 1, g)
                silu_u(g, KD - 1)
                if after(1):
                    root(g + 1)
                act.wait_ge(s_xd, g + 1)
                nc.scalar.activation(dt[0:RANK, :], xd_ps[0:RANK, :], ACT.Copy).then_inc(s_dt, 1)
                act.wait_ge(st_bc, 16 * g + 16)
                nc.scalar.activation(bc[RANK:64, :], xd_ps[RANK:64, :], ACT.Copy).then_inc(s_bc, 1)
                if after(1):
                    act.wait_ge(s_var, g + 3)
                for m in range(KD):
                    n = KD * g + m
                    q = 2 * KD + m
                    act.wait_ge(s_mm, NQ * g + q + 1)
                    act.wait_ge(s_dl, n + 1)
                    nc.scalar.activation(e[:, m, :], mm[:, q % RING, :], ACT.Abs).then_inc(s_ab, 1)
                    if m == 0:
                        act.wait_ge(st_dl, 16 * g + 16)
                    nc.scalar.activation(delta[:, m, :], mm[:, q % RING, :], ACT.Relu).then_inc(s_rl, 1)
                    act.wait_ge(s_ab, n + 1 + KD)
                    nc.scalar.activation(e[:, m, :], e[:, m, :], ACT.Exp, scale=-1.0).then_inc(s_e, 1)
                act.wait_ge(s_e, KD * g + KD)
                act.wait_ge(st_du, 16 * g + 16)
                nc.scalar.activation(du[:], e[:], ACT.Ln, bias=1.0).then_inc(s_ln, 1)

            act.sem_inc(s_warm, 1)
            act.sem_inc(s_u, 2)
            act.sem_inc(s_ab, KD)
            act.sem_inc(s_rl, KD)
            act.sem_inc(s_dt, 1)
            act.sem_inc(s_bc, 1)
            chunks(act, prologue, main)

        @block.tensor
        def _(pe):
            def mean(g):
                pe.wait_ge(s_pre, 2 * g + 1)
                pe.wait_ge(s_rs, g + 1)
                nc.tensor.matmul(st_ps[:], keep.mean_w[:], half[:, 0, :], start=True, stop=True).then_inc(s_mu, 1)

            def var(g):
                pe.wait_ge(s_pre, 2 * g + 2)
                nc.tensor.matmul(st_ps[:], keep.mean_w[:], half[:, 0, :], start=True, stop=True).then_inc(s_var, 1)

            def prologue():
                mean(0)
                var(0)

            def bank_free(g, q):
                if RING <= q < RING + 2 * KD:
                    pe.wait_ge(s_ev, 2 * KD * g + q - RING + 1)
                else:
                    past = KD * g + (q + KD - RING if q < RING else KD + q - 2 * KD - RING) + 1
                    pe.wait_ge(s_ab, past)
                    pe.wait_ge(s_rl, past)

            def main(b, j, after):
                g = b * NJ + j
                pe.wait_ge(s_xh, g + 1)
                pe.wait_ge(s_xl, g + 2)
                for q in range(2 * KD):
                    if q == 11 and after(1):
                        mean(g + 1)
                    bank_free(g, q)
                    col = (q // 2 + (q % 2) * KD) * P
                    for k in range(KC):
                        last = split_matmul(nc, mm[:, q % RING, :], [part[:, k, col:col + P] for part in keep.w_in],
                                            [part[:, k, :] for part in xn], k == 0, k == KC - 1)
                    last.then_inc(s_mm, 1)
                if after(1):
                    var(g + 1)
                pe.wait_ge(s_dt, g + 1)
                pe.wait_ge(s_bc, g + 1)
                for m in range(KD):
                    pe.wait_ge(s_u, KD * g + m + 3)
                    last = nc.tensor.matmul(xd_ps[:], keep.w_xp[:, m, :], u[:, m, :], start=(m == 0), stop=(m == KD - 1))
                last.then_inc(s_xd, 1)
                pe.wait_ge(s_dt, g + 2)
                for m in range(KD):
                    q = 2 * KD + m
                    bank_free(g, q)
                    nc.tensor.matmul(mm[:, q % RING, :], keep.w_dt[:, m * P:(m + 1) * P], dt[:], start=True,
                                     stop=True).then_inc(s_mm, 1)

            pe.sem_inc(s_var, 1)
            pe.wait_ge(s_one, 1)
            chunks(pe, prologue, main)

        @block.vector
        def _(dve):
            nc.vector.memset(dt[RANK:RANK + 1, :], 1.0).then_inc(s_one, 1)
            dve.sem_inc(s_rs, 1)
            dve.sem_inc(s_xl, 1)
            dve.sem_inc(s_cs, 1)
            dve.sem_inc(s_cv, 2)

            def over_blocks(t):
                return t[:].rearrange("p (k t) -> p k t", k=1).broadcast_to([P, KC, T])

            def add_blocks(t, n):
                nc.vector.tensor_tensor(half[:], t[:, 0:2, :], t[:, 2:4, :], ALU.add).then_inc(s_half, 1)
                dve.wait_ge(s_half, n + 1)
                nc.vector.tensor_tensor(half[:, 0, :], half[:, 0, :], half[:, 1, :], ALU.add).then_inc(s_pre, 1)

            def add_values(g):
                dve.wait_ge(s_v, g + 1)
                dve.wait_ge(s_var, g + 1)
                add_blocks(v, 2 * g)

            def add_squares(g):
                dve.wait_ge(s_sq, g + 1)
                add_blocks(sq, 2 * g + 1)

            def centre(g):
                dve.wait_ge(s_mu, g + 1)
                nc.vector.tensor_tensor(v[:], v[:], over_blocks(st_ps), ALU.subtract).then_inc(s_vc, 1)

            def normalise(g):
                dve.wait_ge(s_sd, g + 1)
                nc.vector.reciprocal(rs[:], sd[:]).then_inc(s_rs, 1)
                dve.wait_ge(s_rs, g + 2)
                nc.vector.tensor_tensor(v[:], v[:], over_blocks(rs), ALU.mult).then_inc(s_xn, 1)

            def split(g):
                dve.wait_ge(s_xn, g + 1)
                nc.vector.tensor_copy(xn[0][:], v[:]).then_inc(s_xh, 1)
                dve.wait_ge(s_xh, g + 1)
                nc.vector.tensor_tensor(xn[1][:], v[:], xn[0][:].bitcast(F32), ALU.subtract).then_inc(s_xl, 1)

            def prologue():
                nc.vector.memset(hist[:], 0.0).then_inc(s_zero, 1)
                add_values(0)
                centre(0)
                add_squares(0)
                normalise(0)
                split(0)
                dve.wait_ge(s_zero, 1)

            def conv(g, m):
                n = KD * g + m
                base = 5 * n + 1
                slot = m % 2
                dve.wait_ge(s_ev, 2 * n + 1)
                dve.wait_ge(s_cs, 5 * KD * g + 1)
                nc.vector.tensor_copy(xr[:, slot, 0:HIST], hist[:, m, :]).then_inc(s_cs, 1)
                dve.wait_ge(s_cs, base + 1)
                dve.wait_ge(s_u, n + 1)
                nc.vector.tensor_scalar(acc[:, slot, :], xr[:, slot, 0:T], keep.conv_w[:, m, 0:1],
                                        keep.conv_b[:, m:m + 1], ALU.mult, ALU.add).then_inc(s_cs, 1)
                nc.vector.tensor_copy(hist[:, m, :], xr[:, slot, T:T + HIST]).then_inc(s_cs, 1)
                for i in range(1, TAPS):
                    dve.wait_ge(s_cs, base + 2 + (i if i > 1 else 0))
                    last = nc.vector.scalar_tensor_tensor(acc[:, slot, :], xr[:, slot, i:i + T], keep.conv_w[:, m, i:i + 1],
                                                          acc[:, slot, :], ALU.mult, ALU.add)
                    last.then_inc(s_cs if i < TAPS - 1 else s_cv, 1)

            def rounding_error(g, m):
                n = KD * g + m
                slot = m % 2
                dve.wait_ge(s_e, n + 1)
                dve.wait_ge(s_rc, n + 1)
                nc.vector.tensor_scalar(u1[:, slot, :], e[:, m, :], 1.0, None, ALU.add).then_inc(s_u1, 1)
                dve.wait_ge(s_u1, n + 1)
                nc.vector.scalar_tensor_tensor(u1[:, slot, :], u1[:, slot, :], 1.0, e[:, m, :], ALU.subtract,
                                               ALU.subtract).then_inc(s_c, 1)

            def main(b, j, after):
                g = b * NJ + j
                for m in range(KD):
                    conv(g, m)
                    if m == 3 and after(1):
                        add_values(g + 1)
                    if m == 4 and after(1):
                        centre(g + 1)
                    if m == 6 and after(1):
                        add_squares(g + 1)
                if after(1):
                    normalise(g + 1)
                    split(g + 1)
                for m in range(KD):
                    rounding_error(g, m)
                if after(1) and after(1)[0] != b:
                    dve.wait_ge(s_cs, 5 * KD * (g + 1) + 1)
                    nc.vector.memset(hist[:], 0.0).then_inc(s_zero, 1)
                    dve.wait_ge(s_zero, b + 2)

            chunks(dve, prologue, main)


def scan(nc, keep, d):
    NQ = NS // 4
    NC = KD * NQ
    with ExitStack() as ctx:
        w = Place(nc, ctx, "sc")
        b_all = w.sb("b_all", [P, NS, T])
        c_all = w.sb("c_all", [P, NS, T])
        blk = w.sb("blk", [P, 4, 4, T])
        da = w.sb("da", [P, 2, 4, T])
        dbu = w.sb("dbu", [P, 2, 4, T])
        h = w.sb("h", [P, NQ, 4, T])
        state = w.sb("state", [P, KD, NS])
        e0 = w.sb("e0", [P, 2, NS])
        carry = w.sb("carry", [P, 2, NS])
        yg = w.sb("yg", [P, 2, T])
        w_out = w.sb("w_out", [P, KD, DIM])
        skip = w.sb("skip", [P, KD, P])
        x_res = w.sb("x_res", [P, KC, T])
        y_ps = w.ps("y_ps", [P, 2, T])
        o_ps = w.ps("o_ps", [P, KC, T])

        s_w = w.sem("w_out_loaded")
        s_skip = w.sem("skip_made")
        s_b = [w.sem(f"b_loaded{q}") for q in range(NQ)]
        s_c = [w.sem(f"c_loaded{q}") for q in range(NQ)]
        s_blk = [w.sem(f"block_loaded{i}") for i in range(4)]
        s_x = w.sem("x_loaded")
        s_zero = w.sem("state_zeroed")
        s_gap = w.sem("decay_gap_zeroed")
        s_da = w.sem("da_done")
        s_dbu = w.sem("dbu_done")
        s_h = w.sem("h_done")
        s_st = w.sem("state_kept")
        s_e0 = w.sem("e0_done")
        s_car = w.sem("carry_done")
        s_first = w.sem("first_column_done")
        s_fc = w.sem("first_column_placed")
        s_hc = w.sem("hc_done")
        s_acc = w.sem("hc_summed")
        s_yg = w.sem("gated")
        s_op = w.sem("projected")
        s_res = w.sem("x1_done")
        s_sum = w.sem("x1_summed")
        st_x1 = w.sem("x1_stored")
        block = ctx.enter_context(nc.Block())
        x_view = d.x.rearrange("b (k p) (j r) w -> b j p k (r w)", p=P, j=NJ)

        def chunks(eng, body, before=None):
            for b in range(NB):
                if before:
                    before(b)
                body(b, 0, b * NJ, (b - 1, NJ - 1) if b else None)
                with eng.Fori(1, NJ) as j:
                    body(b, j, b * NJ + j, (b, j - 1))

        @block.sync
        def _(sp):
            sp.sem_inc(st_x1, 16)
            def block_in(g, i):
                sp.wait_ge(s_yg, KD * g + i + 1)
                sp.dma_start(blk[:, i % 4], d.spill[g][:, i]).then_inc(s_blk[i % 4], 16)

            def rows_in(g, t, s_t, read, at, q):
                for s in read:
                    sp.wait_ge(s, NC * g + q + 1)
                src = d.bc[g][at + 4 * q:at + 4 * q + 4, :].rearrange("(a n) t -> a n t", a=1)
                sp.dma_start(t[:, 4 * q:4 * q + 4, :], src.broadcast_to([P, 4, T])).then_inc(s_t[q], 16)

            def first_loads(g):
                block_in(g, 0)
                block_in(g, 1)
                for q in range(NQ + 1):
                    if q < NQ:
                        rows_in(g, b_all, s_b, (s_dbu, s_first), 0, q)
                    if q > 0:
                        rows_in(g, c_all, s_c, (s_hc,), NS, q - 1)
                    if q == 1:
                        block_in(g, 2)

            def store(g):
                sp.wait_ge(s_res, KC * g + 2 * KC)
                sp.dma_start(d.x1[g], x_res[:]).then_inc(st_x1, 16)

            def body(b, j, before, more):
                g = b * NJ + j
                for i in range(3, KD):
                    block_in(g, i)
                    if i == 4 and before:
                        store(g - 1)
                    if i == 5:
                        sp.wait_ge(st_x1, 16 * g + 16)
                        sp.dma_start(x_res[:], x_view[b, j]).then_inc(s_x, 16)
                if more:
                    first_loads(g + 1)

            first_loads(0)
            sp.dma_start(w_out[:], d.w_out).then_inc(s_w, 16)
            for b in range(NB):
                body(b, 0, b > 0, True)
                with sp.Fori(1, NJ - 1) as j:
                    body(b, j, True, True)
                body(b, NJ - 1, True, b < NB - 1)
            store(NG - 1)
            sp.wait_ge(st_x1, 16 * NG + 16)


        @block.gpsimd
        def _(pool):
            pool.sem_inc(s_dbu, NQ)

            def body(b, j, g, past):
                for i in range(KD):
                    pool.wait_ge(s_blk[i % 4], 32 * g + 16 * (i // 4) + 16)
                    for q in range(NQ):
                        n = NC * g + NQ * i + q
                        if i == 0:
                            pool.wait_ge(s_b[q], 16 * g + 16)
                        pool.wait_ge(s_h, n + 1)
                        du = blk[:, i % 4, DU:DU + 1, 1:].broadcast_to([P, 4, T - 1])
                        nc.gpsimd.tensor_tensor(dbu[:, q % 2, :, 1:], b_all[:, 4 * q:4 * q + 4, 1:], du,
                                                ALU.mult).then_inc(s_dbu, 1)

            chunks(pool, body)

        @block.scalar
        def _(act):
            def keep_state(k):
                i, q = divmod(k, NQ)
                nc.scalar.activation(state[:, i, 4 * q:4 * q + 4], h[:, k % NQ, :, T - 1], ACT.Copy).then_inc(s_st, 1)

            def first_decay(g, i):
                act.wait_ge(s_blk[i % 4], 32 * g + 16 * (i // 4) + 16)
                act.wait_ge(s_car, KD * g + i + 1)
                nc.scalar.activation(e0[:, i % 2, :], keep.neg_a[:, i * NS:(i + 1) * NS], ACT.Exp,
                                     scale=blk[:, i % 4, DELTA, 0:1]).then_inc(s_e0, 1)

            def x1_out(g, m):
                act.wait_ge(s_op, KC * (KD * g + KD - 1) + m + 1 + 2 * KC)
                nc.scalar.activation(x_res[:, m, :], o_ps[:, m, :], ACT.Copy).then_inc(s_sum, 1)

            def body(b, j, g, past):
                first_decay(g, 0)
                for k in range(NC):
                    i, q = divmod(k, NQ)
                    act.wait_ge(s_h, NC * g + k + 1)
                    if k >= 2:
                        keep_state(k - 2)
                    elif past:
                        keep_state(NC - 2 + k)
                    for r in range(4):
                        c = i * NS + 4 * q + r
                        last = nc.scalar.activation(da[:, k % 2, r, 1:], blk[:, i % 4, DELTA, 1:], ACT.Exp,
                                                    scale=keep.neg_a[:, c:c + 1])
                    last.then_inc(s_da, 1)
                    if i:
                        act.wait_ge(s_first, NC * g + k + 1 + NQ)
                        nc.scalar.activation(dbu[:, k % 2, :, 0], carry[:, i % 2, 4 * q:4 * q + 4], ACT.Copy).then_inc(s_fc, 1)
                    if 7 <= k < 7 + KC and past:
                        x1_out(g - 1, k - 7)
                    if q == 0 and i < KD - 1:
                        first_decay(g, i + 1)

            act.sem_inc(s_st, NQ)
            act.sem_inc(s_sum, KC)
            chunks(act, body)
            for k in (NC - 2, NC - 1):
                act.wait_ge(s_h, NC * (NG - 1) + k + 3)
                keep_state(k)
            for m in range(KC):
                x1_out(NG - 1, m)

        @block.tensor
        def _(pe):
            pe.sem_inc(s_acc, NQ)
            pe.sem_inc(s_op, 2 * KC)
            pe.wait_ge(s_skip, KD)

            def project(g, i, m):
                if m == 0 and i == 0:
                    pe.wait_ge(s_w, 16)
                if m == 0:
                    pe.wait_ge(s_yg, KD * g + i + 5)
                if i == 0:
                    pe.wait_ge(s_sum, KC * g + m + 1)
                if i == KD - KC + m:
                    if m == 0:
                        pe.wait_ge(s_x, 16 * g + 16)
                    nc.tensor.matmul(o_ps[:, m, :], keep.ident[:], x_res[:, m, :], start=False, stop=False)
                nc.tensor.matmul(o_ps[:, m, :], w_out[:, i, m * P:(m + 1) * P], yg[:, i % 2, :],
                                 start=(i == 0), stop=(i == KD - 1)).then_inc(s_op, 1)

            def body(b, j, g, past):
                for k in range(NC):
                    i, q = divmod(k, NQ)
                    n = KD * g + i
                    if q == 0:
                        pe.wait_ge(s_blk[i % 4], 32 * g + 16 * (i // 4) + 16)
                        pe.wait_ge(s_yg, n + 3)
                        nc.tensor.matmul(y_ps[:, i % 2, :], skip[:, i, :], blk[:, i % 4, U, :], start=True, stop=False)
                    pe.wait_ge(s_hc, NC * g + k + 1 + NQ)
                    for r in range(4):
                        last = nc.tensor.matmul(y_ps[:, i % 2, :], keep.ident[:], h[:, q, r, :],
                                                start=False, stop=(q == NQ - 1 and r == 3))
                    last.then_inc(s_acc, 1)
                    late, m = divmod(k - 7, KC)
                    if late >= 0:
                        project(g, late, m)
                    elif past:
                        project(g - 1, KD + late, m)

            chunks(pe, body)
            for k in range(NC, NC + 7):
                project(NG - 1, *divmod(k - 7, KC))

        @block.vector
        def _(dve):
            for i in range(KD):
                nc.vector.tensor_scalar(skip[:, i, :], keep.ident[:], keep.dskip[:, i:i + 1], None,
                                        ALU.mult).then_inc(s_skip, 1)
            dve.sem_inc(s_h, 2)
            dve.sem_inc(s_car, 2)
            dve.sem_inc(s_first, NQ)
            nc.vector.memset(da[:, :, :, 0], 0.0).then_inc(s_gap, 1)
            dve.wait_ge(s_gap, 1)
            dve.sem_inc(s_hc, NQ)
            dve.sem_inc(s_yg, 4)
            dve.sem_inc(s_res, KC)

            def before(b):
                dve.wait_ge(s_st, b * NJ * NC + NQ)
                dve.wait_ge(s_car, KD * NJ * b + 2)
                nc.vector.memset(state[:], 0.0).then_inc(s_zero, 1)
                dve.wait_ge(s_zero, b + 1)

            def gate(g, i):
                n = KD * g + i
                dve.wait_ge(s_acc, NC * g + NQ * i + NQ + NQ)
                dve.wait_ge(s_op, KC * n + KC)
                nc.vector.tensor_tensor(yg[:, i % 2, :], y_ps[:, i % 2, :], blk[:, i % 4, Z, :],
                                        ALU.mult).then_inc(s_yg, 1)

            def statistics(g, b, j, m):
                dve.wait_ge(s_sum, KC * g + m + 1 + KC)
                nc.vector.bn_stats(keep.stats[:, b * KC + m, j, :], x_res[:, m, :]).then_inc(s_res, 1)

            def body(b, j, g, past):
                def carry_in(i):
                    dve.wait_ge(s_e0, KD * g + i + 1)
                    nc.vector.tensor_tensor(carry[:, i % 2, :], e0[:, i % 2, :], state[:, i, :], ALU.mult).then_inc(s_car, 1)

                def first_column(q):
                    dve.wait_ge(s_h, NC * g + q + 1)
                    dve.wait_ge(s_car, KD * g + 3)
                    dve.wait_ge(s_b[q], 16 * g + 16)
                    nc.vector.scalar_tensor_tensor(dbu[:, q % 2, :, 0], b_all[:, 4 * q:4 * q + 4, 0], blk[:, 0, DU, 0:1],
                                                   carry[:, 0, 4 * q:4 * q + 4], ALU.mult, ALU.add).then_inc(s_first, 1)

                def first_columns(i):
                    dve.wait_ge(s_car, KD * g + i + 3)
                    nc.vector.scalar_tensor_tensor(carry[:, i % 2, :], b_all[:, :, 0], blk[:, i % 4, DU, 0:1],
                                                   carry[:, i % 2, :], ALU.mult, ALU.add).then_inc(s_first, NQ)

                def recur(k):
                    n = NC * g + k
                    if k < NQ:
                        dve.wait_ge(s_first, n + 1 + NQ)
                    else:
                        dve.wait_ge(s_fc, (NC - NQ) * g + k - NQ + 1)
                    dve.wait_ge(s_da, n + 1)
                    dve.wait_ge(s_dbu, n + 1 + NQ)
                    dve.wait_ge(s_acc, n + 1)
                    flat = [t.rearrange("p r t -> p (r t)") for t in (h[:, k % NQ], da[:, k % 2], dbu[:, k % 2])]
                    nc.vector.tensor_tensor_scan(*flat, 0.0, ALU.mult, ALU.add).then_inc(s_h, 1)

                def weigh(k):
                    i, q = divmod(k, NQ)
                    n = NC * g + k
                    dve.wait_ge(s_h, n + 3)
                    if i == 0:
                        dve.wait_ge(s_c[q], 16 * g + 16)
                    dve.wait_ge(s_st, n + 1 + NQ)
                    nc.vector.tensor_tensor(h[:, k % NQ], h[:, k % NQ], c_all[:, 4 * q:4 * q + 4, :],
                                            ALU.mult).then_inc(s_hc, 1)

                carry_in(0)
                first_column(0)
                for k in range(NC):
                    recur(k)
                    if k < NQ - 1:
                        first_column(k + 1)
                    if k % NQ == 2 and k < NC - NQ:
                        carry_in(k // NQ + 1)
                    if k % NQ == 3 and k < NC - NQ:
                        first_columns(k // NQ + 1)
                    if k:
                        weigh(k - 1)
                    if k == 2 and past:
                        gate(g - 1, KD - 1)
                    if 10 <= k < 10 + KC and past:
                        statistics(g - 1, *past, k - 10)
                    if k % NQ == 2 and k > NQ:
                        gate(g, k // NQ - 1)
                weigh(NC - 1)

            chunks(dve, body, before)
            gate(NG - 1, KD - 1)
            for m in range(KC):
                statistics(NG - 1, NB - 1, NJ - 1, m)
            dve.wait_ge(s_res, KC * NG + KC)


def memory_setup(nc, keep, d):
    with ExitStack() as ctx:
        w = Place(nc, ctx, "ms")
        mn = w.sb("mn", [P, KK, DIM])
        sq = w.sb("sq", [P, DIM])
        norm = w.sb("norm", [P, KK])
        tr = w.ps("tr", [P, 4, T])
        s_sq = w.sem("squares")
        s_root = w.sem("root")
        step = w.sem("step")
        s_mn = w.sem("scaled")
        s_tr = w.sem("transposed")
        s_hi = w.sem("high")
        s_lo = w.sem("low")
        block = ctx.enter_context(nc.Block())
        HALVES = [(c, f) for c in range(KC) for f in range(KM // T)]
        PER = T // P

        @block.scalar
        def _(act):
            act.wait_ge(keep.m_loaded, 16)
            for k in range(KK):
                if k:
                    act.wait_ge(s_sq, k)
                nc.scalar.activation(sq[:], keep.m[:, k, :], ACT.Square, accum_out=norm[:, k:k + 1]).then_inc(s_sq, 1)
            act.wait_ge(s_sq, KK)
            nc.scalar.activation(norm[:], norm[:], ACT.Sqrt).then_inc(s_root, 1)
            for n, (c, f) in enumerate(HALVES):
                act.wait_ge(s_tr, n + 1)
                nc.scalar.activation(keep.mt[0][:, c, f * T:(f + 1) * T], tr[:, n % 4, :], ACT.Copy).then_inc(s_hi, 1)

        @block.tensor
        def _(pe):
            pe.sem_inc(s_lo, 4)
            pe.wait_ge(s_mn, KK)
            for n, (c, f) in enumerate(HALVES):
                pe.wait_ge(s_lo, n + 1)
                for i in range(PER):
                    last = nc.tensor.transpose(tr[:, n % 4, i * P:(i + 1) * P], mn[:, f * PER + i, c * P:(c + 1) * P],
                                               keep.ident[:])
                last.then_inc(s_tr, 1)

        @block.vector
        def _(dve):
            dve.wait_ge(s_root, 1)
            nc.vector.tensor_scalar(norm[:], norm[:], NORM_EPS, None, ALU.max).then_inc(step, 1)
            dve.wait_ge(step, 1)
            nc.vector.reciprocal(norm[:], norm[:]).then_inc(step, 1)
            dve.wait_ge(step, 2)
            for k in range(KK):
                nc.vector.tensor_scalar(mn[:, k, :], keep.m[:, k, :], norm[:, k:k + 1], None, ALU.mult).then_inc(s_mn, 1)
            for n, (c, f) in enumerate(HALVES):
                cols = slice(f * T, (f + 1) * T)
                dve.wait_ge(s_hi, n + 1)
                nc.vector.tensor_tensor(keep.mt[1][:, c, cols], tr[:, n % 4, :], keep.mt[0][:, c, cols].bitcast(F32),
                                        ALU.subtract).then_inc(s_lo, 1)
            dve.wait_ge(s_lo, len(HALVES) + 4)
            dve.wait_ge(keep.iota_loaded, 16)


def assign(nc, keep, d):
    SUMS = (0, 2, 4, 6, KK)
    TT = T // P
    with ExitStack() as ctx:
        w = Place(nc, ctx, "as")
        v = keep.v
        vp = [w.sb("v_hi", [P, KC, T], F32R), w.sb("v_lo", [P, KC, T], F32R)]
        xt = [w.sb("xt_hi", [P, 2, TT, DIM], F32R), w.sb("xt_lo", [P, 2, TT, DIM], F32R)]
        sq = w.sb("sq", [P, DIM])
        ss = w.sb("ss", [P, TT])
        nrm = w.sb("nrm", [P, TT])
        rn = w.sb("rn", [P, TT])
        top = w.sb("top", [P, TT, 8])
        nb = w.sb("nb", [P, TT])
        idx = w.sb("idx", [P, TT, 8], U32)
        idxf = w.sb("idxf", [P, TT])
        oh = w.sb("oh", [P, 2, TT, KM], F32R)
        e = w.sb("e", [P, 2, KM])
        es = w.sb("es", [P, TT])
        er = w.sb("er", [P, TT])
        et = w.sb("et", [P, 2, KK, T])
        sc_ps = w.ps("sc_ps", [P, 2, KM])
        tr_ps = w.ps("tr_ps", [P, 2, T])
        sum_ps = w.ps("sum_ps", [P, 2, T])

        s_x = keep.x_loaded
        s_v = w.sem("v_done")
        s_vh = w.sem("v_hi_done")
        s_vl = w.sem("v_lo_done")
        s_vt = w.sem("tokens_transposed")
        s_tt = w.sem("softmax_transposed")
        s_xh = w.sem("xt_hi_done")
        s_ss = w.sem("squares")
        s_xl = w.sem("xt_lo_done")
        s_nr = w.sem("norm_done")
        s_cl = w.sem("norm_clamped")
        s_rn = w.sem("rn_done")
        s_sc = w.sem("scored")
        s_top = w.sem("top_done")
        s_nb = w.sem("bias_done")
        s_ix = w.sem("index_done")
        s_if = w.sem("index_float")
        s_oh = w.sem("onehot_done")
        s_ex = w.sem("exp_done")
        s_er = w.sem("exp_sum_inverted")
        s_en = w.sem("softmax_done")
        s_et = w.sem("softmax_turned")
        s_sp = w.sem("sums_done")
        s_ad = w.sem("sums_added")
        s_ct = w.sem("counted")
        s_zc = w.sem("count_zeroed")
        s_zs = w.sem("sums_zeroed")
        st_e = [w.sem(f"softmax_stored{i}") for i in range(2)]
        block = ctx.enter_context(nc.Block())

        def chunks(eng, main):
            def pair(b, i, fixed):
                for u in range(2):
                    g = b * NJ + 2 * i + u
                    if fixed:
                        main(g, u, g // 2, lambda n: (g + n) // NJ if g + n < NG else None, g == 0)
                    else:
                        main(g, u, b * (NJ // 2) + i, lambda n: b, False)

            for b in range(NB):
                head = 1 if b == 0 else 0
                for i in range(head):
                    pair(b, i, True)
                with eng.Fori(head, NJ // 2 - 1) as i:
                    pair(b, i, False)
                pair(b, NJ // 2 - 1, True)

        @block.sync
        def _(sp):
            def load(g):
                sp.wait_ge(s_vl, g + 1)
                sp.wait_ge(s_vt, TT * g + TT)
                sp.dma_start(v[:], d.x1[g]).then_inc(s_x, 16)

            def store(g, u):
                sp.wait_ge(s_et, 2 * TT * g + 4 * TT)
                sp.dma_start(d.soft[g], et[:, u]).then_inc(st_e[u], 16)

            def main(g, u, i, after, first):
                if after(1) is not None:
                    load(g + 1)
                if not first:
                    store(g - 1, 1 - u)

            for u in range(2):
                sp.sem_inc(st_e[u], 16)
            chunks(sp, main)
            store(NG - 1, 1)
            for u in range(2):
                sp.wait_ge(st_e[u], 16 * NG // 2 + 16)

        @block.gpsimd
        def _(pool):
            nc.gpsimd.memset(keep.count[:], 0.0).then_inc(s_zc, 1)
            pool.wait_ge(s_zc, 1)

            def main(g, u, i, after, first):
                for s in range(TT):
                    n = TT * g + s
                    pool.wait_ge(s_oh, n + 3)
                    pool.wait_ge(s_ct, n + TT + 1)
                    nc.gpsimd.tensor_tensor(keep.count[:], keep.count[:], oh[:, u, s, :].bitcast(F32),
                                            ALU.add).then_inc(s_ct, 1)

            pool.sem_inc(s_ct, TT + 1)
            chunks(pool, main)
            pool.wait_ge(s_ct, TT * NG + TT + 1)

        @block.scalar
        def _(act):
            def norm_v(b, g):
                act.wait_ge(s_x, 16 * g + 16)
                for k in range(KC):
                    c = b * KC + k
                    last = nc.scalar.activation(v[:, k, :], v[:, k, :], ACT.Identity,
                                                bias=keep.shift[:, c:c + 1], scale=keep.scale[:, c:c + 1])
                last.then_inc(s_v, 1)

            def split(g):
                act.wait_ge(s_v, g + 1)
                act.wait_ge(s_sc, TT * g + 1)
                nc.scalar.activation(vp[0][:], v[:], ACT.Copy).then_inc(s_vh, 1)

            def tokens(g, u, s):
                act.wait_ge(s_vt, TT * g + s + 1 + TT)
                if s == 0:
                    act.wait_ge(s_sp, KK * g + KK)
                nc.scalar.activation(xt[0][:, u, s, :], tr_ps[:, s % 2, :], ACT.Copy).then_inc(s_xh, 1)
                act.wait_ge(s_ss, TT * g + s + 1)
                nc.scalar.activation(sq[:], tr_ps[:, s % 2, :], ACT.Square, accum_out=ss[:, s:s + 1]).then_inc(s_ss, 1)

            def exp(g, s):
                act.wait_ge(s_nb, TT * g + s + 1)
                act.wait_ge(s_ix, TT * g + s + 1)
                act.wait_ge(s_tt, 2 * TT * g + 2 * s + 2 * TT - 2)
                nc.scalar.activation(e[:, s % 2, :], sc_ps[:, s % 2, :], ACT.Exp, bias=nb[:, s:s + 1],
                                     scale=rn[:, s:s + 1], accum_out=es[:, s:s + 1]).then_inc(s_ex, 1)

            def turned(g, u, i, s):
                if s == 0:
                    act.wait_ge(st_e[u], 16 * i + 16)
                for f in range(2):
                    act.wait_ge(s_tt, 2 * TT * g + 2 * s + f + 1 + 2 * TT)
                    nc.scalar.activation(et[:, u, 4 * f:4 * f + 4, s * P:(s + 1) * P],
                                         tr_ps[:, f, :].rearrange("p (k t) -> p k t", t=P), ACT.Copy).then_inc(s_et, 1)

            def main(g, u, i, after, first):
                for s in range(TT):
                    tokens(g, u, s)
                act.wait_ge(s_ss, TT * g + TT + 1)
                act.wait_ge(s_cl, g + 1)
                nc.scalar.activation(nrm[:], ss[:], ACT.Sqrt).then_inc(s_nr, 1)
                for s in range(TT):
                    if s == 0 and not first:
                        turned(g - 1, 1 - u, i, TT - 1)
                    if s == TT - 1 and after(1) is not None:
                        split(g + 1)
                    exp(g, s)
                    if s > 0:
                        turned(g, u, i, s - 1)
                    if s == 1 and after(1) is not None:
                        norm_v(after(1), g + 1)

            act.sem_inc(s_ex, 2)
            act.sem_inc(s_ss, 1)
            act.sem_inc(s_et, 2 * TT)
            norm_v(0, 0)
            split(0)
            chunks(act, main)
            turned(NG - 1, 1, 0, TT - 1)

        @block.tensor
        def _(pe):
            def turn_tokens(g, s):
                if s < 2:
                    pe.wait_ge(s_et, 2 * TT * g + 5 + s)
                else:
                    pe.wait_ge(s_xl, TT * g + s - 1)
                for k in range(KC):
                    last = nc.tensor.transpose(tr_ps[:, s % 2, k * P:(k + 1) * P], v[:, k, s * P:(s + 1) * P],
                                               keep.ident[:])
                last.then_inc(s_vt, 1)

            def turn_exp(g, s, tokens_before=None):
                pe.wait_ge(s_en, TT * g + s + 1)
                for f in range(2):
                    if tokens_before is not None:
                        pe.wait_ge(s_xl, TT * tokens_before + f + 3)
                    pe.wait_ge(s_et, 2 * TT * g + 2 * s + f - 1 + 2 * TT)
                    for i in range(4):
                        k = 4 * f + i
                        last = nc.tensor.transpose(tr_ps[:, f, i * P:(i + 1) * P], e[:, s % 2, k * P:(k + 1) * P],
                                                   keep.ident[:])
                    last.then_inc(s_tt, 1)

            def sums(g, u, k):
                pe.wait_ge(s_oh, TT * g + TT + 2)
                pe.wait_ge(s_xl, TT * g + TT)
                pe.wait_ge(s_ad, KK * g + k + 1)
                for s in range(TT):
                    for part in xt:
                        last = nc.tensor.matmul(sum_ps[:, k % 2, :], oh[:, u, s, k * P:(k + 1) * P], part[:, u, s, :],
                                                start=(s == 0 and part is xt[0]), stop=(s == TT - 1 and part is xt[1]))
                last.then_inc(s_sp, 1)

            def main(g, u, i, after, first):
                pe.wait_ge(s_v, g + 1)
                turn_tokens(g, 0)
                turn_tokens(g, 1)
                pe.wait_ge(s_vh, g + 1)
                pe.wait_ge(s_vl, g + 2)
                for s in range(TT):
                    n = TT * g + s
                    pe.wait_ge(s_ex, n + 1)
                    pe.wait_ge(s_oh, n + 1)
                    for f in range(KM // T):
                        cols = slice(f * T, (f + 1) * T)
                        for k in range(KC):
                            last = split_matmul(nc, sc_ps[:, s % 2, cols], [t[:, k, s * P:(s + 1) * P] for t in vp],
                                                [t[:, k, cols] for t in keep.mt], k == 0, k == KC - 1)
                    last.then_inc(s_sc, 1)
                    if s == 0:
                        turn_tokens(g, 2)
                        turn_tokens(g, 3)
                    for k in range(SUMS[s], SUMS[s + 1]):
                        if not first:
                            sums(g - 1, 1 - u, k)
                    if s > 0:
                        turn_exp(g, s - 1, g if s == 1 else None)
                    elif not first:
                        turn_exp(g - 1, TT - 1, g)

            pe.sem_inc(s_vt, TT)
            pe.sem_inc(s_tt, 2 * TT)
            pe.sem_inc(s_sc, 1)
            pe.sem_inc(s_sp, 2 * KK)
            chunks(pe, main)
            for k in range(KK):
                sums(NG - 1, 1, k)
                if k == 0:
                    turn_exp(NG - 1, TT - 1)

        @block.vector
        def _(dve):
            nc.vector.memset(keep.sums[:], 0.0).then_inc(s_zs, 1)
            dve.wait_ge(s_zs, 1)
            dve.sem_inc(s_oh, 2)
            dve.sem_inc(s_ad, 2)
            dve.sem_inc(s_vl, 1)
            dve.sem_inc(s_cl, 1)

            def split(g):
                dve.wait_ge(s_vh, g + 1)
                nc.vector.tensor_tensor(vp[1][:], v[:], vp[0][:].bitcast(F32), ALU.subtract).then_inc(s_vl, 1)

            def tokens(g, u, s):
                dve.wait_ge(s_xh, TT * g + s + 1)
                dve.wait_ge(s_ss, TT * g + s + 2)
                nc.vector.tensor_tensor(xt[1][:, u, s, :], tr_ps[:, s % 2, :], xt[0][:, u, s, :].bitcast(F32),
                                        ALU.subtract).then_inc(s_xl, 1)

            def nearest(g, u, s):
                n = TT * g + s
                dve.wait_ge(s_sc, n + 2)
                nc.vector.memset(nb[:, s:s + 1], 0.0)
                nc.vector.max(top[:, s, :], sc_ps[:, s % 2, :]).then_inc(s_top, 1)
                dve.wait_ge(s_top, n + 1)
                nc.vector.memset(idxf[:, s:s + 1], 0.0)
                nc.vector.max_index(idx[:, s, :], top[:, s, :], sc_ps[:, s % 2, :]).then_inc(s_ix, 1)
                if s == 0:
                    dve.wait_ge(s_nr, g + 1)
                    nc.vector.tensor_scalar(rn[:], nrm[:], NORM_EPS, None, ALU.max).then_inc(s_cl, 1)
                    dve.wait_ge(s_cl, g + 2)
                    nc.vector.reciprocal(rn[:], rn[:]).then_inc(s_rn, 1)
                    dve.wait_ge(s_rn, g + 1)
                nc.vector.tensor_scalar(nb[:, s:s + 1], top[:, s, 0:1], rn[:, s:s + 1], -1.0, ALU.mult,
                                        ALU.mult).then_inc(s_nb, 1)
                dve.wait_ge(s_ix, n + 1)
                nc.vector.tensor_copy(idxf[:, s:s + 1], idx[:, s, 0:1]).then_inc(s_if, 1)
                dve.wait_ge(s_if, n + 1)
                if s == 0:
                    dve.wait_ge(s_ct, TT * g + 1)
                    dve.wait_ge(s_sp, KK * g + KK)
                nc.vector.tensor_scalar(oh[:, u, s, :], keep.iota[:], idxf[:, s:s + 1], None, ALU.is_equal).then_inc(s_oh, 1)

            def softmax(g, s):
                n = TT * g + s
                dve.wait_ge(s_ex, n + 3)
                nc.vector.reciprocal(er[:, s:s + 1], es[:, s:s + 1]).then_inc(s_er, 1)
                dve.wait_ge(s_er, n + 1)
                nc.vector.tensor_scalar(e[:, s % 2, :], e[:, s % 2, :], er[:, s:s + 1], None, ALU.mult).then_inc(s_en, 1)

            def add(g, k):
                dve.wait_ge(s_sp, KK * g + k + 1 + 2 * KK)
                nc.vector.tensor_tensor(keep.sums[:, k, :], keep.sums[:, k, :], sum_ps[:, k % 2, :], ALU.add).then_inc(s_ad, 1)

            def main(g, u, i, after, first):
                for s in range(TT):
                    tokens(g, u, s)
                for s in range(TT):
                    if s:
                        softmax(g, s - 1)
                    nearest(g, u, s)
                    if s == TT - 1 and after(1) is not None:
                        split(g + 1)
                    for k in range(SUMS[s], SUMS[s + 1]):
                        if not first:
                            add(g - 1, k)
                softmax(g, TT - 1)

            split(0)
            chunks(dve, main)
            for k in range(KK):
                add(NG - 1, k)
            dve.wait_ge(s_ad, KK * NG + 2)


def readout(nc, keep, d):
    with ExitStack() as ctx:
        w = Place(nc, ctx, "ro")
        nm = [w.sb("nm_hi", [P, KK, DIM], F32R), w.sb("nm_lo", [P, KK, DIM], F32R)]
        share = w.sb("share", [P, KK])
        ones = w.sb("ones", [P, 1])
        et = w.sb("et", [P, 2, KK, T])
        ep = [w.sb("e_hi", [P, 2, KK, T], F32R), w.sb("e_lo", [P, 2, KK, T], F32R)]
        x1 = w.sb("x1", [P, 2, KC, T])
        o_ps = w.ps("o_ps", [P, 2, KC, T])

        s_step = w.sem("step")
        s_one = w.sem("ones_set")
        s_cnt = w.sem("counts_done")
        s_nm = w.sem("new_m_done")
        s_nh = w.sem("new_m_hi")
        s_nl = w.sem("new_m_lo")
        s_e = [w.sem(f"softmax_loaded{i}") for i in range(2)]
        s_x = [w.sem(f"x1_loaded{i}") for i in range(2)]
        s_eh = w.sem("e_hi_done")
        s_el = w.sem("e_lo_done")
        s_o = w.sem("out_summed")
        s_r = w.sem("residual_added")
        s_st = [w.sem(f"out_stored{i}") for i in range(2)]
        block = ctx.enter_context(nc.Block())
        out_view = d.out.rearrange("b (k p) (j r) w -> b j p k (r w)", p=P, j=NJ)

        def chunks(eng, body):
            with eng.Fori(0, NG // 2) as i:
                for u in range(2):
                    body(2 * i + u, u, i)

        @block.gpsimd
        def _(pool):
            def body(g, u, i):
                pool.wait_ge(s_el, g + 1)
                pool.dma_start(et[:, u], d.soft[g]).then_inc(s_e[u], 16)
                pool.wait_ge(s_st[u], 16 * i + 16)
                pool.dma_start(x1[:, u], d.x1[g]).then_inc(s_x[u], 16)

            chunks(pool, body)

        @block.sync
        def _(sp):
            for u in range(2):
                sp.sem_inc(s_st[u], 16)
            for b in range(NB):
                with sp.Fori(0, NJ // 2) as i:
                    for u in range(2):
                        j = 2 * i + u
                        sp.wait_ge(s_r, KC * (b * NJ + j) + 3 * KC)
                        sp.dma_start(out_view[b, j], x1[:, u]).then_inc(s_st[u], 16)
            for u in range(2):
                sp.wait_ge(s_st[u], 16 * NG // 2 + 16)

        @block.scalar
        def _(act):
            for k in range(KK):
                act.wait_ge(s_nm, k + 1)
                nc.scalar.activation(nm[0][:, k, :], keep.m[:, k, :], ACT.Copy).then_inc(s_nh, 1)

            def body(g, u, i):
                act.wait_ge(s_e[u], 16 * i + 16)
                act.wait_ge(s_o, KC * g + KC)
                nc.scalar.activation(ep[0][:, u], et[:, u], ACT.Copy).then_inc(s_eh, 1)

            chunks(act, body)

        @block.tensor
        def _(pe):
            pe.sem_inc(s_o, 2 * KC)
            pe.wait_ge(s_one, 1)
            for k in range(KK):
                last = nc.tensor.matmul(o_ps[:, 0, 0, k:k + 1], keep.count[:, k * P:(k + 1) * P], ones[:],
                                        start=True, stop=True)
            last.then_inc(s_cnt, 1)
            pe.wait_ge(s_nl, KK)

            def body(g, u, i):
                pe.wait_ge(s_eh, g + 1)
                pe.wait_ge(s_el, g + 3)
                for m in range(KC):
                    pe.wait_ge(s_r, KC * g + m + 1)
                    for k in range(KK):
                        last = split_matmul(nc, o_ps[:, u, m, :], [t[:, k, m * P:(m + 1) * P] for t in nm],
                                            [t[:, u, k, :] for t in ep], k == 0, k == KK - 1)
                    last.then_inc(s_o, 1)

            chunks(pe, body)

        @block.vector
        def _(dve):
            dve.sem_inc(s_r, 2 * KC)
            dve.sem_inc(s_el, 2)
            nc.vector.memset(ones[:], 1.0).then_inc(s_one, 1)
            nc.vector.tensor_scalar(keep.m[:], keep.m[:], RATE, None, ALU.mult).then_inc(s_step, 1)
            dve.wait_ge(s_cnt, 1)
            nc.vector.tensor_scalar(share[:], o_ps[:, 0, 0, 0:KK], MEAN_EPS, None, ALU.add).then_inc(s_step, 1)
            dve.wait_ge(s_step, 2)
            nc.vector.reciprocal(share[:], share[:]).then_inc(s_step, 1)
            dve.wait_ge(s_step, 3)
            nc.vector.tensor_scalar(share[:], share[:], 1.0 - RATE, None, ALU.mult).then_inc(s_step, 1)
            dve.wait_ge(s_step, 4)
            for k in range(KK):
                nc.vector.scalar_tensor_tensor(keep.m[:, k, :], keep.sums[:, k, :], share[:, k:k + 1], keep.m[:, k, :],
                                               ALU.mult, ALU.add).then_inc(s_nm, 1)
            for k in range(KK):
                dve.wait_ge(s_nh, k + 1)
                nc.vector.tensor_tensor(nm[1][:, k, :], keep.m[:, k, :], nm[0][:, k, :].bitcast(F32),
                                        ALU.subtract).then_inc(s_nl, 1)

            def split(g, u):
                dve.wait_ge(s_eh, g + 1)
                nc.vector.tensor_tensor(ep[1][:, u], et[:, u], ep[0][:, u].bitcast(F32), ALU.subtract).then_inc(s_el, 1)

            def residual(g, u, i):
                dve.wait_ge(s_x[u], 16 * i + 16)
                for m in range(KC):
                    dve.wait_ge(s_o, KC * g + m + 1 + 2 * KC)
                    nc.vector.tensor_tensor(x1[:, u, m, :], x1[:, u, m, :], o_ps[:, u, m, :], ALU.add).then_inc(s_r, 1)

            split(0, 0)
            with dve.Fori(0, NG // 2 - 1) as i:
                for u in range(2):
                    split(2 * i + u + 1, 1 - u)
                    residual(2 * i + u, u, i)
            split(NG - 1, 1)
            residual(NG - 2, 0, NG // 2 - 1)
            residual(NG - 1, 1, NG // 2 - 1)


class Names:
    pass


def program(nc, d):
    d.spill = nc.dram_tensor("spill", (NG, P, KD, 4, T), F32).ap()
    d.bc = nc.dram_tensor("bc", (NG, 2 * NS, T), F32).ap()
    d.x1 = nc.dram_tensor("x1", (NG, P, KC, T), F32).ap()
    d.soft = nc.dram_tensor("soft", (NG, P, KK, T), F32).ap()
    keep = Names()
    with ExitStack() as all_phases:
        w = Place(nc, all_phases, "keep")
        keep.ident = w.sb("ident", [P, P])
        keep.gavg = w.sb("gavg", [P, P])
        keep.gn_eps = w.sb("gn_eps", [P, 1])
        keep.stats = w.sb("stats", [P, NB * KC, NJ, 6])
        keep.scale = w.sb("scale", [P, NB * KC])
        keep.shift = w.sb("shift", [P, NB * KC])
        with ExitStack() as mamba:
            w = Place(nc, mamba, "l0")
            keep.neg_a = w.sb("neg_a", [P, KD * NS])
            keep.dskip = w.sb("dskip", [P, KD])
            with ExitStack() as first:
                w = Place(nc, first, "l0f")
                keep.w_in = [w.sb("w_in_hi", [P, KC, 2 * DI], F32R), w.sb("w_in_lo", [P, KC, 2 * DI], F32R)]
                keep.b_in = w.sb("b_in", [P, 2 * KD])
                keep.mean_w = w.sb("mean_w", [P, P])
                keep.conv_w = w.sb("conv_w", [P, KD, TAPS])
                keep.conv_b = w.sb("conv_b", [P, KD])
                keep.w_xp = w.sb("w_xp", [P, KD, 64])
                keep.w_dt = w.sb("w_dt", [RANK + 1, DI])
                keep.v = w.sb("v", [P, KC, T])
                keep.x_loaded = w.sem("x_loaded")
                setup(nc, keep, d)
                first_x = d.x.rearrange("b (k p) (j r) w -> b j p k (r w)", p=P, j=NJ)[0, 0]
                group_params(nc, "g1", keep, keep.stats, keep.scale, keep.shift, [(keep.v, first_x, keep.x_loaded)])
                front(nc, keep, d)
            scan(nc, keep, d)
        with ExitStack() as memory:
            w = Place(nc, memory, "l1")
            keep.m = w.sb("m", [P, KK, DIM])
            keep.sums = w.sb("sums", [P, KK, DIM])
            keep.count = w.sb("count", [P, KM])
            with ExitStack() as scores:
                w = Place(nc, scores, "l1s")
                keep.mt = [w.sb("mt_hi", [P, KC, KM], F32R), w.sb("mt_lo", [P, KC, KM], F32R)]
                keep.iota = w.sb("iota", [P, KM])
                keep.v = w.sb("v", [P, KC, T])
                keep.m_loaded = w.sem("m_loaded")
                keep.iota_loaded = w.sem("iota_loaded")
                keep.x_loaded = w.sem("x1_loaded")
                group_params(nc, "g2", keep, keep.stats, keep.scale, keep.shift, [
                    (keep.m, d.m.rearrange("(k p) c -> p k c", p=P), keep.m_loaded),
                    (keep.v, d.x1[0], keep.x_loaded),
                    (keep.iota, d.iota.broadcast_to([P, KM]), keep.iota_loaded)])
                memory_setup(nc, keep, d)
                assign(nc, keep, d)
            readout(nc, keep, d)


def kernel(**inputs):
    import numpy as np
    from concourse import bacc
    from concourse.bass_utils import run_bass_kernel_spmd

    a = {k.replace("L0_conv_", "").replace("L1_conv_", ""): np.asarray(v) for k, v in inputs.items()}
    rows = lambda t: t.reshape(-1, P, *t.shape[1:]).swapaxes(0, 1)
    channel = np.arange(P)
    arrays = {
        "x": a["x"],
        "m": a["m"],
        "w_in": rows(a["in_proj_w"].T),
        "w_out": rows(a["out_proj_w"].T),
        "w_xp": rows(a["x_proj_w"].T),
        "w_dt": a["dt_proj_w"].T,
        "b_dt": a["dt_proj_b"][None, :],
        "ln_w": rows(a["ln_w"]),
        "ln_b": rows(a["ln_b"]),
        "conv_w": rows(a["conv_w"]),
        "conv_b": rows(a["conv_b"]),
        "d_skip": rows(a["D_skip"]),
        "a_log": rows(a["A_log"]).reshape(P, -1),
        "ident": np.eye(P, dtype=np.float32),
        "gavg": ((channel[:, None] // 16 == channel[None, :] // 16) / np.float32(16)).astype(np.float32),
        "iota": np.arange(KM, dtype=np.float32)[None, :],
    }
    nc = bacc.Bacc("TRN2", target_bir_lowering=False, num_devices=1)
    d = Names()
    sent = {}
    for name, value in arrays.items():
        value = np.ascontiguousarray(value)
        sent[f"in_{name}"] = value
        d.__dict__[name] = nc.dram_tensor(f"in_{name}", value.shape, mybir.dt.from_np(value.dtype), kind="ExternalInput").ap()
    d.out = nc.dram_tensor("out", (NB, DIM, 64, 64), F32, kind="ExternalOutput").ap()
    program(nc, d)
    r = run_bass_kernel_spmd(nc, [sent], core_ids=[0])
    return r.results[0]["out"]
```
